# Optimizing a Trainium2 kernel written in Bass

```python
import numpy as np
import jax
import jax.numpy as jnp

def _softmax(x, axis=-1):
    return jax.nn.softmax(x, axis=axis)

def _gelu(x):
    return jax.nn.gelu(x, approximate=True)

def _silu(x):
    return jax.nn.silu(x)

def _sigmoid(x):
    return jax.nn.sigmoid(x)

def _layernorm(x, axis=-1, eps=1e-05):
    m = jnp.mean(x, axis=axis, keepdims=True)
    v = jnp.var(x, axis=axis, keepdims=True)
    return (x - m) / jnp.sqrt(v + eps)

def _scatter_add(tgt, idx, src, axis=0):
    return tgt.at[idx].add(src)

def _segment_sum(src, seg, n):
    return jax.ops.segment_sum(src, seg, n)
kernel_name = 'mk_flamingo_gated_d1_seqx_r4_896e5e'

def setup_inputs(seed: int=0):
    np.random.seed(seed)
    _w = jnp.asarray

    def _rec_inputs():
        import jax
        import jax.numpy as jnp
        _rk = jax.random.key(seed)
        x = -0.0002928 + 1 * jax.random.normal(jax.random.fold_in(_rk, 1), (32, 256, 256), jnp.float32)
        _lenS = 256 - jax.random.randint(jax.random.fold_in(_rk, 7), (32,), 0, max(1, 256 // 4) + 1, jnp.int32)
        _lenS2 = 256 - jax.random.randint(jax.random.fold_in(_rk, 8), (32,), 0, max(1, 256 // 4) + 1, jnp.int32)
        _ctx_1024P = jax.random.normal(jax.random.fold_in(_rk, 11), (32, 16, 256), jnp.float32)
        _ctx_1024c = jax.random.dirichlet(jax.random.fold_in(_rk, 511), 0.3 * jnp.ones((16,), jnp.float32), (32, 256))
        _ctx_1024t = jnp.einsum('bsk,bkd->bsd', _ctx_1024c, _ctx_1024P)
        _ctx_1024t = _ctx_1024t * jax.lax.rsqrt(jnp.mean(jnp.square(_ctx_1024t)) + 1e-12) * 0.953939
        ctx_1024 = -1.39393e-06 + 0.999914 * (_ctx_1024t + 0.3 * jax.random.normal(jax.random.fold_in(_rk, 611), (32, 256, 256), jnp.float32))
        _g = jax.random.normal(jax.random.fold_in(_rk, 9001), (2, 1), jnp.float32)
        _g = jnp.sign(_g) * jnp.maximum(jnp.abs(_g), 1.0) + (_g == 0) * 1.0
        g_xattn = _g[0]
        g_ffn = _g[1]
        return (x, ctx_1024, g_xattn, g_ffn)
    x, ctx_1024, g_xattn, g_ffn = _rec_inputs()

    def _L0_xattn_setup():
        import jax, jax.numpy as jnp
        import numpy as np
        H = 16
        D_MODEL = 256
        D_K = D_MODEL // H
        WINDOW = 50
        ROPE_BASE = 10000.0

        def _rope_tables(seq_len, dim, dtype):
            inv_freq = 1.0 / ROPE_BASE ** (jnp.arange(0, dim, 2, dtype=jnp.float32) / dim)
            t = jnp.arange(seq_len, dtype=jnp.float32)
            freqs = t[:, None] * inv_freq[None, :]
            emb = jnp.concatenate([freqs, freqs], axis=-1)
            return (jnp.cos(emb).astype(dtype), jnp.sin(emb).astype(dtype))

        def _rotate_half(x):
            d = x.shape[-1] // 2
            return jnp.concatenate([-x[..., d:], x[..., :d]], axis=-1)
        key = jax.random.key(seed)
        ks = jax.random.split(key, 11)
        B, S = (2, 512)
        scale = 1.0 / np.sqrt(D_MODEL)
        inp = {'query': jax.random.normal(ks[0], (B, S, D_MODEL), jnp.float32), 'key': jax.random.normal(ks[1], (B, S, D_MODEL), jnp.float32), 'value': jax.random.normal(ks[2], (B, S, D_MODEL), jnp.float32), 'Wq': jax.random.normal(ks[3], (D_MODEL, D_MODEL), jnp.float32) * scale, 'bq': jnp.zeros((D_MODEL,), jnp.float32), 'Wk': jax.random.normal(ks[4], (D_MODEL, D_MODEL), jnp.float32) * scale, 'bk': jnp.zeros((D_MODEL,), jnp.float32), 'Wv': jax.random.normal(ks[5], (D_MODEL, D_MODEL), jnp.float32) * scale, 'bv': jnp.zeros((D_MODEL,), jnp.float32), 'Wo': jax.random.normal(ks[6], (D_MODEL, D_MODEL), jnp.float32) * scale, 'bo': jnp.zeros((D_MODEL,), jnp.float32)}
        return inp
    _L0_xattn_all = _L0_xattn_setup()
    _L0_xattn_in = {k: v for k, v in _L0_xattn_all.items() if k in ('Wq', 'bq', 'Wk', 'bk', 'Wv', 'bv', 'Wo', 'bo')}
    del _L0_xattn_all

    def _L0_ffn_setup():
        import jax, jax.numpy as jnp
        import numpy as np
        BLOCK = 32
        W_BITS = 4
        ACT_BITS = 16

        def act_qdq(x):
            qmax = 2.0 ** (ACT_BITS - 1) - 1.0
            scale = jnp.maximum(jnp.max(jnp.abs(x)) / qmax, 1e-12)
            return jnp.clip(jnp.round(x / scale), -qmax - 1.0, qmax) * scale

        def fixed_qdq_u16(x):
            scale = 1.0 / 65536.0
            return jnp.clip(jnp.round(x / scale), 0.0, 65535.0) * scale

        def lpbq_dequant(w):
            O, I = w.shape
            qmax = 2.0 ** (W_BITS - 1) - 1.0
            wb = w.reshape(O, I // BLOCK, BLOCK)
            s = jnp.maximum(jnp.max(jnp.abs(wb), axis=-1, keepdims=True) / qmax, 1e-12)
            wq = jnp.clip(jnp.round(wb / s), -qmax - 1.0, qmax) * s
            return wq.reshape(O, I)
        key = jax.random.key(seed)
        k1, k2, k3, k4 = jax.random.split(key, 4)
        B, S, H, I = (2, 1024, 256, 768)
        x = jax.random.normal(k1, (B, S, H), jnp.float32)
        w_gate = jax.random.normal(k2, (I, H), jnp.float32) * 0.02
        w_up = jax.random.normal(k3, (I, H), jnp.float32) * 0.02
        w_down = jax.random.normal(k4, (H, I), jnp.float32) * 0.02
        return {'x': x, 'w_gate': w_gate, 'w_up': w_up, 'w_down': w_down}
    _L0_ffn_all = _L0_ffn_setup()
    _L0_ffn_in = {k: v for k, v in _L0_ffn_all.items() if k in ('w_gate', 'w_up', 'w_down')}
    del _L0_ffn_all
    return {'x': x, 'ctx_1024': ctx_1024, 'g_xattn': g_xattn, 'g_ffn': g_ffn, 'L0_xattn_Wq': _L0_xattn_in['Wq'], 'L0_xattn_bq': _L0_xattn_in['bq'], 'L0_xattn_Wk': _L0_xattn_in['Wk'], 'L0_xattn_bk': _L0_xattn_in['bk'], 'L0_xattn_Wv': _L0_xattn_in['Wv'], 'L0_xattn_bv': _L0_xattn_in['bv'], 'L0_xattn_Wo': _L0_xattn_in['Wo'], 'L0_xattn_bo': _L0_xattn_in['bo'], 'L0_ffn_w_gate': _L0_ffn_in['w_gate'], 'L0_ffn_w_up': _L0_ffn_in['w_up'], 'L0_ffn_w_down': _L0_ffn_in['w_down']}

def reference(x, ctx_1024, g_xattn, g_ffn, L0_xattn_Wq, L0_xattn_bq, L0_xattn_Wk, L0_xattn_bk, L0_xattn_Wv, L0_xattn_bv, L0_xattn_Wo, L0_xattn_bo, L0_ffn_w_gate, L0_ffn_w_up, L0_ffn_w_down):
    import jax
    import jax.numpy as jnp

    def _L0_xattn_ref(query, key, value, Wq, bq, Wk, bk, Wv, bv, Wo, bo):
        import jax, jax.numpy as jnp
        import numpy as np
        H = 16
        D_MODEL = 256
        D_K = D_MODEL // H
        WINDOW = 50
        ROPE_BASE = 10000.0

        def _rope_tables(seq_len, dim, dtype):
            inv_freq = 1.0 / ROPE_BASE ** (jnp.arange(0, dim, 2, dtype=jnp.float32) / dim)
            t = jnp.arange(seq_len, dtype=jnp.float32)
            freqs = t[:, None] * inv_freq[None, :]
            emb = jnp.concatenate([freqs, freqs], axis=-1)
            return (jnp.cos(emb).astype(dtype), jnp.sin(emb).astype(dtype))

        def _rotate_half(x):
            d = x.shape[-1] // 2
            return jnp.concatenate([-x[..., d:], x[..., :d]], axis=-1)
        B, S, _ = query.shape

        def proj(x, W, b):
            return (x @ W.T + b).reshape(B, S, H, D_K).transpose(0, 2, 1, 3)
        q = proj(query, Wq, bq)
        k = proj(key, Wk, bk)
        v = proj(value, Wv, bv)
        cos, sin = _rope_tables(S, D_K, q.dtype)
        q = q * cos + _rotate_half(q) * sin
        k = k * cos + _rotate_half(k) * sin
        scores = jnp.einsum('bhqd,bhkd->bhqk', q, k) / np.sqrt(D_K)
        idx = jnp.arange(S)
        dist = jnp.abs(idx[None, :] - idx[:, None])
        scores = jnp.where(dist <= WINDOW, scores, jnp.asarray(-1000000000.0, scores.dtype))
        p = jax.nn.softmax(scores, axis=-1)
        out = jnp.einsum('bhqk,bhkd->bhqd', p, v)
        out = out.transpose(0, 2, 1, 3).reshape(B, S, D_MODEL)
        return out @ Wo.T + bo

    def _L0_ffn_ref(x, w_gate, w_up, w_down):
        import jax, jax.numpy as jnp
        import numpy as np
        BLOCK = 32
        W_BITS = 4
        ACT_BITS = 16

        def act_qdq(x):
            qmax = 2.0 ** (ACT_BITS - 1) - 1.0
            scale = jnp.maximum(jnp.max(jnp.abs(x)) / qmax, 1e-12)
            return jnp.clip(jnp.round(x / scale), -qmax - 1.0, qmax) * scale

        def fixed_qdq_u16(x):
            scale = 1.0 / 65536.0
            return jnp.clip(jnp.round(x / scale), 0.0, 65535.0) * scale

        def lpbq_dequant(w):
            O, I = w.shape
            qmax = 2.0 ** (W_BITS - 1) - 1.0
            wb = w.reshape(O, I // BLOCK, BLOCK)
            s = jnp.maximum(jnp.max(jnp.abs(wb), axis=-1, keepdims=True) / qmax, 1e-12)
            wq = jnp.clip(jnp.round(wb / s), -qmax - 1.0, qmax) * s
            return wq.reshape(O, I)
        x = act_qdq(x)
        up = act_qdq(x @ lpbq_dequant(w_up).T)
        gate = act_qdq(x @ lpbq_dequant(w_gate).T)
        sig = fixed_qdq_u16(jax.nn.sigmoid(gate))
        gate = act_qdq(gate * sig)
        o = act_qdq(gate * up)
        return o @ lpbq_dequant(w_down).T
    x = x + jnp.tanh(g_xattn[0]) * _L0_xattn_ref(_layernorm(x, axis=-1), ctx_1024, ctx_1024, L0_xattn_Wq, L0_xattn_bq, L0_xattn_Wk, L0_xattn_bk, L0_xattn_Wv, L0_xattn_bv, L0_xattn_Wo, L0_xattn_bo)
    x = x + jnp.tanh(g_ffn[0]) * _L0_ffn_ref(_layernorm(x, axis=-1), L0_ffn_w_gate, L0_ffn_w_up, L0_ffn_w_down)
    return x

_drawn_inputs = setup_inputs


def setup_inputs(seed=0):
    import zlib

    import numpy as np

    out = dict(_drawn_inputs(seed))
    spreads = {'L0_xattn_bq': (0.0, 0.498),
     'L0_xattn_bk': (0.0, 0.8),
     'L0_xattn_bv': (0.0, 0.1),
     'L0_xattn_bo': (0.0, 0.1)}
    factors = {}
    for name, (base, spread) in spreads.items():
        noise = np.random.default_rng([zlib.crc32(name.encode()), seed]).standard_normal(out[name].shape)
        drawn = base * np.exp(spread * noise) if base else spread * noise
        out[name] = jnp.asarray(drawn.astype(out[name].dtype))
    for name, factor in factors.items():
        out[name] = (out[name] * factor).astype(out[name].dtype)
    return out
```

```python
from contextlib import ExitStack

import numpy as np

import concourse.bass as bass
from concourse import mybir

F32 = mybir.dt.float32
BF16 = mybir.dt.bfloat16
I16 = mybir.dt.int16
U16 = mybir.dt.uint16
ALU = mybir.AluOpType
ACT = mybir.ActivationFunctionType
X = mybir.AxisListType.X
XY = mybir.AxisListType.XY
RMAX = bass.bass_isa.ReduceOp.max

P = 128
B, S, D = 32, 256, 256
H, DK = 16, 16
HALF = DK // 2
I = 768
WINDOW = 50
BLOCK, WQMAX = 32, 7.0
AQMAX = 32767.0
EPS_LN, EPS_Q = 1e-5, 1e-12
T = S // P
C = D // P
SPAN = P + WINDOW
FAR = S - SPAN
PAIRS = H // 2
SLOTS = PAIRS
NBUF = 3
HALVES = 2
STACK_Q = (0, 0, 0, 1, 1, 2)
STACK_K = (0, 1, 2, 0, 1, 0)
STACK = len(STACK_Q) * DK
SHIFT = 2
OUT = 2 * DK
TILE = 512
RING = 4
FIRST_ROUND, LAST_ROUND = 3, B // NBUF
LATE = 4


class Batch:

    def __init__(self, rnd, unit, late):
        back, self.buf = divmod(unit - late, NBUF)
        self.rnd = rnd + back
        self.n = self.rnd * NBUF + self.buf
        self.fixed = isinstance(self.n, int)
        self.real = 0 <= self.n < B if self.fixed else True

    def before(self, k):
        return Batch(self.rnd, self.buf, k)


def reached(eng, sem, batch, per, k):
    value = batch.n * per + k
    if isinstance(value, int) and value <= 0:
        return
    eng.wait_ge(sem, value)


def carry(eng, sem):
    eng.sem_inc(sem, 1)


def loaded(eng, sems, batch):
    eng.wait_ge(sems[batch.buf], batch.rnd * 16 + 16)


def prepare(nc, dram, w, banks, keep):
    with ExitStack() as ctx:
        def sb(name, shape, dt=F32):
            return ctx.enter_context(nc.sbuf_tensor(name, shape, dt))

        def sem(name):
            return ctx.enter_context(nc.semaphore(name))

        attn = ("Wq", "Wk", "Wv", "Wo")
        ffn = ("w_gate", "w_up", "w_down")
        nat = {n: sb(f"nat_{n}", [P, T * D]) for n in attn}
        nat.update({n: sb(f"nat_{n}", [P, I * D // P]) for n in ffn})
        brow = sb("brow", [1, 4 * D])
        bpart = sb("bpart", [1, 3, 4 * D], BF16)
        brest = sb("brest", [1, 4 * D])
        brest2 = sb("brest2", [1, 4 * D])
        grow = sb("grow", [1, 2])
        one_row = sb("one_row", [1, P])
        nblk = I * D // P // BLOCK
        wabs = sb("wabs", [P, nblk])
        wscale = sb("wscale", [P, nblk])
        winv = sb("winv", [P, nblk])
        wint = sb("wint", [P, I * D // P])
        wround = sb("wround", [P, I * D // P], I16)
        consts_in = sem("consts_in")
        gates_in = sem("gates_in")
        bias_in = sem("bias_in")
        nat_in = {n: sem(f"in_{n}") for n in attn + ffn}
        weight_quantised = sem("weight_quantised")
        dve_step = sem("dve_step")
        part_step = sem("part_step")
        ones_set = sem("ones_set")
        blocks_transposed = sem("blocks_transposed")
        bank_copied = sem("bank_copied")
        gates_spread = sem("gates_spread")
        bias_rows = sem("bias_rows")
        block = ctx.enter_context(nc.Block())

        @block.sync
        def _(sp):
            sp.dma_start(keep["ident"][:], dram["ident"]).then_inc(consts_in, 16)
            for n in attn:
                sp.dma_start(nat[n][:].rearrange("p (o i) -> p o i", o=T),
                             w[n].rearrange("(o p) i -> p o i", p=P)).then_inc(nat_in[n], 16)
            for n in ffn:
                rows = w[n].shape[0] // P
                sp.dma_start(nat[n][:].rearrange("p (o i) -> p o i", o=rows),
                             w[n].rearrange("(o p) i -> p o i", p=P)).then_inc(nat_in[n], 16)
            sp.dma_start(keep["cos"][:], dram["cos"]).then_inc(consts_in, 16)
            sp.dma_start(keep["sin"][:], dram["sin"]).then_inc(consts_in, 16)
            sp.dma_start(keep["band"][:], dram["band"]).then_inc(consts_in, 16)
            for k, n in enumerate(("bq", "bk", "bv", "bo")):
                sp.dma_start(brow[:, k * D:(k + 1) * D], w[n].rearrange("(a n) -> a n", a=1)).then_inc(bias_in, 16)
            sp.dma_start(grow[:, 0:1], w["g_xattn"].rearrange("(a n) -> a n", a=1)).then_inc(gates_in, 16)
            sp.dma_start(grow[:, 1:2], w["g_ffn"].rearrange("(a n) -> a n", a=1)).then_inc(gates_in, 16)
            sp.wait_ge(part_step, 5)
            for k in range(3):
                sp.dma_start(keep["bias"][k:k + 1, :], bpart[:, k, :]).then_inc(bias_rows, 16)
            sp.wait_ge(bias_rows, 48)
            sp.wait_ge(consts_in, 64)

        @block.vector
        def _(dve):
            nc.vector.memset(one_row[:], 1.0).then_inc(ones_set, 1)
            nc.vector.memset(keep["ones3"][:], 1.0).then_inc(ones_set, 1)
            nc.vector.memset(keep["lnconst"][:, 0:2], EPS_LN).then_inc(ones_set, 1)
            nc.vector.memset(keep["lnconst"][:, 2:4], -0.5).then_inc(ones_set, 1)
            dve.wait_ge(consts_in, 64)
            nc.vector.tensor_copy(keep["identb"][:], keep["ident"][:]).then_inc(ones_set, 1)
            dve.wait_ge(bias_in, 64)
            nc.vector.tensor_copy(bpart[:, 0, :], brow[:]).then_inc(part_step, 1)
            dve.wait_ge(part_step, 1)
            nc.vector.tensor_tensor(brest[:], brow[:], bpart[:, 0, :], ALU.subtract).then_inc(part_step, 1)
            dve.wait_ge(part_step, 2)
            nc.vector.tensor_copy(bpart[:, 1, :], brest[:]).then_inc(part_step, 1)
            dve.wait_ge(part_step, 3)
            nc.vector.tensor_tensor(brest2[:], brest[:], bpart[:, 1, :], ALU.subtract).then_inc(part_step, 1)
            dve.wait_ge(part_step, 4)
            nc.vector.tensor_copy(bpart[:, 2, :], brest2[:]).then_inc(part_step, 1)
            steps = 0
            for n in ffn:
                def step(ins):
                    ins.then_inc(dve_step, 1)
                dve.wait_ge(nat_in[n], 16)
                blocks = nat[n][:].rearrange("p (k i) -> p k i", i=BLOCK)
                spread = [P, nblk, BLOCK]
                step(nc.vector.tensor_reduce(wabs[:], blocks, X, ALU.max, apply_absolute_value=True))
                dve.wait_ge(dve_step, steps + 1)
                step(nc.vector.tensor_scalar(wscale[:], wabs[:], 1.0 / WQMAX, EPS_Q, ALU.mult, ALU.max))
                dve.wait_ge(dve_step, steps + 2)
                step(nc.vector.reciprocal(winv[:], wscale[:]))
                dve.wait_ge(dve_step, steps + 3)
                step(nc.vector.tensor_tensor(wint[:].rearrange("p (k i) -> p k i", i=BLOCK), blocks,
                                             winv[:].unsqueeze(2).to_broadcast(spread), ALU.mult))
                dve.wait_ge(dve_step, steps + 4)
                step(nc.vector.tensor_copy(wround[:], wint[:]))
                dve.wait_ge(dve_step, steps + 5)
                nc.vector.tensor_tensor(blocks, wround[:].rearrange("p (k i) -> p k i", i=BLOCK),
                                        wscale[:].unsqueeze(2).to_broadcast(spread), ALU.mult)\
                    .then_inc(weight_quantised, 1)
                steps += 5
                dve.wait_ge(weight_quantised, steps // 5)

        plan = []
        for n in attn:
            plan.append([(n, o, c, keep[n + "T"][:], D) for c in range(C) for o in range(T)])
        for n in ffn:
            rows, cols = w[n].shape[0] // P, w[n].shape[1] // P
            blks = [(n, o, c, keep[n + "T"][:], rows * P) for c in range(cols) for o in range(rows)]
            plan += [blks[k:k + 4] for k in range(0, len(blks), 4)]

        @block.tensor
        def _(pe):
            pe.wait_ge(ones_set, 5)
            for k, blks in enumerate(plan):
                n = blks[0][0]
                if n in attn:
                    pe.wait_ge(nat_in[n], 16)
                else:
                    pe.wait_ge(weight_quantised, ffn.index(n) + 1)
                if k >= 4:
                    pe.wait_ge(bank_copied, k - 3)
                for q, (_, o, c, _, _) in enumerate(blks):
                    width = w[n].shape[1]
                    last = nc.tensor.transpose(banks[k % 4][:, q * P:(q + 1) * P],
                                               nat[n][:, o * width + c * P:o * width + (c + 1) * P],
                                               keep["ident"][:])
                last.then_inc(blocks_transposed, 1)
            pe.wait_ge(gates_in, 32)
            nc.tensor.matmul(banks[4][:, 0:2], one_row[:], grow[:], start=True, stop=True).then_inc(gates_spread, 1)

        @block.scalar
        def _(act):
            for k, blks in enumerate(plan):
                act.wait_ge(blocks_transposed, k + 1)
                _, o, c, dst, rows = blks[0]
                at = c * rows + o * P
                nc.scalar.activation(dst[:, at:at + 4 * P], banks[k % 4][:], ACT.Copy).then_inc(bank_copied, 1)
            act.wait_ge(gates_spread, 1)
            nc.scalar.activation(keep["tanh"][:], banks[4][:, 0:2], ACT.Tanh).then_inc(bank_copied, 1)
            act.wait_ge(bank_copied, len(plan) + 1)


def attention(nc, dram, x, ctx_in, scratch, banks, keep):
    with ExitStack() as ctx:
        def sb(name, shape, dt=F32):
            return ctx.enter_context(nc.sbuf_tensor(name, shape, dt))

        def sem(name):
            return ctx.enter_context(nc.semaphore(name))

        def bufs(name, shape, dt=F32, n=NBUF):
            return [sb(f"{name}{k}", shape, dt) for k in range(n)]

        W2 = T * D
        x_in, c_in = sb("x_in", [P, T, D]), sb("c_in", [P, T, D])
        stats, moments, rstd = sb("stats", [P, T, 6]), sb("moments", [P, T, 2]), sb("rstd", [P, T])
        veps = sb("veps", [P, T])
        xn = sb("xn", [P, T, D])
        xT, cT = sb("xT", [P, C, S]), sb("cT", [P, C, S])
        by_cos = {n: sb(f"{n}_cos", [P, W2]) for n in "qk"}
        by_sin = {n: sb(f"{n}_sin", [P, W2]) for n in "qk"}
        rot = by_cos
        parts = {n: sb(f"{n}_parts", [P, 3, C * S], BF16) for n in "qk"}
        rest = by_sin
        q_stack, k_stack = bufs("q_stack", [P, H, S], BF16), bufs("k_stack", [P, H, S], BF16)
        V = bufs("V", [P, T * H, OUT])
        smax = bufs("smax", [P, T, H])
        shift = sb("shift", [P, T, HALVES, SHIFT, H // 2], BF16)
        shiftT = bufs("shiftT", [SHIFT * H // 2, S], BF16, HALVES)
        probs = bufs("probs", [P, 2, SPAN], n=RING)
        outT = sb("outT", [P, 4, S])
        rden = sb("rden", [P, T, H])
        att = sb("att", [P, T, D])
        attT = sb("attT", [P, C, S])
        x2 = bufs("x2", [P, T, D])
        stats2, moments2, rstd2 = sb("stats2", [P, T, 6]), sb("moments2", [P, T, 2]), sb("rstd2", [P, T])
        veps2 = sb("veps2", [P, T])
        xn2 = sb("xn2", [P, T, D])

        score_bank, scoreT_bank, out_bank = banks[0:2], banks[2:4], banks[4:6]
        bank_a, bank_b = banks[6], banks[7]

        x_loaded, c_loaded = sem("x_loaded"), sem("c_loaded")
        xres_loaded = [sem(f"xres_loaded{k}") for k in range(NBUF)]
        parts_stored = {n: sem(f"{n}_parts_stored") for n in "qk"}
        stack_loaded = {n: [sem(f"{n}_stack_loaded{k}") for k in range(NBUF)] for n in "qk"}
        shift_loaded = [[sem(f"shift_loaded{h}_{k}") for k in range(NBUF)] for h in range(HALVES)]
        x2_stored = [sem(f"x2_stored{k}") for k in range(NBUF)]
        dve_carried, pool_carried, sp_carried = sem("dve_carried"), sem("pool_carried"), sem("sp_carried")
        consts_set = sem("consts_set")
        stats_taken, moments_taken = sem("stats_taken"), sem("moments_taken")
        x_normed = sem("x_normed")
        multiplied = {n: sem(f"{n}_multiplied") for n in "qk"}
        rest_ready = {n: sem(f"{n}_rest_ready") for n in "qk"}
        low_ready = {n: sem(f"{n}_low_ready") for n in "qk"}
        max_taken = sem("max_taken")
        shift_high, shift_ready = sem("shift_high"), sem("shift_ready")
        rden_ready, out_normed = sem("rden_ready"), sem("out_normed")
        x2_ready, stats2_taken, moments2_taken = sem("x2_ready"), sem("stats2_taken"), sem("moments2_taken")
        x2_normed, xmax_taken = sem("x2_normed"), sem("xmax_taken")
        cT_copied, xT_copied, v_copied = sem("cT_copied"), sem("xT_copied"), sem("v_copied")
        high_ready = {n: sem(f"{n}_high_ready") for n in "qk"}
        mid_ready = {n: sem(f"{n}_mid_ready") for n in "qk"}
        shiftT_copied, exp_done = sem("shiftT_copied"), sem("exp_done")
        outT_copied, attT_copied, xn2T_copied = sem("outT_copied"), sem("attT_copied"), sem("xn2T_copied")
        eps_added, rstd_ready = sem("eps_added"), sem("rstd_ready")
        eps2_added, rstd2_ready = sem("eps2_added"), sem("rstd2_ready")
        rotated = {n: sem(f"{n}_rotated") for n in "qk"}
        below_cut, band_cut = sem("below_cut"), sem("band_cut")
        c_transposed, x_transposed = sem("c_transposed"), sem("x_transposed")
        projected = {n: sem(f"{n}_projected") for n in "qkv"}
        rot_transposed = {n: sem(f"{n}_rot_transposed") for n in "qk"}
        shift_transposed = sem("shift_transposed")
        scored, scoredT, weighted = sem("scored"), sem("scoredT"), sem("weighted")
        out_transposed, att_transposed = sem("out_transposed"), sem("att_transposed")
        att_projected, x2_transposed = sem("att_projected"), sem("x2_transposed")


        rows_x = x.rearrange("b (t p) d -> b p t d", p=P)
        rows_c = ctx_in.rearrange("b (t p) d -> b p t d", p=P)

        def run(eng, steps):
            for it in range(FIRST_ROUND * NBUF):
                steps(it // NBUF, it % NBUF)
            with eng.Fori(FIRST_ROUND, LAST_ROUND) as rnd:
                for unit in range(NBUF):
                    steps(rnd, unit)
            for it in range(LAST_ROUND * NBUF, B + LATE + 1):
                steps(it // NBUF, it % NBUF)

        def pair_at(slot, first):
            return (slot - first) % SLOTS, (first + (slot - first) % SLOTS) // SLOTS

        S_FIRST, ST_FIRST, PV_FIRST = 11, 18, 19
        block = ctx.enter_context(nc.Block())

        @block.sync
        def _(sp):
            def load_x(b):
                if not b.real:
                    return
                reached(sp, x_normed, b.before(1), T, T)
                sp.dma_start(x_in[:], rows_x[b.n]).then_inc(x_loaded, 16)
                reached(sp, c_transposed, b.before(1), 1, 1)
                sp.dma_start(c_in[:], rows_c[b.n]).then_inc(c_loaded, 16)

            def load_residual(b):
                if not b.real:
                    return
                bb = b.before(NBUF)
                if not bb.fixed or bb.n >= 0:
                    sp.wait_ge(x2_stored[b.buf], bb.rnd * 16 + 16)
                reached(sp, x2_normed, bb, T, T)
                sp.dma_start(x2[b.buf][:], rows_x[b.n]).then_inc(xres_loaded[b.buf], 16)

            def store_parts(b, n):
                if not b.real:
                    return
                reached(sp, mid_ready[n], b, 1, 1)
                reached(sp, low_ready[n], b, 1, 1)
                if not b.fixed:
                    carry(sp, sp_carried)
                if not b.fixed or b.n >= NBUF:
                    sp.wait_ge(stack_loaded[n][b.buf], b.rnd * 48)
                for k in range(3):
                    sp.dma_start(scratch[n][b.buf][k].rearrange("d (h ct) -> h d ct", h=PAIRS), parts[n][:, k, :])\
                        .then_inc(parts_stored[n], 16)

            def load_stacks(b, n):
                if not b.real:
                    return
                stack = (q_stack if n == "q" else k_stack)[b.buf]
                reached(sp, parts_stored[n], b, 48, 48)
                reached(sp, scoredT, b.before(NBUF), 2 * PAIRS, 2 * PAIRS)
                row = 0
                for g in range(3):
                    rows = (3 - g) * DK
                    sp.dma_start(stack[row:row + rows, :, :].rearrange("r s t -> r (s t)"), scratch[n + "_rows"](b.buf, g)).then_inc(stack_loaded[n][b.buf], 16)
                    row += rows

            def load_shift(b, half):
                if not b.real:
                    return
                reached(sp, shiftT_copied, b, HALVES, half + 1)
                for k in range(SHIFT):
                    sp.dma_start(q_stack[b.buf][STACK + k:STACK + k + 1, half * 8:half * 8 + 8, :],
                                 shiftT[half][k * 8:(k + 1) * 8, :]).then_inc(shift_loaded[half][b.buf], 16)

            def store_x2(b):
                if not b.real:
                    return
                reached(sp, x2_ready, b, 1, 1)
                sp.dma_start(scratch["x2"][b.n], x2[b.buf][:]).then_inc(x2_stored[b.buf], 16)

            load_x(Batch(0, 0, 0))

            def steps(rnd, unit):
                load_shift(Batch(rnd, unit, 2), 0)
                load_stacks(Batch(rnd, unit, 1), "q")
                load_x(Batch(rnd, unit, -1))
                load_residual(Batch(rnd, unit, 3))
                load_shift(Batch(rnd, unit, 2), 1)
                store_parts(Batch(rnd, unit, 0), "k")
                store_parts(Batch(rnd, unit, 0), "q")
                load_stacks(Batch(rnd, unit, 0), "k")
                store_x2(Batch(rnd, unit, 3))

            run(sp, steps)
            for k in range(NBUF):
                sp.wait_ge(x2_stored[k], 16 * len(range(k, B, NBUF)))

        @block.gpsimd
        def _(pool):
            def scale_of(b, taken, added, ready, mom, eps, out):
                if not b.real:
                    return
                reached(pool, taken, b, T, T)
                nc.gpsimd.tensor_tensor(eps[:], mom[:, :, 1], keep["lnconst"][:, 0:2], ALU.add).then_inc(added, 1)
                reached(pool, added, b, 1, 1)
                nc.gpsimd.tensor_tensor(out[:], eps[:], keep["lnconst"][:, 2:4], ALU.pow).then_inc(ready, 1)

            def rotate(b, n):
                if not b.real:
                    return
                reached(pool, multiplied[n], b, 3, 3)
                nc.gpsimd.tensor_tensor(rot[n][:], by_cos[n][:], by_sin[n][:], ALU.add).then_inc(rotated[n], 1)

            def cut(b, pair):
                if not b.real:
                    return
                for c in range(T):
                    off = c * WINDOW
                    t = probs[(2 * pair + c) % RING]
                    reached(pool, exp_done, b, 2 * PAIRS, 2 * pair + c + 1)
                    if not b.fixed:
                        carry(pool, pool_carried)
                    n = P - 1 - WINDOW + off
                    nc.gpsimd.affine_select(out=t[:, :, 0:n], in_=t[:, :, 0:n], pattern=[[0, 2], [1, n]],
                                            compare_op=ALU.is_ge, fill=0.0, base=WINDOW - off,
                                            channel_multiplier=-1).then_inc(below_cut, 1)
                for c in range(T):
                    off = c * WINDOW
                    t = probs[(2 * pair + c) % RING]
                    reached(pool, below_cut, b, 2 * PAIRS, 2 * pair + c + 1)
                    if not b.fixed:
                        carry(pool, pool_carried)
                    n = WINDOW + 1 + off
                    nc.gpsimd.affine_select(out=t[:, :, n:SPAN], in_=t[:, :, n:SPAN], pattern=[[0, 2], [-1, SPAN - n]],
                                            compare_op=ALU.is_ge, fill=0.0, base=WINDOW + off - n,
                                            channel_multiplier=1).then_inc(band_cut, 1)

            def steps(rnd, unit):
                for slot in range(SLOTS):
                    if slot == 0:
                        scale_of(Batch(rnd, unit, 0), moments_taken, eps_added, rstd_ready, moments, veps, rstd)
                    if slot == 2:
                        rotate(Batch(rnd, unit, 0), "k")
                    if slot == 3:
                        rotate(Batch(rnd, unit, 0), "q")
                    if slot == 7:
                        scale_of(Batch(rnd, unit, 3), moments2_taken, eps2_added, rstd2_ready, moments2, veps2, rstd2)
                    pair, late = pair_at(slot, ST_FIRST)
                    cut(Batch(rnd, unit, late), pair)

            run(pool, steps)

        @block.scalar
        def _(act):
            def copy_out(b, done, per, k, src, dst, signal, free=()):
                if not b.real:
                    return
                reached(act, done, b, per, k)
                for f in free:
                    reached(act, *f)
                nc.scalar.activation(dst, src, ACT.Copy).then_inc(signal, 1)

            def high(b, n, bank):
                if not b.real:
                    return
                reached(act, rot_transposed[n], b, 1, 1)
                reached(act, parts_stored[n], b.before(1), 48, 48)
                nc.scalar.activation(parts[n][:, 0, :], bank[:], ACT.Copy).then_inc(high_ready[n], 1)

            def middle(b, n):
                if not b.real:
                    return
                reached(act, rest_ready[n], b, 1, 1)
                nc.scalar.activation(parts[n][:, 1, :], rest[n][:], ACT.Copy).then_inc(mid_ready[n], 1)

            def exps(b, pair):
                if not b.real:
                    return
                for c in range(T):
                    reached(act, scoredT, b, 2 * PAIRS, 2 * pair + c + 1)
                    reached(act, weighted, b, PAIRS, pair - RING // 2 + 1)
                    nc.scalar.activation(probs[(2 * pair + c) % RING][:].rearrange("p e j -> p (e j)"),
                                         scoreT_bank[c][:, 0:2 * SPAN], ACT.Exp, scale=DK ** -0.5)\
                        .then_inc(exp_done, 1)

            def shift_copy(b, half):
                if not b.real:
                    return
                reached(act, shift_transposed, b, HALVES, half + 1)
                bb = b.before(1)
                if not bb.fixed or bb.n >= 0:
                    act.wait_ge(shift_loaded[half][bb.buf], bb.rnd * 16 * SHIFT + 16 * SHIFT)
                nc.scalar.activation(shiftT[half][:], bank_b[0:SHIFT * 8, 0:S // 2].bitcast(BF16), ACT.Copy)\
                    .then_inc(shiftT_copied, 1)

            def steps(rnd, unit):
                for slot in range(SLOTS):
                    b0, b1, b2, b3, b4 = (Batch(rnd, unit, k) for k in range(5))
                    if slot == 0:
                        copy_out(b0, c_transposed, 1, 1, bank_a[:], cT[:].rearrange("p c t -> p (c t)"), cT_copied,
                                 [(projected["v"], b0.before(1), 1, 1)])
                    if slot == 1:
                        if b4.real:
                            reached(act, x2_transposed, b4, 1, 1)
                            nc.scalar.activation(keep["xnT"][:, :, bass.ds(b4.n * S, S)],
                                                 bank_b[:].rearrange("p (c t) -> p c t", c=C), ACT.Copy)\
                                .then_inc(xn2T_copied, 1)
                        copy_out(b0, x_transposed, 1, 1, bank_a[:], xT[:].rearrange("p c t -> p (c t)"), xT_copied,
                                 [(projected["q"], b0.before(1), 1, 1)])
                    if slot == 3:
                        if b3.real:
                            copy_out(b3, weighted, PAIRS, PAIRS, out_bank[1][:],
                                     outT[:, 2:4, :].rearrange("p a t -> p (a t)"), outT_copied,
                                     [(out_transposed, b3.before(1), T, T)])
                        high(b0, "k", bank_b)
                        if b0.real:
                            copy_out(b0, projected["v"], 1, 1, bank_a[:].rearrange("p (h d) -> p h d", d=DK),
                                     V[b0.buf][:, :, 0:DK], v_copied, [(weighted, b0.before(NBUF), PAIRS, PAIRS)])
                    if slot == 4:
                        middle(b0, "k")
                        shift_copy(b2, 1)
                        high(b0, "q", bank_a)
                    if slot == 5:
                        middle(b0, "q")
                    if slot == 6:
                        copy_out(b3, att_transposed, 1, 1, bank_a[:], attT[:].rearrange("p c t -> p (c t)"),
                                 attT_copied, [(att_projected, b3.before(1), 1, 1)])
                    if slot == 7:
                        if b2.real:
                            copy_out(b2, weighted, PAIRS, PAIRS // 2, out_bank[0][:],
                                     outT[:, 0:2, :].rearrange("p a t -> p (a t)"), outT_copied,
                                     [(out_transposed, b2.before(1), T, T)])
                        shift_copy(b1, 0)
                    pair, late = pair_at(slot, ST_FIRST)
                    exps(Batch(rnd, unit, late), pair)

            run(act, steps)

        @block.vector
        def _(dve):
            for k in range(NBUF):
                nc.vector.memset(k_stack[k][STACK:P, :, :], 1.0).then_inc(consts_set, 1)
                nc.vector.memset(V[k][:], 0.0).then_inc(consts_set, 1)
            dve.wait_ge(consts_set, 2 * NBUF)
            for k in range(NBUF):
                nc.vector.memset(V[k][:, :, DK:DK + 1], 1.0).then_inc(consts_set, 1)
            dve.wait_ge(consts_set, 3 * NBUF)

            def statistics(b, src, st, mom, taken, aggregated):
                for t in range(T):
                    nc.vector.bn_stats(st[:, t, :], src[:, t, :]).then_inc(taken, 1)
                for t in range(T):
                    reached(dve, taken, b, T, t + 1)
                    if not b.fixed:
                        carry(dve, dve_carried)
                    nc.vector.bn_aggr(mom[:, t, :], st[:, t, :]).then_inc(aggregated, 1)

            def normalise(b, src, dst, mom, scale, ready, signal):
                reached(dve, ready, b, 1, 1)
                for t in range(T):
                    nc.vector.tensor_scalar(dst[:, t, :], src[:, t, :], mom[:, t, 0:1], scale[:, t:t + 1],
                                            ALU.subtract, ALU.mult).then_inc(signal, 1)

            def rope(b, n, bank):
                if not b.real:
                    return
                reached(dve, projected[n], b, 1, 1)
                reached(dve, rot_transposed[n], b.before(1), 1, 1)
                nc.vector.tensor_tensor(by_cos[n][:], bank[:], keep["cos"][:], ALU.mult).then_inc(multiplied[n], 1)
                src = bank[:].rearrange("p (h d) -> p h d", d=DK)
                sin = keep["sin"][:].rearrange("p (h d) -> p h d", d=DK)
                dst = by_sin[n][:].rearrange("p (h d) -> p h d", d=DK)
                nc.vector.tensor_tensor(dst[:, :, 0:HALF], src[:, :, HALF:DK], sin[:, :, 0:HALF], ALU.mult)\
                    .then_inc(multiplied[n], 1)
                nc.vector.tensor_tensor(dst[:, :, HALF:DK], src[:, :, 0:HALF], sin[:, :, HALF:DK], ALU.mult)\
                    .then_inc(multiplied[n], 1)

            def remainder(b, n, bank):
                if not b.real:
                    return
                reached(dve, high_ready[n], b, 1, 1)
                nc.vector.tensor_tensor(rest[n][:], bank[:], parts[n][:, 0, :], ALU.subtract)\
                    .then_inc(rest_ready[n], 1)

            def low(b, n):
                if not b.real:
                    return
                reached(dve, mid_ready[n], b, 1, 1)
                nc.vector.tensor_tensor(parts[n][:, 2, :], rest[n][:], parts[n][:, 1, :], ALU.subtract)\
                    .then_inc(low_ready[n], 1)

            def maxima(b, pair):
                if not b.real:
                    return
                for t in range(T):
                    reached(dve, scored, b, 2 * PAIRS, 2 * pair + t + 1)
                    nc.vector.tensor_reduce(smax[b.buf][:, t, 2 * pair:2 * pair + 2],
                                            score_bank[t][:, 0:2 * SPAN].rearrange("p (e j) -> p e j", e=2),
                                            X, ALU.max).then_inc(max_taken, 1)

            def shift_parts(b, half):
                if not b.real:
                    return
                reached(dve, max_taken, b, 2 * PAIRS, PAIRS * (half + 1))
                reached(dve, shift_transposed, b.before(1), HALVES, half + 1)
                src = smax[b.buf][:, :, half * 8:half * 8 + 8]
                nc.vector.tensor_scalar(shift[:, :, half, 0, :], src, -1.0, None, ALU.mult).then_inc(shift_high, 1)
                reached(dve, shift_high, b, HALVES, half + 1)
                nc.vector.scalar_tensor_tensor(shift[:, :, half, 1, :], src, -1.0, shift[:, :, half, 0, :],
                                               ALU.mult, ALU.subtract).then_inc(shift_ready, 1)

            def divide(b, t, bank):
                if not b.real:
                    return
                reached(dve, out_transposed, b, T, t + 1)
                src = bank[:].rearrange("p (h d) -> p h d", d=OUT)
                nc.vector.reciprocal(rden[:, t, :], src[:, :, DK]).then_inc(rden_ready, 1)
                reached(dve, rden_ready, b, T, t + 1)
                reached(dve, att_transposed, b.before(1), 1, 1)
                for c in range(C):
                    ins = nc.vector.tensor_tensor(att[:, t, c * P:(c + 1) * P].rearrange("p (h d) -> p h d", d=DK),
                                                  src[:, c::2, 0:DK],
                                                  rden[:, t, c::2].unsqueeze(2).to_broadcast([P, PAIRS, DK]), ALU.mult)
                ins.then_inc(out_normed, 1)

            def residual(b):
                if not b.real:
                    return
                loaded(dve, xres_loaded, b)
                reached(dve, att_projected, b, 1, 1)
                nc.vector.scalar_tensor_tensor(x2[b.buf][:].rearrange("p t d -> p (t d)"), bank_b[:],
                                               keep["tanh"][:, 0:1], x2[b.buf][:].rearrange("p t d -> p (t d)"),
                                               ALU.mult, ALU.add).then_inc(x2_ready, 1)
                reached(dve, x2_ready, b, 1, 1)
                statistics(b, x2[b.buf], stats2, moments2, stats2_taken, moments2_taken)

            def steps(rnd, unit):
                for slot in range(SLOTS):
                    b0, b1, b2, b3, b4 = (Batch(rnd, unit, k) for k in range(5))
                    if slot == 0:
                        if b0.real:
                            reached(dve, x_loaded, b0, 16, 16)
                            statistics(b0, x_in, stats, moments, stats_taken, moments_taken)
                        if b4.real:
                            reached(dve, x2_transposed, b4.before(1), 1, 1)
                            normalise(b4, x2[b4.buf], xn2, moments2, rstd2, rstd2_ready, x2_normed)
                    if slot == 1 and b4.real:
                        reached(dve, xn2T_copied, b4, 1, 1)
                        nc.vector.tensor_reduce(keep["xmax"][:, bass.ds(b4.n, 1)], keep["xnT"][:, :, bass.ds(b4.n * S, S)],
                                                XY, ALU.max, apply_absolute_value=True).then_inc(xmax_taken, 1)
                    if slot == 2:
                        rope(b0, "k", bank_b)
                    if slot == 3:
                        rope(b0, "q", bank_a)
                        shift_parts(b2, 1)
                    if slot == 4:
                        remainder(b0, "k", bank_b)
                    if slot == 5:
                        low(b0, "k")
                        remainder(b0, "q", bank_a)
                        divide(b3, 0, bank_a)
                        divide(b3, 1, bank_b)
                    if slot == 6:
                        low(b0, "q")
                    if slot == 7:
                        shift_parts(b1, 0)
                        residual(b3)
                    pair, late = pair_at(slot, S_FIRST)
                    maxima(Batch(rnd, unit, late), pair)
                    if slot == 0 and b0.real:
                        reached(dve, x_transposed, b0.before(1), 1, 1)
                        normalise(b0, x_in, xn, moments, rstd, rstd_ready, x_normed)

            run(dve, steps)
            dve.wait_ge(xmax_taken, B)

        @block.tensor
        def _(pe):
            pe.wait_ge(consts_set, 3 * NBUF)
            ident, identb = keep["ident"], keep["identb"]

            def transpose4(bank, src):
                for t in range(T):
                    for c in range(C):
                        last = nc.tensor.transpose(bank[:, c * S + t * P:c * S + (t + 1) * P],
                                                   src[:, t * D + c * P:t * D + (c + 1) * P], ident[:])
                return last

            def project(bank, srcT, weight, which):
                for t in range(T):
                    out = bank[:, t * D:(t + 1) * D]
                    nc.tensor.matmul(out, keep["ones3"][:], keep["bias"][:, which * D:(which + 1) * D],
                                     start=True, stop=False)
                    for c in range(C):
                        last = nc.tensor.matmul(out, srcT[:, c, t * P:(t + 1) * P], weight[:, c * D:(c + 1) * D],
                                                start=False, stop=(c == C - 1))
                return last

            def scores(b, pair):
                if not b.real:
                    return
                if pair == 0:
                    pe.wait_ge(stack_loaded["k"][b.buf], b.rnd * 48 + 48)
                    pe.wait_ge(stack_loaded["q"][b.buf], b.rnd * 48 + 48)
                for t in range(T):
                    reached(pe, max_taken, b, 2 * PAIRS, 2 * pair + t - 1)
                    bank = score_bank[t]
                    nc.tensor.matmul(bank[:, 0:2 * SPAN], identb[:], keep["band"][:, t * 2 * SPAN:(t + 1) * 2 * SPAN],
                                     start=True, stop=False)
                    for e in range(2):
                        h = 2 * pair + e
                        last = nc.tensor.matmul(bank[:, e * SPAN:(e + 1) * SPAN],
                                                q_stack[b.buf][0:STACK, h, t * P:(t + 1) * P],
                                                k_stack[b.buf][0:STACK, h, t * FAR:t * FAR + SPAN],
                                                start=False, stop=(e == 1))
                    last.then_inc(scored, 1)

            def scoresT(b, pair):
                if not b.real:
                    return
                if pair % 4 == 0:
                    pe.wait_ge(shift_loaded[pair // 4][b.buf], b.rnd * 16 * SHIFT + 16 * SHIFT)
                for c in range(T):
                    reached(pe, exp_done, b, 2 * PAIRS, 2 * pair + c - 1)
                    for e in range(2):
                        h = 2 * pair + e
                        last = nc.tensor.matmul(scoreT_bank[c][:, e * SPAN:(e + 1) * SPAN],
                                                k_stack[b.buf][0:STACK + SHIFT, h, c * P:(c + 1) * P],
                                                q_stack[b.buf][0:STACK + SHIFT, h, c * FAR:c * FAR + SPAN],
                                                start=True, stop=True)
                    last.then_inc(scoredT, 1)

            def weigh(b, pair):
                if not b.real:
                    return
                half, col = pair // 4, (pair // 2 % 2) * S
                if pair == 0:
                    reached(pe, v_copied, b, 1, 1)
                if pair % 4 == 0:
                    reached(pe, outT_copied, b, 2, half - 1)
                reached(pe, band_cut, b, 2 * PAIRS, 2 * pair + 2)
                for e in range(2):
                    h = 2 * pair + e
                    row = (h % 4) * OUT
                    for c in range(T):
                        last = nc.tensor.matmul(out_bank[half][row:row + OUT, col + c * FAR:col + c * FAR + SPAN],
                                                V[b.buf][:, c * H + h // 2 + PAIRS * (h % 2), :], probs[(2 * pair + c) % RING][:, e, :],
                                                start=(c == 0), stop=(c == T - 1), skip_group_check=True)
                last.then_inc(weighted, 1)

            def shift_rows(b, half):
                if not b.real:
                    return
                reached(pe, shift_ready, b, HALVES, half + 1)
                for t in range(T):
                    last = nc.tensor.transpose(bank_b[0:SHIFT * 8, t * P // 2:(t + 1) * P // 2].bitcast(BF16),
                                               shift[:, t, half, :, :].rearrange("p a h -> p (a h)"), identb[:])
                last.then_inc(shift_transposed, 1)

            def out_rows(b, t, bank):
                if not b.real:
                    return
                for quad in range(4):
                    last = nc.tensor.transpose(bank[:, quad * P:(quad + 1) * P], outT[:, quad, t * P:(t + 1) * P],
                                               ident[:])
                last.then_inc(out_transposed, 1)

            def steps(rnd, unit):
                b0, b1, b2, b3, b4 = (Batch(rnd, unit, k) for k in range(5))
                for slot in range(SLOTS):
                    if slot == 0 and b0.real:
                        reached(pe, c_loaded, b0, 16, 16)
                        if b4.real:
                            reached(pe, attT_copied, b4, 1, 1)
                        else:
                            reached(pe, rest_ready["q"], b0.before(1), 1, 1)
                        transpose4(bank_a, c_in[:].rearrange("p t d -> p (t d)")).then_inc(c_transposed, 1)
                    if slot == 1 and b0.real:
                        reached(pe, x_normed, b0, T, T)
                        reached(pe, cT_copied, b0, 1, 1)
                        transpose4(bank_a, xn[:].rearrange("p t d -> p (t d)")).then_inc(x_transposed, 1)
                    if slot == 2 and b0.real:
                        reached(pe, xT_copied, b0, 1, 1)
                        project(bank_a, xT, keep["WqT"], 0).then_inc(projected["q"], 1)
                    if slot == 3 and b0.real:
                        reached(pe, rotated["k"], b0, 1, 1)
                        transpose4(bank_b, rot["k"]).then_inc(rot_transposed["k"], 1)
                    if slot == 5 and b3.real:
                        reached(pe, outT_copied, b3, 2, 2)
                        reached(pe, rest_ready["q"], b0 if b0.real else Batch(B // NBUF, B % NBUF, 1), 1, 1)
                        out_rows(b3, 0, bank_a)
                        reached(pe, shiftT_copied, b2 if b2.real else Batch(B // NBUF, B % NBUF, 1), HALVES, 2)
                        out_rows(b3, 1, bank_b)
                    if slot == 6 and b3.real:
                        reached(pe, out_normed, b3, T, T)
                        transpose4(bank_a, att[:].rearrange("p t d -> p (t d)")).then_inc(att_transposed, 1)

                    pair, late = pair_at(slot, S_FIRST)
                    scores(Batch(rnd, unit, late), pair)

                    if slot == 0 and b4.real:
                        reached(pe, x2_normed, b4, T, T)
                        reached(pe, shiftT_copied, b2 if b2.real else Batch(B // NBUF, B % NBUF, 1), HALVES, 1)
                        transpose4(bank_b, xn2[:].rearrange("p t d -> p (t d)")).then_inc(x2_transposed, 1)
                    if slot == 1 and b0.real:
                        reached(pe, xn2T_copied, b4, 1, 1)
                        reached(pe, shiftT_copied, b2, HALVES, 1)
                        project(bank_b, cT, keep["WkT"], 1).then_inc(projected["k"], 1)
                    if slot == 3 and b0.real:
                        reached(pe, multiplied["q"], b0, 3, 3)
                        project(bank_a, cT, keep["WvT"], 2).then_inc(projected["v"], 1)
                    if slot == 4:
                        if b0.real:
                            reached(pe, v_copied, b0, 1, 1)
                            reached(pe, rotated["q"], b0, 1, 1)
                            transpose4(bank_a, rot["q"]).then_inc(rot_transposed["q"], 1)
                            reached(pe, rest_ready["k"], b0, 1, 1)
                        shift_rows(b2, 1)
                    if slot == 6 and b3.real:
                        reached(pe, attT_copied, b3, 1, 1)
                        project(bank_b, attT, keep["WoT"], 3).then_inc(att_projected, 1)
                    if slot == 7:
                        if b3.real:
                            reached(pe, x2_ready, b3, 1, 1)
                        elif b2.real or b1.real:
                            reached(pe, rest_ready["k"], b0, 1, 1)
                        shift_rows(b1, 0)

                    pair, late = pair_at(slot, ST_FIRST)
                    scoresT(Batch(rnd, unit, late), pair)
                    pair, late = pair_at(slot, PV_FIRST)
                    weigh(Batch(rnd, unit, late), pair)

            run(pe, steps)


def feed_forward(nc, scratch, out, banks, keep, rows):
    TILES = B * S // TILE
    F = I // P
    HF = F // 2
    UW = HF * TILE
    UNITS = 2 * TILES
    with ExitStack() as ctx:
        def sb(name, shape, dt=F32):
            return ctx.enter_context(nc.sbuf_tensor(name, shape, dt))

        def sem(name):
            return ctx.enter_context(nc.semaphore(name))

        def bufs(name, shape, dt=F32):
            return [sb(f"{name}{k}", shape, dt) for k in range(2)]

        scales = keep["scales"]
        (X_MAX, X_S, X_INV, G_MAX, G_S, G_INV, U_MAX, U_S, U_INV, H_MAX, H_S, H_INV, O_MAX, O_S, O_INV, UNIT_O) = range(16)
        col = lambda k: scales[:, k:k + 1]
        peak = keep["peak"]
        gmx, gmn, umx, hmx, omx = (keep["maxima"][:, k, :] for k in range(5))
        xnT = keep["xnT"]

        carried = sem("carried")
        small = sem("small")
        reduced = sem("reduced")
        asked = sem("asked")

        def scale_chain(dve, first, src, parts, maxi, s, inv, done_small, n_red):
            nc.vector.tensor_reduce(peak[:, 0:1], src, X, ALU.max).then_inc(asked, 1)
            dve.wait_ge(reduced, n_red)
            nc.vector.tensor_scalar(col(s), col(maxi), 1.0 / AQMAX, EPS_Q, ALU.mult, ALU.max).then_inc(small, 1)
            dve.wait_ge(small, done_small + 1)
            nc.vector.reciprocal(col(inv), col(s)).then_inc(small, 1)
            dve.wait_ge(small, done_small + 2)

        with ExitStack() as c1:
            def sb1(name, shape, dt=F32):
                return c1.enter_context(nc.sbuf_tensor(name, shape, dt))

            def sem1(name):
                return c1.enter_context(nc.semaphore(name))

            g_stage = [sb1(f"g_stage{k}", [P, UW]) for k in range(2)]
            xint = sb1("xint", [P, C, TILE], I16)
            x_rounded, x_quantised = sem1("x_rounded"), sem1("x_quantised")
            gate_made, gate_copied, gate_seen = sem1("gate_made"), sem1("gate_copied"), sem1("gate_seen")
            gate_stored = [sem1(f"gate_stored{k}") for k in range(2)]
            scale_set = sem1("scale_set")
            block = c1.enter_context(nc.Block())

            @block.sync
            def _(sp):
                with sp.Fori(0, TILES) as j:
                    for h in range(2):
                        sp.wait_ge(gate_copied, j * F + HF * (h + 1))
                        sp.dma_start(scratch["gate"][j][:, h * UW:(h + 1) * UW], g_stage[h][:])\
                            .then_inc(gate_stored[h], 16)
                for h in range(2):
                    sp.wait_ge(gate_stored[h], 16 * TILES)

            @block.gpsimd
            def _(pool):
                pool.wait_ge(asked, 1)
                nc.gpsimd.partition_all_reduce(col(X_MAX), peak[:, 0:1], P, RMAX).then_inc(reduced, 1)

            @block.vector
            def _(dve):
                scale_chain(dve, True, keep["xmax"][:], B, X_MAX, X_S, X_INV, 0, 1)

                def quantise(j):
                    cols = xnT[:, :, bass.ds(j * TILE, TILE)]
                    nc.vector.tensor_scalar(xint[:], cols, col(X_INV), None, ALU.mult).then_inc(x_rounded, 1)
                    dve.wait_ge(x_rounded, j + 1)
                    nc.vector.tensor_scalar(cols, xint[:], col(X_S), None, ALU.mult).then_inc(x_quantised, 1)
                    dve.wait_ge(x_quantised, j + 1)

                def extremes(j):
                    for h in range(2):
                        dve.wait_ge(gate_copied, j * F + HF * (h + 1))
                        nc.vector.tensor_reduce(gmx[:, bass.ds(j * 2 + h, 1)], g_stage[h][:], X, ALU.max)
                        nc.vector.tensor_reduce(gmn[:, bass.ds(j * 2 + h, 1)], g_stage[h][:], X, ALU.min)\
                            .then_inc(gate_seen, 1)

                quantise(0)
                with dve.Fori(0, TILES - 1) as j:
                    quantise(j + 1)
                    extremes(j)
                extremes(TILES - 1)
                dve.wait_ge(gate_seen, UNITS)

            @block.scalar
            def _(act):
                def copies(j, first):
                    for f in range(F):
                        h = f // HF
                        act.wait_ge(gate_made, j * F + f + 1)
                        if f % HF == 0 and not first:
                            act.wait_ge(gate_seen, j * 2 + h - 1)
                            act.wait_ge(gate_stored[h], j * 16)
                        nc.scalar.activation(g_stage[h][:, (f % HF) * TILE:(f % HF + 1) * TILE], banks[f][:], ACT.Copy)\
                            .then_inc(gate_copied, 1)
                copies(0, True)
                with act.Fori(1, TILES) as j:
                    copies(j, False)

            @block.tensor
            def _(pe):
                def products(j, first):
                    pe.wait_ge(x_quantised, j + 1)
                    for f in range(F):
                        if not first:
                            pe.wait_ge(gate_copied, j * F - F + f + 1)
                        for c in range(C):
                            last = nc.tensor.matmul(banks[f][:], keep["w_gateT"][:, c * I + f * P:c * I + (f + 1) * P],
                                                    xnT[:, c, bass.ds(j * TILE, TILE)], start=(c == 0), stop=(c == C - 1))
                        last.then_inc(gate_made, 1)
                products(0, True)
                with pe.Fori(1, TILES) as j:
                    products(j, False)

        with ExitStack() as c2:
            def sb2(name, shape, dt=F32):
                return c2.enter_context(nc.sbuf_tensor(name, shape, dt))

            def sem2(name):
                return c2.enter_context(nc.semaphore(name))

            u_stage = [sb2(f"u_stage{k}", [P, UW]) for k in range(2)]
            g_in = [sb2(f"g_in{k}", [P, UW]) for k in range(2)]
            g_int = [sb2(f"g_int{k}", [P, UW], I16) for k in range(2)]
            sig = [sb2(f"sig{k}", [P, UW]) for k in range(2)]
            sig_int = [sb2(f"sig_int{k}", [P, UW], U16) for k in range(2)]
            silu = [sb2(f"silu{k}", [P, UW]) for k in range(2)]
            unit_max, max_kept = sb2("unit_max_h", [P, 2]), sem2("h_max_kept")
            probe = sb2("probe", [P, 4])
            probe_int = sb2("probe_int", [P, 1], I16)
            probe_sig = sb2("probe_sig", [P, 1], U16)
            up_made, up_copied, up_seen = sem2("up_made"), sem2("up_copied"), sem2("up_seen")
            up_stored = [sem2(f"up_stored{k}") for k in range(2)]
            gate_loaded = [sem2(f"gate_loaded{k}") for k in range(2)]
            silu_stored = [sem2(f"silu_stored{k}") for k in range(2)]
            gate_rounded, sig_done = sem2("gate_rounded"), sem2("sig_done")
            sig_rounded, silu_done = sem2("sig_rounded"), sem2("silu_done")
            scale_ready, probe_step, probe_act = sem2("scale_ready"), sem2("probe_step"), sem2("probe_act")
            block = c2.enter_context(nc.Block())

            @block.sync
            def _(sp):
                def load(j, h):
                    sp.dma_start(g_in[h][:], scratch["gate"][j][:, h * UW:(h + 1) * UW]).then_inc(gate_loaded[h], 16)

                def store(j, h):
                    sp.wait_ge(up_copied, j * F + HF * (h + 1))
                    sp.dma_start(scratch["up"][j][:, h * UW:(h + 1) * UW], u_stage[h][:]).then_inc(up_stored[h], 16)
                    sp.wait_ge(silu_done, j * 2 + h + 1)
                    sp.dma_start(scratch["silu"][j][:, h * UW:(h + 1) * UW], silu[h][:]).then_inc(silu_stored[h], 16)

                for h in range(2):
                    load(0, h)
                with sp.Fori(1, TILES) as j:
                    for h in range(2):
                        sp.wait_ge(gate_rounded, j * 2 + h - 1)
                        load(j, h)
                        store(j - 1, h)
                for h in range(2):
                    store(TILES - 1, h)
                for h in range(2):
                    sp.wait_ge(up_stored[h], 16 * TILES)
                    sp.wait_ge(silu_stored[h], 16 * TILES)

            @block.gpsimd
            def _(pool):
                pool.wait_ge(asked, 3)
                nc.gpsimd.partition_all_reduce(col(G_MAX), peak[:, 0:1], P, RMAX).then_inc(reduced, 1)
                nc.gpsimd.partition_all_reduce(probe[:, 0:1], peak[:, 1:2], P, RMAX).then_inc(reduced, 1)

            @block.vector
            def _(dve):
                nc.vector.tensor_reduce(peak[:, 1:2], gmx, X, ALU.max).then_inc(asked, 1)
                nc.vector.tensor_reduce(peak[:, 2:3], gmn, X, ALU.min).then_inc(small, 1)
                dve.wait_ge(asked, 2)
                dve.wait_ge(small, 3)
                nc.vector.scalar_tensor_tensor(peak[:, 0:1], peak[:, 2:3], -1.0, peak[:, 1:2], ALU.mult, ALU.max)\
                    .then_inc(asked, 1)
                dve.wait_ge(reduced, 3)
                nc.vector.tensor_scalar(col(G_S), col(G_MAX), 1.0 / AQMAX, EPS_Q, ALU.mult, ALU.max).then_inc(small, 1)
                dve.wait_ge(small, 4)
                nc.vector.reciprocal(col(G_INV), col(G_S)).then_inc(small, 1)
                nc.vector.tensor_scalar(col(UNIT_O), col(G_S), -1.0 / 65536.0, None, ALU.mult).then_inc(small, 1)
                dve.wait_ge(small, 6)
                nc.vector.tensor_scalar(probe_int[:], probe[:, 0:1], col(G_INV), None, ALU.mult).then_inc(scale_ready, 1)
                dve.wait_ge(probe_act, 1)
                nc.vector.tensor_scalar(probe_sig[:], probe[:, 1:2], 65536.0, 65535.0, ALU.mult, ALU.min)\
                    .then_inc(probe_step, 1)
                dve.wait_ge(probe_step, 1)
                nc.vector.tensor_scalar(probe[:, 2:3], probe_sig[:], col(UNIT_O), -1.0, ALU.mult, ALU.mult)\
                    .then_inc(probe_step, 1)
                dve.wait_ge(probe_step, 2)
                nc.vector.tensor_tensor(peak[:, 3:4], probe[:, 2:3], probe_int[:], ALU.mult).then_inc(probe_step, 1)

                def unit(j, h, first):
                    dve.wait_ge(sig_done, j * 2 + h + 1)
                    nc.vector.tensor_scalar(sig_int[h][:], sig[h][:], 65536.0, 65535.0, ALU.mult, ALU.min)\
                        .then_inc(sig_rounded, 1)
                    dve.wait_ge(up_copied, j * F + HF * (h + 1))
                    nc.vector.tensor_reduce(umx[:, bass.ds(j * 2 + h, 1)], u_stage[h][:], X, ALU.max,
                                            apply_absolute_value=True).then_inc(up_seen, 1)
                    dve.wait_ge(sig_rounded, j * 2 + h + 1)
                    if not first:
                        dve.wait_ge(silu_stored[h], j * 16)
                    carry(dve, carried)
                    nc.vector.tensor_tensor_reduce(out=silu[h][:], in0=g_int[h][:], in1=sig_int[h][:],
                                                   scale=col(UNIT_O), scalar=0.0, op0=ALU.mult, op1=ALU.max,
                                                   accum_out=unit_max[:, h:h + 1]).then_inc(silu_done, 1)
                    dve.wait_ge(silu_done, j * 2 + h + 1)
                    nc.vector.tensor_copy(hmx[:, bass.ds(j * 2 + h, 1)], unit_max[:, h:h + 1]).then_inc(max_kept, 1)

                for h in range(2):
                    unit(0, h, True)
                with dve.Fori(1, TILES) as j:
                    for h in range(2):
                        unit(j, h, False)
                dve.wait_ge(silu_done, UNITS)
                dve.wait_ge(max_kept, UNITS)
                dve.wait_ge(up_seen, UNITS)
                dve.wait_ge(probe_step, 3)

            @block.scalar
            def _(act):
                act.wait_ge(scale_ready, 1)
                nc.scalar.activation(probe[:, 1:2], probe_int[:], ACT.Sigmoid, scale=col(G_S)).then_inc(probe_act, 1)

                def unit(j, h, first):
                    for k in range(HF):
                        f = h * HF + k
                        act.wait_ge(up_made, j * F + f + 1)
                        if k == 0 and not first:
                            act.wait_ge(up_seen, j * 2 + h - 1)
                            act.wait_ge(up_stored[h], j * 16)
                        nc.scalar.activation(u_stage[h][:, k * TILE:(k + 1) * TILE], banks[f][:], ACT.Copy)\
                            .then_inc(up_copied, 1)
                    act.wait_ge(gate_loaded[h], j * 16 + 16)
                    if not first:
                        act.wait_ge(silu_done, j * 2 + h - 1)
                    nc.scalar.activation(g_int[h][:], g_in[h][:], ACT.Copy, scale=col(G_INV)).then_inc(gate_rounded, 1)
                    act.wait_ge(gate_rounded, j * 2 + h + 1)
                    if not first:
                        act.wait_ge(sig_rounded, j * 2 + h - 1)
                    nc.scalar.activation(sig[h][:], g_int[h][:], ACT.Sigmoid, scale=col(G_S)).then_inc(sig_done, 1)

                for h in range(2):
                    unit(0, h, True)
                with act.Fori(1, TILES) as j:
                    for h in range(2):
                        unit(j, h, False)

            @block.tensor
            def _(pe):
                def products(j, first):
                    for f in range(F):
                        if not first:
                            pe.wait_ge(up_copied, j * F - F + f + 1)
                        for c in range(C):
                            last = nc.tensor.matmul(banks[f][:], keep["w_upT"][:, c * I + f * P:c * I + (f + 1) * P],
                                                    xnT[:, c, bass.ds(j * TILE, TILE)], start=(c == 0), stop=(c == C - 1))
                        last.then_inc(up_made, 1)
                products(0, True)
                with pe.Fori(1, TILES) as j:
                    products(j, False)

        rows.close()
        silu_int = sb("silu_int", [P, TILES * 2 * UW], I16)

        with ExitStack() as c3:
            def sb3(name, shape, dt=F32):
                return c3.enter_context(nc.sbuf_tensor(name, shape, dt))

            def sem3(name):
                return c3.enter_context(nc.semaphore(name))

            N = 2
            h_in = [sb3(f"h_in{k}", [P, UW]) for k in range(N)]
            u_in = [sb3(f"u_in{k}", [P, UW]) for k in range(N)]
            h_abs = [sb3(f"h_abs{k}", [P, UW], I16) for k in range(N)]
            u_abs = [sb3(f"u_abs{k}", [P, UW], I16) for k in range(N)]
            unit_max, max_kept = sb3("unit_max_o", [P, 2]), sem3("o_max_kept")
            prod = sb3("prod", [P, UW])
            h_loaded, u_loaded = [sem3(f"h_loaded{k}") for k in range(N)], [sem3(f"u_loaded{k}") for k in range(N)]
            silu_rounded, silu_sized, up_sized, prod_seen = (sem3("silu_rounded"), sem3("silu_sized"),
                                                             sem3("up_sized"), sem3("prod_seen"))
            scales_known = sem3("scales_known")
            block = c3.enter_context(nc.Block())

            @block.sync
            def _(sp):
                def load(j, h):
                    sp.dma_start(h_in[h][:], scratch["silu"][j][:, h * UW:(h + 1) * UW]).then_inc(h_loaded[h], 16)
                    sp.dma_start(u_in[h][:], scratch["up"][j][:, h * UW:(h + 1) * UW]).then_inc(u_loaded[h], 16)
                for h in range(N):
                    load(0, h)
                with sp.Fori(1, TILES) as j:
                    for h in range(N):
                        sp.wait_ge(silu_rounded, j * 2 + h - 1)
                        sp.wait_ge(silu_sized, j * 2 + h - 1)
                        sp.wait_ge(up_sized, j * 2 + h - 1)
                        load(j, h)

            @block.gpsimd
            def _(pool):
                pool.wait_ge(asked, 4)
                nc.gpsimd.partition_all_reduce(col(U_MAX), peak[:, 0:1], P, RMAX).then_inc(reduced, 1)
                pool.wait_ge(asked, 6)
                nc.gpsimd.partition_all_reduce(col(H_MAX), peak[:, 1:2], P, RMAX).then_inc(reduced, 1)

            @block.vector
            def _(dve):
                nc.vector.tensor_reduce(peak[:, 0:1], umx, X, ALU.max).then_inc(asked, 1)
                nc.vector.tensor_reduce(peak[:, 2:3], hmx, X, ALU.max).then_inc(asked, 1)
                dve.wait_ge(asked, 5)
                nc.vector.tensor_tensor(peak[:, 1:2], peak[:, 2:3], peak[:, 3:4], ALU.max).then_inc(asked, 1)
                dve.wait_ge(reduced, 4)
                nc.vector.tensor_scalar(col(U_S), col(U_MAX), 1.0 / AQMAX, EPS_Q, ALU.mult, ALU.max).then_inc(small, 1)
                dve.wait_ge(reduced, 5)
                nc.vector.tensor_scalar(col(H_S), col(H_MAX), 1.0 / AQMAX, EPS_Q, ALU.mult, ALU.max).then_inc(small, 1)
                dve.wait_ge(small, 8)
                nc.vector.reciprocal(col(U_INV), col(U_S)).then_inc(scales_known, 1)
                nc.vector.reciprocal(col(H_INV), col(H_S)).then_inc(scales_known, 1)
                dve.wait_ge(scales_known, 2)

                def unit(j, h):
                    dve.wait_ge(h_loaded[h], j * 16 + 16)
                    mine = silu_int[:, bass.ds(j * (2 * UW) + h * UW, UW)]
                    nc.vector.tensor_scalar(mine, h_in[h][:], col(H_INV), None, ALU.mult).then_inc(silu_rounded, 1)
                    dve.wait_ge(silu_sized, j * 2 + h + 1)
                    dve.wait_ge(up_sized, j * 2 + h + 1)
                    carry(dve, carried)
                    nc.vector.tensor_tensor_reduce(out=prod[:], in0=h_abs[h][:], in1=u_abs[h][:], scale=1.0,
                                                   scalar=0.0, op0=ALU.mult, op1=ALU.max,
                                                   accum_out=unit_max[:, h:h + 1]).then_inc(prod_seen, 1)
                    dve.wait_ge(prod_seen, j * 2 + h + 1)
                    nc.vector.tensor_copy(omx[:, bass.ds(j * 2 + h, 1)], unit_max[:, h:h + 1]).then_inc(max_kept, 1)

                with dve.Fori(0, TILES) as j:
                    for h in range(N):
                        unit(j, h)
                dve.wait_ge(max_kept, UNITS)

            @block.scalar
            def _(act):
                act.wait_ge(scales_known, 2)

                def unit(j, h, first):
                    act.wait_ge(u_loaded[h], j * 16 + 16)
                    if not first:
                        act.wait_ge(prod_seen, j * 2 + h - 1)
                    nc.scalar.activation(u_abs[h][:], u_in[h][:], ACT.Abs, scale=col(U_INV)).then_inc(up_sized, 1)
                    act.wait_ge(h_loaded[h], j * 16 + 16)
                    nc.scalar.activation(h_abs[h][:], h_in[h][:], ACT.Abs, scale=col(H_INV)).then_inc(silu_sized, 1)
                for h in range(N):
                    unit(0, h, True)
                with act.Fori(1, TILES) as j:
                    for h in range(N):
                        unit(j, h, False)

        with ExitStack() as c4:
            def sb4(name, shape, dt=F32):
                return c4.enter_context(nc.sbuf_tensor(name, shape, dt))

            def sem4(name):
                return c4.enter_context(nc.semaphore(name))

            u_in = [sb4(f"up_in{k}", [P, UW]) for k in range(2)]
            u_int = [sb4(f"u_int{k}", [P, UW], I16) for k in range(2)]
            o_int = [sb4(f"o_int{k}", [P, UW], I16) for k in range(2)]
            o = [sb4(f"o{k}", [P, UW]) for k in range(2)]
            SUB = TILE // P
            x2_in = sb4("x2_in", [P, SUB, D])
            y = sb4("y", [P, SUB, D])
            up_loaded = [sem4(f"up_loaded{k}") for k in range(2)]
            x2_loaded, y_stored = sem4("x2_loaded"), sem4("y_stored")
            up_rounded, o_rounded, o_ready, y_made, y_ready = (sem4("up_rounded"), sem4("o_rounded"), sem4("o_ready"),
                                                               sem4("y_made"), sem4("y_ready"))
            o_scale, o_step = sem4("o_scale"), sem4("o_step")
            x2_rows = scratch["x2"].rearrange("b p t d -> p b t d")
            out_rows = out.rearrange("b (t p) d -> p b t d", p=P)
            BT = TILE // S
            block = c4.enter_context(nc.Block())

            @block.sync
            def _(sp):
                def load(j, h):
                    sp.dma_start(u_in[h][:], scratch["up"][j][:, h * UW:(h + 1) * UW]).then_inc(up_loaded[h], 16)

                def load_x2(j):
                    sp.dma_start(x2_in[:].rearrange("p (b t) d -> p b t d", b=BT), x2_rows[:, bass.ds(j * BT, BT)])\
                        .then_inc(x2_loaded, 16)

                def store(j):
                    sp.wait_ge(y_ready, j * SUB + SUB)
                    for k in range(BT):
                        sp.dma_start(out_rows[:, j * BT + k], y[:, k * T:(k + 1) * T, :]).then_inc(y_stored, 16)

                for h in range(2):
                    load(0, h)
                load_x2(0)
                with sp.Fori(1, TILES) as j:
                    for h in range(2):
                        sp.wait_ge(up_rounded, j * 2 + h - 1)
                        load(j, h)
                    store(j - 1)
                    load_x2(j)
                store(TILES - 1)
                sp.wait_ge(y_stored, 16 * BT * TILES)

            @block.gpsimd
            def _(pool):
                pool.wait_ge(asked, 7)
                nc.gpsimd.partition_all_reduce(col(O_MAX), peak[:, 4:5], P, RMAX).then_inc(reduced, 1)

            @block.vector
            def _(dve):
                nc.vector.tensor_reduce(peak[:, 4:5], omx, X, ALU.max).then_inc(asked, 1)
                nc.vector.tensor_tensor(col(UNIT_O), col(H_S), col(U_S), ALU.mult).then_inc(o_step, 1)
                dve.wait_ge(reduced, 6)
                dve.wait_ge(o_step, 1)
                nc.vector.tensor_tensor(peak[:, 5:6], col(O_MAX), col(UNIT_O), ALU.mult).then_inc(o_step, 1)
                dve.wait_ge(o_step, 2)
                nc.vector.tensor_scalar(col(O_S), peak[:, 5:6], 1.0 / AQMAX, EPS_Q, ALU.mult, ALU.max).then_inc(o_step, 1)
                dve.wait_ge(o_step, 3)
                nc.vector.reciprocal(peak[:, 6:7], col(O_S)).then_inc(o_step, 1)
                dve.wait_ge(o_step, 4)
                nc.vector.scalar_tensor_tensor(col(O_INV), peak[:, 6:7], -1.0, col(UNIT_O), ALU.mult, ALU.mult)\
                    .then_inc(o_scale, 1)
                dve.wait_ge(o_scale, 1)

                def round_product(j, h, first):
                    dve.wait_ge(up_rounded, j * 2 + h + 1)
                    if not first:
                        dve.wait_ge(o_ready, j * 2 + h - 1)
                    nc.vector.scalar_tensor_tensor(o_int[h][:], silu_int[:, bass.ds(j * (2 * UW) + h * UW, UW)],
                                                   col(O_INV), u_int[h][:], ALU.mult, ALU.mult).then_inc(o_rounded, 1)

                def residual(j, first):
                    dve.wait_ge(x2_loaded, j * 16 + 16)
                    if not first:
                        dve.wait_ge(y_stored, j * 16 * BT)
                    for s in range(SUB):
                        dve.wait_ge(y_made, j * SUB + s + 1)
                        nc.vector.scalar_tensor_tensor(y[:, s, :], banks[s % 2 + 2 * (s // 2)][:, 0:D], keep["tanh"][:, 1:2],
                                                       x2_in[:, s, :], ALU.mult, ALU.add).then_inc(y_ready, 1)

                for h in range(2):
                    round_product(0, h, True)
                residual_first = True
                for h in range(2):
                    round_product(1, h, False)
                residual(0, residual_first)
                with dve.Fori(2, TILES) as j:
                    for h in range(2):
                        round_product(j, h, False)
                    residual(j - 1, False)
                residual(TILES - 1, False)

            @block.scalar
            def _(act):
                act.wait_ge(o_scale, 1)

                def unit(j, h, first):
                    act.wait_ge(up_loaded[h], j * 16 + 16)
                    if not first:
                        act.wait_ge(o_rounded, j * 2 + h - 1)
                    nc.scalar.activation(u_int[h][:], u_in[h][:], ACT.Copy, scale=col(U_INV)).then_inc(up_rounded, 1)

                def dequantise(j, h, first):
                    act.wait_ge(o_rounded, j * 2 + h + 1)
                    if not first:
                        act.wait_ge(y_made, j * SUB)
                    nc.scalar.activation(o[h][:], o_int[h][:], ACT.Copy, scale=col(O_S)).then_inc(o_ready, 1)

                for h in range(2):
                    unit(0, h, True)
                for h in range(2):
                    dequantise(0, h, True)
                with act.Fori(1, TILES) as j:
                    for h in range(2):
                        unit(j, h, False)
                    for h in range(2):
                        dequantise(j, h, False)

            @block.tensor
            def _(pe):
                def rows(j, first):
                    for s in range(SUB):
                        bank = banks[s % 2 + 2 * (s // 2)]
                        if not first:
                            pe.wait_ge(y_ready, j * SUB - SUB + s + 1)
                        for f in range(F):
                            if s == 0 and f % HF == 0:
                                pe.wait_ge(o_ready, j * 2 + f // HF + 1)
                            at = (f % HF) * TILE + s * P
                            last = nc.tensor.matmul(bank[:, 0:D], o[f // HF][:, at:at + P],
                                                    keep["w_downT"][:, f * D:(f + 1) * D],
                                                    start=(f == 0), stop=(f == F - 1))
                        last.then_inc(y_made, 1)
                rows(0, True)
                with pe.Fori(1, TILES) as j:
                    rows(j, False)


def build(nc, dram, x, ctx_in, w, out):
    tile_of = nc.dram_tensor("gate_scratch", (B * S // TILE, P, I // P * TILE), F32, kind="Internal").ap()
    up = nc.dram_tensor("up_scratch", (B * S // TILE, P, I // P * TILE), F32, kind="Internal").ap()
    silu = nc.dram_tensor("silu_scratch", (B * S // TILE, P, I // P * TILE), F32, kind="Internal").ap()
    x2 = nc.dram_tensor("x2_scratch", (B, P, T, D), F32, kind="Internal").ap()
    scratch = {"gate": tile_of, "up": up, "silu": silu, "x2": x2}
    for n in "qk":
        parts = nc.dram_tensor(f"{n}_parts_scratch", (NBUF, 3, DK, H * S), BF16, kind="Internal").ap()
        scratch[n] = parts

        def rows_of(buf, g, n=n, parts=parts):
            if n == "q":
                return parts[buf][g].unsqueeze(0).to_broadcast([3 - g, DK, H * S])
            return parts[buf][0:3 - g]

        scratch[n + "_rows"] = rows_of

    with ExitStack() as ctx:
        def sb(name, shape, dt=F32):
            return ctx.enter_context(nc.sbuf_tensor(name, shape, dt))

        banks = [ctx.enter_context(nc.psum_tensor(f"bank{k}", [P, 512], F32)) for k in range(8)]
        keep = {
            "ident": sb("ident", [P, P]), "identb": sb("identb", [P, P], BF16),
            "cos": sb("cos", [P, T * D]), "sin": sb("sin", [P, T * D]), "band": sb("band", [P, T * 2 * SPAN], BF16),
            "ones3": sb("ones3", [3, P], BF16), "bias": sb("bias", [3, 4 * D], BF16),
            "lnconst": sb("lnconst", [P, 4]), "tanh": sb("tanh", [P, 2]),
            "xmax": sb("xmax", [P, B]), "scales": sb("scales", [P, 16]), "peak": sb("peak", [P, 8]),
            "maxima": sb("maxima", [P, 5, 2 * B * S // TILE]),
        }
        for n in ("Wq", "Wk", "Wv", "Wo"):
            keep[n + "T"] = sb(n + "T", [P, C * D])
        for n in ("w_gate", "w_up", "w_down"):
            keep[n + "T"] = sb(n + "T", [P, I * D // P])
        rows = ctx.enter_context(ExitStack())
        keep["xnT"] = rows.enter_context(nc.sbuf_tensor("xnT", [P, C, B * S], F32))
        prepare(nc, dram, w, banks, keep)
        attention(nc, dram, x, ctx_in, scratch, banks, keep)
        feed_forward(nc, scratch, out, banks, keep, rows)


def tables():
    inv = np.float32(1.0) / np.float32(10000.0) ** (np.arange(0, DK, 2, dtype=np.float32) / np.float32(DK))
    angle = np.arange(S, dtype=np.float32)[:, None] * inv[None, :].astype(np.float32)
    cos, sin = np.cos(angle).astype(np.float32), np.sin(angle).astype(np.float32)
    cos = np.tile(np.concatenate([cos, cos], 1), (1, H))
    sin = np.tile(np.concatenate([-sin, sin], 1), (1, H))
    lay = lambda a: np.ascontiguousarray(a.reshape(T, P, D).transpose(1, 0, 2).reshape(P, T * D))
    band = np.zeros((P, T, 2, SPAN), np.float32)
    for t in range(T):
        query = t * P + np.arange(P)[:, None]
        key = t * FAR + np.arange(SPAN)[None, :]
        band[:, t] = np.where(np.abs(query - key) <= WINDOW, 0.0, -1e9)[:, None, :]
    return {"cos": lay(cos), "sin": lay(sin), "band": band.reshape(P, -1), "ident": np.eye(P, dtype=np.float32)}


_INS = ["x", "ctx_1024", "g_xattn", "g_ffn", "L0_xattn_Wq", "L0_xattn_bq", "L0_xattn_Wk", "L0_xattn_bk",
        "L0_xattn_Wv", "L0_xattn_bv", "L0_xattn_Wo", "L0_xattn_bo", "L0_ffn_w_gate", "L0_ffn_w_up", "L0_ffn_w_down"]


def kernel(**inputs):
    import ml_dtypes
    import numpy as _np
    import concourse.bacc as _bacc
    from concourse import mybir as _mybir
    from concourse.bass_utils import run_bass_kernel_spmd as _run

    nc = _bacc.Bacc("TRN2", target_bir_lowering=False, num_devices=1)
    arrays, aps = {}, {}
    for name in _INS:
        a = _np.ascontiguousarray(inputs[name])
        arrays[f"in_{name}"] = a
        aps[name] = nc.dram_tensor(f"in_{name}", a.shape, _mybir.dt.from_np(a.dtype), kind="ExternalInput").ap()
    dram = {}
    for name, a in tables().items():
        a = a.astype(ml_dtypes.bfloat16) if name == "band" else a
        arrays[f"table_{name}"] = a
        dram[name] = nc.dram_tensor(f"table_{name}", a.shape, _mybir.dt.from_np(a.dtype), kind="ExternalInput").ap()
    out = nc.dram_tensor("out", (B, S, D), F32, kind="ExternalOutput").ap()
    w = {n.rsplit("L0_xattn_")[-1].rsplit("L0_ffn_")[-1]: a for n, a in aps.items()}
    build(nc, dram, aps["x"], aps["ctx_1024"], w, out)
    r = _run(nc, [arrays], core_ids=[0])
    return r.results[0]["out"]
```

```python
from contextlib import ExitStack

import numpy as np

import concourse.bass as bass
from concourse import mybir

F32 = mybir.dt.float32
BF16 = mybir.dt.bfloat16
F16 = mybir.dt.float16
I16 = mybir.dt.int16
U16 = mybir.dt.uint16
ALU = mybir.AluOpType
ACT = mybir.ActivationFunctionType
X = mybir.AxisListType.X
XY = mybir.AxisListType.XY
RMAX = bass.bass_isa.ReduceOp.max

P = 128
B, S, D = 32, 256, 256
H, DK = 16, 16
HALF = DK // 2
I = 768
WINDOW = 50
BLOCK, WQMAX = 32, 7.0
AQMAX = 32767.0
EPS_LN, EPS_Q = 1e-5, 1e-12
WTOP = 2048.0
PRODUCTS = ((0, 0), (0, 1), (1, 0))
T = S // P
C = D // P
SPAN = P + WINDOW
FAR = S - SPAN
PAIRS = H // 2
SLOTS = PAIRS
NBUF = 3
HALVES = 2
STACK_Q = (0, 0, 0, 1, 1, 2)
STACK_K = (0, 1, 2, 0, 1, 0)
STACK = len(STACK_Q) * DK
SHIFT = 2
OUT = 2 * DK
TILE = 512
RING = 6
FIRST_ROUND, LAST_ROUND = 3, B // NBUF
LATE = 4


class Batch:

    def __init__(self, rnd, unit, late):
        back, self.buf = divmod(unit - late, NBUF)
        self.rnd = rnd + back
        self.n = self.rnd * NBUF + self.buf
        self.fixed = isinstance(self.n, int)
        self.real = 0 <= self.n < B if self.fixed else True

    def before(self, k):
        return Batch(self.rnd, self.buf, k)


def ring_tile(probs, b, pair, c):
    return probs[(b.buf * T * PAIRS + T * pair + c) % RING]


def reached(eng, sem, batch, per, k):
    value = batch.n * per + k
    if isinstance(value, int) and value <= 0:
        return
    eng.wait_ge(sem, value)


def carry(eng, sem):
    eng.sem_inc(sem, 1)


def loaded(eng, sems, batch):
    eng.wait_ge(sems[batch.buf], batch.rnd * 16 + 16)


def prepare(nc, dram, w, banks, keep):
    with ExitStack() as ctx:
        def sb(name, shape, dt=F32):
            return ctx.enter_context(nc.sbuf_tensor(name, shape, dt))

        def sem(name):
            return ctx.enter_context(nc.semaphore(name))

        attn = ("Wq", "Wk", "Wv", "Wo")
        ffn = ("w_gate", "w_up", "w_down")
        nat = {n: sb(f"nat_{n}", [P, T * D]) for n in attn}
        nat.update({n: sb(f"nat_{n}", [P, I * D // P]) for n in ffn})
        brow = sb("brow", [1, 4 * D])
        bpart = sb("bpart", [1, 3, 4 * D], BF16)
        brest = sb("brest", [1, 4 * D])
        brest2 = sb("brest2", [1, 4 * D])
        grow = sb("grow", [1, 2])
        one_row = sb("one_row", [1, P])
        nblk = I * D // P // BLOCK
        wabs = sb("wabs", [P, nblk])
        wscale = sb("wscale", [P, nblk])
        winv = sb("winv", [P, nblk])
        wint = sb("wint", [P, I * D // P])
        wround = sb("wround", [P, I * D // P], I16)
        consts_in = sem("consts_in")
        gates_in = sem("gates_in")
        bias_in = sem("bias_in")
        nat_in = {n: sem(f"in_{n}") for n in attn + ffn}
        weight_quantised = sem("weight_quantised")
        scales_max, scales_spread = sem("scales_max"), sem("scales_spread")
        low_parts = sem("low_parts")
        smax = sb("smax", [P, 2 * len(ffn)])
        dve_step = sem("dve_step")
        part_step = sem("part_step")
        ones_set = sem("ones_set")
        blocks_transposed = sem("blocks_transposed")
        bank_copied = sem("bank_copied")
        gates_spread = sem("gates_spread")
        bias_rows = sem("bias_rows")
        block = ctx.enter_context(nc.Block())

        @block.sync
        def _(sp):
            sp.dma_start(keep["ident"][:], dram["ident"]).then_inc(consts_in, 16)
            for n in attn:
                sp.dma_start(nat[n][:].rearrange("p (o i) -> p o i", o=T),
                             w[n].rearrange("(o p) i -> p o i", p=P)).then_inc(nat_in[n], 16)
            for n in ffn:
                rows = w[n].shape[0] // P
                sp.dma_start(nat[n][:].rearrange("p (o i) -> p o i", o=rows),
                             w[n].rearrange("(o p) i -> p o i", p=P)).then_inc(nat_in[n], 16)
            sp.dma_start(keep["cos"][:], dram["cos"]).then_inc(consts_in, 16)
            sp.dma_start(keep["sin"][:], dram["sin"]).then_inc(consts_in, 16)
            sp.dma_start(keep["band"][:], dram["band"]).then_inc(consts_in, 16)
            for k, n in enumerate(("bq", "bk", "bv", "bo")):
                sp.dma_start(brow[:, k * D:(k + 1) * D], w[n].rearrange("(a n) -> a n", a=1)).then_inc(bias_in, 16)
            sp.dma_start(grow[:, 0:1], w["g_xattn"].rearrange("(a n) -> a n", a=1)).then_inc(gates_in, 16)
            sp.dma_start(grow[:, 1:2], w["g_ffn"].rearrange("(a n) -> a n", a=1)).then_inc(gates_in, 16)
            sp.wait_ge(part_step, 5)
            for k in range(3):
                sp.dma_start(keep["bias"][k:k + 1, :], bpart[:, k, :]).then_inc(bias_rows, 16)
            sp.wait_ge(bias_rows, 48)
            sp.wait_ge(consts_in, 64)

        plan = []
        for n in attn:
            plan.append([(n, o, c, [keep[n + "T"]], D) for c in range(C) for o in range(T)])
        for n in ffn:
            rows, cols = w[n].shape[0] // P, w[n].shape[1] // P
            blks = [(n, o, c, keep[n + "T"], rows * P) for c in range(cols) for o in range(rows)]
            plan += [blks[k:k + 4] for k in range(0, len(blks), 4)]

        def place(blks):
            _, o, c, _, rows = blks[0]
            return c * rows + o * P

        @block.vector
        def _(dve):
            nc.vector.memset(one_row[:], 1.0).then_inc(ones_set, 1)
            nc.vector.memset(keep["ones3"][:], 1.0).then_inc(ones_set, 1)
            for k, value in enumerate((EPS_LN, -0.5, -1.0)):
                nc.vector.memset(keep["lnconst"][:, k * T:(k + 1) * T], value).then_inc(ones_set, 1)
            dve.wait_ge(consts_in, 64)
            nc.vector.tensor_copy(keep["identb"][:], keep["ident"][:]).then_inc(ones_set, 1)
            dve.wait_ge(bias_in, 64)
            nc.vector.tensor_copy(bpart[:, 0, :], brow[:]).then_inc(part_step, 1)
            dve.wait_ge(part_step, 1)
            nc.vector.tensor_tensor(brest[:], brow[:], bpart[:, 0, :], ALU.subtract).then_inc(part_step, 1)
            dve.wait_ge(part_step, 2)
            nc.vector.tensor_copy(bpart[:, 1, :], brest[:]).then_inc(part_step, 1)
            dve.wait_ge(part_step, 3)
            nc.vector.tensor_tensor(brest2[:], brest[:], bpart[:, 1, :], ALU.subtract).then_inc(part_step, 1)
            dve.wait_ge(part_step, 4)
            nc.vector.tensor_copy(bpart[:, 2, :], brest2[:]).then_inc(part_step, 1)
            steps = 0
            banks_used = len(attn)
            for m, n in enumerate(ffn):
                def step(ins):
                    ins.then_inc(dve_step, 1)
                dve.wait_ge(nat_in[n], 16)
                blocks = nat[n][:].rearrange("p (k i) -> p k i", i=BLOCK)
                spread = [P, nblk, BLOCK]
                step(nc.vector.tensor_reduce(wabs[:], blocks, X, ALU.max, apply_absolute_value=True))
                dve.wait_ge(dve_step, steps + 1)
                step(nc.vector.tensor_scalar(wscale[:], wabs[:], 1.0 / WQMAX, EPS_Q, ALU.mult, ALU.max))
                dve.wait_ge(dve_step, steps + 2)
                step(nc.vector.reciprocal(winv[:], wscale[:]))
                nc.vector.tensor_reduce(smax[:, 2 * m:2 * m + 1], wscale[:], X, ALU.max).then_inc(scales_max, 1)
                dve.wait_ge(dve_step, steps + 3)
                step(nc.vector.tensor_tensor(wint[:].rearrange("p (k i) -> p k i", i=BLOCK), blocks,
                                             winv[:].unsqueeze(2).to_broadcast(spread), ALU.mult))
                dve.wait_ge(dve_step, steps + 4)
                step(nc.vector.tensor_copy(wround[:], wint[:]))
                dve.wait_ge(scales_spread, m + 1)
                largest = smax[:, 2 * m + 1:2 * m + 2]
                step(nc.vector.tensor_scalar(keep["unscale"][:, m:m + 1], largest, 1.0 / WTOP, None, ALU.mult))
                dve.wait_ge(dve_step, steps + 6)
                step(nc.vector.reciprocal(smax[:, 2 * m:2 * m + 1], keep["unscale"][:, m:m + 1]))
                dve.wait_ge(dve_step, steps + 7)
                step(nc.vector.tensor_scalar(wscale[:], wscale[:], smax[:, 2 * m:2 * m + 1], None, ALU.mult))
                dve.wait_ge(dve_step, steps + 8)
                nc.vector.tensor_tensor(blocks, wround[:].rearrange("p (k i) -> p k i", i=BLOCK),
                                        wscale[:].unsqueeze(2).to_broadcast(spread), ALU.mult)\
                    .then_inc(weight_quantised, 1)
                steps += 8
                dve.wait_ge(weight_quantised, m + 1)
                for k in range(banks_used, banks_used + nat[n].shape[1] // (4 * P)):
                    dve.wait_ge(bank_copied, k + 1)
                    _, _, _, dst, rows = plan[k][0]
                    at = place(plan[k])
                    nc.vector.tensor_tensor(dst[1][:, at:at + 4 * P], banks[k % 4][:], dst[0][:, at:at + 4 * P],
                                            ALU.subtract).then_inc(low_parts, 1)
                banks_used = k + 1
            dve.wait_ge(low_parts, len(plan) - len(attn))

        @block.gpsimd
        def _(pool):
            for m in range(len(ffn)):
                pool.wait_ge(scales_max, m + 1)
                nc.gpsimd.partition_all_reduce(smax[:, 2 * m + 1:2 * m + 2], smax[:, 2 * m:2 * m + 1], P, RMAX)\
                    .then_inc(scales_spread, 1)

        @block.tensor
        def _(pe):
            pe.wait_ge(ones_set, 6)
            for k, blks in enumerate(plan):
                n = blks[0][0]
                if n in attn:
                    pe.wait_ge(nat_in[n], 16)
                else:
                    pe.wait_ge(weight_quantised, ffn.index(n) + 1)
                if k >= 4:
                    pe.wait_ge(bank_copied, k - 3)
                if k - 4 >= len(attn):
                    pe.wait_ge(low_parts, k - 3 - len(attn))
                for q, (_, o, c, _, _) in enumerate(blks):
                    width = w[n].shape[1]
                    last = nc.tensor.transpose(banks[k % 4][:, q * P:(q + 1) * P],
                                               nat[n][:, o * width + c * P:o * width + (c + 1) * P],
                                               keep["ident"][:])
                last.then_inc(blocks_transposed, 1)
            pe.wait_ge(gates_in, 32)
            nc.tensor.matmul(banks[4][:, 0:2], one_row[:], grow[:], start=True, stop=True).then_inc(gates_spread, 1)

        @block.scalar
        def _(act):
            for k, blks in enumerate(plan):
                act.wait_ge(blocks_transposed, k + 1)
                at = place(blks)
                nc.scalar.activation(blks[0][3][0][:, at:at + 4 * P], banks[k % 4][:], ACT.Copy).then_inc(bank_copied, 1)
            act.wait_ge(gates_spread, 1)
            nc.scalar.activation(keep["tanh"][:], banks[4][:, 0:2], ACT.Tanh).then_inc(bank_copied, 1)
            act.wait_ge(bank_copied, len(plan) + 1)


def attention(nc, dram, x, ctx_in, scratch, banks, keep):
    with ExitStack() as ctx:
        def sb(name, shape, dt=F32):
            return ctx.enter_context(nc.sbuf_tensor(name, shape, dt))

        def sem(name):
            return ctx.enter_context(nc.semaphore(name))

        def bufs(name, shape, dt=F32, n=NBUF):
            return [sb(f"{name}{k}", shape, dt) for k in range(n)]

        W2 = T * D
        x_in, c_in = sb("x_in", [P, T, D]), sb("c_in", [P, T, D])
        stats, moments = sb("stats", [P, T, 6]), sb("moments", [P, T, 2])
        scale, scale_small = sb("ln_scale", [P, 2 * T]), sb("ln_small", [P, 2 * T])
        xn = x_in
        xT, cT = sb("xT", [P, C, S]), sb("cT", [P, C, S])
        by_cos = {n: sb(f"{n}_cos", [P, W2]) for n in "qk"}
        by_sin = {n: sb(f"{n}_sin", [P, W2]) for n in "qk"}
        rot = by_cos
        parts = {n: sb(f"{n}_parts", [P, 3, C * S], BF16) for n in "qk"}
        rest = by_sin
        q_stack, k_stack = bufs("q_stack", [P, H, S], BF16), bufs("k_stack", [P, H, S], BF16)
        V = bufs("V", [P, T * H, OUT])
        smax = bufs("smax", [P, T, H])
        shift = sb("shift", [P, T, HALVES, SHIFT, H // 2], BF16)
        shiftT = bufs("shiftT", [SHIFT * H // 2, S], BF16, HALVES)
        probs = bufs("probs", [P, 2, SPAN], n=RING)
        outT = sb("outT", [P, 4, S])
        rden = sb("rden", [P, T, H])
        att = sb("att", [P, T, D])
        attT = sb("attT", [P, C, S])
        x2 = bufs("x2", [P, T, D])
        stats2, moments2 = sb("stats2", [P, T, 6]), sb("moments2", [P, T, 2])
        scale2, scale2_small = sb("ln_scale2", [P, 2 * T]), sb("ln_small2", [P, 2 * T])
        xn2 = sb("xn2", [P, T, D])

        score_bank, scoreT_bank, out_bank = banks[0:2], banks[2:4], banks[4:6]
        bank_a, bank_b = banks[6], banks[7]
        shift_bank = (out_bank[1], out_bank[0])

        x_loaded, c_loaded = sem("x_loaded"), sem("c_loaded")
        xres_loaded = [sem(f"xres_loaded{k}") for k in range(NBUF)]
        parts_stored = {n: sem(f"{n}_parts_stored") for n in "qk"}
        stack_loaded = {n: [sem(f"{n}_stack_loaded{k}") for k in range(NBUF)] for n in "qk"}
        shift_loaded = [[sem(f"shift_loaded{h}_{k}") for k in range(NBUF)] for h in range(HALVES)]
        x2_stored = [sem(f"x2_stored{k}") for k in range(NBUF)]
        dve_carried, pool_carried, sp_carried = sem("dve_carried"), sem("pool_carried"), sem("sp_carried")
        consts_set = sem("consts_set")
        stats_taken, moments_taken = sem("stats_taken"), sem("moments_taken")
        x_normed = sem("x_normed")
        multiplied = {n: sem(f"{n}_multiplied") for n in "qk"}
        rest_ready = {n: sem(f"{n}_rest_ready") for n in "qk"}
        low_ready = {n: sem(f"{n}_low_ready") for n in "qk"}
        max_taken = sem("max_taken")
        shift_high, shift_ready = sem("shift_high"), sem("shift_ready")
        rden_ready, out_normed = sem("rden_ready"), sem("out_normed")
        x2_ready, stats2_taken, moments2_taken = sem("x2_ready"), sem("stats2_taken"), sem("moments2_taken")
        x2_normed, xmax_taken = sem("x2_normed"), sem("xmax_taken")
        cT_copied, xT_copied, v_copied = sem("cT_copied"), sem("xT_copied"), sem("v_copied")
        high_ready = {n: sem(f"{n}_high_ready") for n in "qk"}
        mid_ready = {n: sem(f"{n}_mid_ready") for n in "qk"}
        shiftT_copied, exp_done = sem("shiftT_copied"), sem("exp_done")
        outT_copied, attT_copied, xn2T_copied = sem("outT_copied"), sem("attT_copied"), sem("xn2T_copied")
        scale_steps, scale_ready = sem("scale_steps"), sem("ln_scale_ready")
        scale2_steps, scale2_ready = sem("scale2_steps"), sem("ln_scale2_ready")
        rotated = {n: sem(f"{n}_rotated") for n in "qk"}
        below_cut, band_cut = sem("below_cut"), sem("band_cut")
        c_transposed, x_transposed = sem("c_transposed"), sem("x_transposed")
        projected = {n: sem(f"{n}_projected") for n in "qkv"}
        rot_transposed = {n: sem(f"{n}_rot_transposed") for n in "qk"}
        shift_transposed = sem("shift_transposed")
        scored, scoredT, weighted = sem("scored"), sem("scoredT"), sem("weighted")
        out_transposed, att_transposed = sem("out_transposed"), sem("att_transposed")
        att_projected, x2_transposed = sem("att_projected"), sem("x2_transposed")


        rows_x = x.rearrange("b (t p) d -> b p t d", p=P)
        rows_c = ctx_in.rearrange("b (t p) d -> b p t d", p=P)

        def run(eng, steps):
            for it in range(-1, FIRST_ROUND * NBUF):
                steps(it // NBUF, it % NBUF)
            with eng.Fori(FIRST_ROUND, LAST_ROUND) as rnd:
                for unit in range(NBUF):
                    steps(rnd, unit)
            for it in range(LAST_ROUND * NBUF, B + LATE + 1):
                steps(it // NBUF, it % NBUF)

        def pair_at(slot, first):
            return (slot - first) % SLOTS, (first + (slot - first) % SLOTS) // SLOTS

        def low(eng, by, b, n):
            if not b.real:
                return
            reached(eng, mid_ready[n], b, 1, 1)
            by.tensor_tensor(parts[n][:, 2, :], rest[n][:], parts[n][:, 1, :], ALU.subtract)\
                .then_inc(low_ready[n], 1)

        S_FIRST, ST_FIRST, PV_FIRST = 11, 18, 20
        block = ctx.enter_context(nc.Block())

        @block.sync
        def _(sp):
            def load_x(b):
                if not b.real:
                    return
                reached(sp, x_transposed, b.before(1), 1, 1)
                sp.dma_start(x_in[:], rows_x[b.n]).then_inc(x_loaded, 16)
                reached(sp, c_transposed, b.before(1), 1, 1)
                sp.dma_start(c_in[:], rows_c[b.n]).then_inc(c_loaded, 16)

            def load_residual(b):
                if not b.real:
                    return
                bb = b.before(NBUF)
                if not bb.fixed or bb.n >= 0:
                    sp.wait_ge(x2_stored[b.buf], bb.rnd * 16 + 16)
                reached(sp, x2_normed, bb, T, T)
                sp.dma_start(x2[b.buf][:], rows_x[b.n]).then_inc(xres_loaded[b.buf], 16)

            def store_parts(b, n):
                if not b.real:
                    return
                reached(sp, mid_ready[n], b, 1, 1)
                reached(sp, low_ready[n], b, 1, 1)
                if not b.fixed:
                    carry(sp, sp_carried)
                if not b.fixed or b.n >= NBUF:
                    sp.wait_ge(stack_loaded[n][b.buf], b.rnd * 48)
                for k in range(3):
                    sp.dma_start(scratch[n][b.buf][k].rearrange("d (h ct) -> h d ct", h=PAIRS), parts[n][:, k, :])\
                        .then_inc(parts_stored[n], 16)

            def load_stacks(b, n):
                if not b.real:
                    return
                stack = (q_stack if n == "q" else k_stack)[b.buf]
                reached(sp, parts_stored[n], b, 48, 48)
                reached(sp, scoredT, b.before(NBUF), 2 * PAIRS, 2 * PAIRS)
                row = 0
                for g in range(3):
                    rows = (3 - g) * DK
                    sp.dma_start(stack[row:row + rows, :, :].rearrange("r s t -> r (s t)"), scratch[n + "_rows"](b.buf, g)).then_inc(stack_loaded[n][b.buf], 16)
                    row += rows

            def load_shift(b, half):
                if not b.real:
                    return
                reached(sp, shiftT_copied, b, HALVES, half + 1)
                for k in range(SHIFT):
                    sp.dma_start(q_stack[b.buf][STACK + k:STACK + k + 1, half * 8:half * 8 + 8, :],
                                 shiftT[half][k * 8:(k + 1) * 8, :]).then_inc(shift_loaded[half][b.buf], 16)

            def store_x2(b):
                if not b.real:
                    return
                reached(sp, x2_ready, b, 1, 1)
                sp.dma_start(scratch["x2"][b.n], x2[b.buf][:]).then_inc(x2_stored[b.buf], 16)

            def steps(rnd, unit):
                load_shift(Batch(rnd, unit, 2), 0)
                load_stacks(Batch(rnd, unit, 1), "q")
                load_x(Batch(rnd, unit, -1))
                store_x2(Batch(rnd, unit, 4))
                load_residual(Batch(rnd, unit, 3))
                load_shift(Batch(rnd, unit, 2), 1)
                store_parts(Batch(rnd, unit, 0), "k")
                store_parts(Batch(rnd, unit, 0), "q")
                load_stacks(Batch(rnd, unit, 0), "k")

            run(sp, steps)
            for k in range(NBUF):
                sp.wait_ge(x2_stored[k], 16 * len(range(k, B, NBUF)))

        @block.gpsimd
        def _(pool):
            def scale_of(b, taken, steps_done, ready, mom, small, out):
                if not b.real:
                    return
                consts = keep["lnconst"]
                reached(pool, taken, b, T, T)
                nc.gpsimd.tensor_tensor(small[:, 0:T], mom[:, :, 1], consts[:, 0:T], ALU.add).then_inc(steps_done, 1)
                nc.gpsimd.tensor_tensor(small[:, T:2 * T], mom[:, :, 0], consts[:, 2 * T:3 * T], ALU.mult)\
                    .then_inc(steps_done, 1)
                reached(pool, steps_done, b, 3, 2)
                nc.gpsimd.tensor_tensor(out[:, 0:T], small[:, 0:T], consts[:, T:2 * T], ALU.pow).then_inc(steps_done, 1)
                reached(pool, steps_done, b, 3, 3)
                nc.gpsimd.tensor_tensor(out[:, T:2 * T], small[:, T:2 * T], out[:, 0:T], ALU.mult).then_inc(ready, 1)

            def rotate(b, n):
                if not b.real:
                    return
                reached(pool, multiplied[n], b, 3, 3)
                nc.gpsimd.tensor_tensor(rot[n][:], by_cos[n][:], by_sin[n][:], ALU.add).then_inc(rotated[n], 1)

            def cut(b, pair):
                if not b.real:
                    return
                for c in range(T):
                    off = c * WINDOW
                    t = ring_tile(probs, b, pair, c)
                    reached(pool, exp_done, b, 2 * PAIRS, 2 * pair + c + 1)
                    if not b.fixed:
                        carry(pool, pool_carried)
                    n = P - 1 - WINDOW + off
                    nc.gpsimd.affine_select(out=t[:, :, 0:n], in_=t[:, :, 0:n], pattern=[[0, 2], [1, n]],
                                            compare_op=ALU.is_ge, fill=0.0, base=WINDOW - off,
                                            channel_multiplier=-1).then_inc(below_cut, 1)
                for c in range(T):
                    off = c * WINDOW
                    t = ring_tile(probs, b, pair, c)
                    reached(pool, below_cut, b, 2 * PAIRS, 2 * pair + c + 1)
                    if not b.fixed:
                        carry(pool, pool_carried)
                    n = WINDOW + 1 + off
                    nc.gpsimd.affine_select(out=t[:, :, n:SPAN], in_=t[:, :, n:SPAN], pattern=[[0, 2], [-1, SPAN - n]],
                                            compare_op=ALU.is_ge, fill=0.0, base=WINDOW + off - n,
                                            channel_multiplier=1).then_inc(band_cut, 1)

            def steps(rnd, unit):
                for slot in range(SLOTS):
                    if slot == 5:
                        scale_of(Batch(rnd, unit, -1), moments_taken, scale_steps, scale_ready, moments, scale_small, scale)
                    if slot == 2:
                        rotate(Batch(rnd, unit, 0), "k")
                    if slot == 3:
                        rotate(Batch(rnd, unit, 0), "q")
                    if slot == 1:
                        scale_of(Batch(rnd, unit, 4), moments2_taken, scale2_steps, scale2_ready, moments2, scale2_small, scale2)
                    pair, late = pair_at(slot, ST_FIRST)
                    cut(Batch(rnd, unit, late), pair)
                    if slot == 5:
                        low(pool, nc.gpsimd, Batch(rnd, unit, 0), "q")

            run(pool, steps)

        @block.scalar
        def _(act):
            def copy_out(b, done, per, k, src, dst, signal, free=()):
                if not b.real:
                    return
                reached(act, done, b, per, k)
                for f in free:
                    reached(act, *f)
                nc.scalar.activation(dst, src, ACT.Copy).then_inc(signal, 1)

            def normalise(b, src, dst, scale, ready, signal):
                reached(act, ready, b, 1, 1)
                for t in range(T):
                    nc.scalar.activation(dst[:, t, :], src[:, t, :], ACT.Identity, scale=scale[:, t:t + 1],
                                         bias=scale[:, T + t:T + t + 1]).then_inc(signal, 1)

            def high(b, n, bank):
                if not b.real:
                    return
                reached(act, rot_transposed[n], b, 1, 1)
                reached(act, parts_stored[n], b.before(1), 48, 48)
                nc.scalar.activation(parts[n][:, 0, :], bank[:], ACT.Copy).then_inc(high_ready[n], 1)

            def middle(b, n):
                if not b.real:
                    return
                reached(act, rest_ready[n], b, 1, 1)
                nc.scalar.activation(parts[n][:, 1, :], rest[n][:], ACT.Copy).then_inc(mid_ready[n], 1)

            def exps(b, pair):
                if not b.real:
                    return
                for c in range(T):
                    reached(act, scoredT, b, 2 * PAIRS, 2 * pair + c + 1)
                    reached(act, weighted, b, PAIRS, pair - RING // 2 + 1)
                    nc.scalar.activation(ring_tile(probs, b, pair, c)[:].rearrange("p e j -> p (e j)"),
                                         scoreT_bank[c][:, 0:2 * SPAN], ACT.Exp, scale=DK ** -0.5)\
                        .then_inc(exp_done, 1)

            def shift_copy(b, half):
                if not b.real:
                    return
                reached(act, shift_transposed, b, HALVES, half + 1)
                bb = b.before(1)
                if not bb.fixed or bb.n >= 0:
                    act.wait_ge(shift_loaded[half][bb.buf], bb.rnd * 16 * SHIFT + 16 * SHIFT)
                nc.scalar.activation(shiftT[half][:], shift_bank[half][0:SHIFT * 8, 0:S // 2].bitcast(BF16), ACT.Copy)\
                    .then_inc(shiftT_copied, 1)

            def copy_outT(b, half):
                copy_out(b, weighted, PAIRS, PAIRS // 2 * (half + 1), out_bank[half][:],
                         outT[:, 2 * half:2 * half + 2, :].rearrange("p a t -> p (a t)"), outT_copied,
                         [(out_transposed, b.before(1), HALVES, half + 1)])

            def steps(rnd, unit):
                nxt, b0, b1, b2, b3, b4 = (Batch(rnd, unit, k) for k in range(-1, 5))
                for slot in range(SLOTS):
                    if slot == 0:
                        copy_outT(b3, 0)
                        copy_out(b0, c_transposed, 1, 1, bank_a[:], cT[:].rearrange("p c t -> p (c t)"), cT_copied,
                                 [(projected["v"], b0.before(1), 1, 1)])
                    if slot == 1:
                        copy_out(b0, x_transposed, 1, 1, bank_a[:], xT[:].rearrange("p c t -> p (c t)"), xT_copied,
                                 [(projected["q"], b0.before(1), 1, 1)])
                    if slot == 3:
                        high(b0, "k", bank_b)
                    if slot == 4:
                        shift_copy(b2, 1)
                        copy_outT(b3, 1)
                        middle(b0, "k")
                        high(b0, "q", bank_a)
                    if slot == 5:
                        if b0.real:
                            copy_out(b0, projected["v"], 1, 1, bank_b[:].rearrange("p (h d) -> p h d", d=DK),
                                     V[b0.buf][:, :, 0:DK], v_copied, [(weighted, b0.before(NBUF), PAIRS, PAIRS)])
                        middle(b0, "q")
                    if slot == 6:
                        if b4.real:
                            reached(act, x2_transposed, b4, 1, 1)
                            nc.scalar.activation(keep["xnT"][:, :, bass.ds(b4.n * S, S)],
                                                 bank_b[:].rearrange("p (c t) -> p c t", c=C), ACT.Copy)\
                                .then_inc(xn2T_copied, 1)
                    if slot == 7:
                        copy_out(b3, att_transposed, 1, 1, bank_a[:], attT[:].rearrange("p c t -> p (c t)"),
                                 attT_copied, [(att_projected, b3.before(1), 1, 1)])
                        if nxt.real:
                            normalise(nxt, x_in, xn, scale, scale_ready, x_normed)
                    pair, late = pair_at(slot, ST_FIRST)
                    exps(Batch(rnd, unit, late), pair)
                    if slot == 4 and b4.real:
                        reached(act, x2_transposed, b4.before(1), 1, 1)
                        normalise(b4, x2[b4.buf], xn2, scale2, scale2_ready, x2_normed)
                    if slot == 7:
                        shift_copy(b1, 0)

            run(act, steps)

        @block.vector
        def _(dve):
            for k in range(NBUF):
                nc.vector.memset(k_stack[k][STACK:P, :, :], 1.0).then_inc(consts_set, 1)
                nc.vector.memset(V[k][:], 0.0).then_inc(consts_set, 1)
            dve.wait_ge(consts_set, 2 * NBUF)
            for k in range(NBUF):
                nc.vector.memset(V[k][:, :, DK:DK + 1], 1.0).then_inc(consts_set, 1)
            dve.wait_ge(consts_set, 3 * NBUF)

            def statistics(b, src, st, mom, taken, aggregated):
                for t in range(T):
                    nc.vector.bn_stats(st[:, t, :], src[:, t, :]).then_inc(taken, 1)
                for t in range(T):
                    reached(dve, taken, b, T, t + 1)
                    if not b.fixed:
                        carry(dve, dve_carried)
                    nc.vector.bn_aggr(mom[:, t, :], st[:, t, :]).then_inc(aggregated, 1)

            def rope(b, n, bank):
                if not b.real:
                    return
                reached(dve, projected[n], b, 1, 1)
                reached(dve, rot_transposed[n], b.before(1), 1, 1)
                if n == "q":
                    reached(dve, low_ready[n], b.before(1), 1, 1)
                nc.vector.tensor_tensor(by_cos[n][:], bank[:], keep["cos"][:], ALU.mult).then_inc(multiplied[n], 1)
                src = bank[:].rearrange("p (h d) -> p h d", d=DK)
                sin = keep["sin"][:].rearrange("p (h d) -> p h d", d=DK)
                dst = by_sin[n][:].rearrange("p (h d) -> p h d", d=DK)
                nc.vector.tensor_tensor(dst[:, :, 0:HALF], src[:, :, HALF:DK], sin[:, :, 0:HALF], ALU.mult)\
                    .then_inc(multiplied[n], 1)
                nc.vector.tensor_tensor(dst[:, :, HALF:DK], src[:, :, 0:HALF], sin[:, :, HALF:DK], ALU.mult)\
                    .then_inc(multiplied[n], 1)

            def remainder(b, n, bank):
                if not b.real:
                    return
                reached(dve, high_ready[n], b, 1, 1)
                nc.vector.tensor_tensor(rest[n][:], bank[:], parts[n][:, 0, :], ALU.subtract)\
                    .then_inc(rest_ready[n], 1)

            def maxima(b, pair):
                if not b.real:
                    return
                for t in range(T):
                    reached(dve, scored, b, 2 * PAIRS, 2 * pair + t + 1)
                    if not b.fixed:
                        carry(dve, dve_carried)
                    for e in range(2):
                        h = 2 * pair + e
                        mine = score_bank[t][:, e * SPAN:(e + 1) * SPAN]
                        ins = nc.vector.tensor_tensor_reduce(
                            out=mine, in0=mine, in1=keep["band"][:, t, :],
                            scale=1.0, scalar=-3e38, op0=ALU.add, op1=ALU.max, accum_out=smax[b.buf][:, t, h:h + 1])
                    ins.then_inc(max_taken, 1)

            def shift_parts(b, half):
                if not b.real:
                    return
                reached(dve, max_taken, b, 2 * PAIRS, PAIRS * (half + 1))
                reached(dve, shift_transposed, b.before(1), HALVES, half + 1)
                src = smax[b.buf][:, :, half * 8:half * 8 + 8]
                nc.vector.tensor_scalar(shift[:, :, half, 0, :], src, -1.0, None, ALU.mult).then_inc(shift_high, 1)
                reached(dve, shift_high, b, HALVES, half + 1)
                nc.vector.scalar_tensor_tensor(shift[:, :, half, 1, :], src, -1.0, shift[:, :, half, 0, :],
                                               ALU.mult, ALU.subtract).then_inc(shift_ready, 1)

            def divide(b, half):
                if not b.real:
                    return
                reached(dve, out_transposed, b, HALVES, half + 1)
                src = out_bank[half][:].rearrange("p (t s d) -> p t s d", t=T, d=OUT)
                mine = rden[:, :, half * PAIRS:(half + 1) * PAIRS]
                nc.vector.reciprocal(mine, src[:, :, :, DK]).then_inc(rden_ready, 1)
                reached(dve, rden_ready, b, HALVES, half + 1)
                reached(dve, att_transposed, b.before(1), 1, 1)
                heads = PAIRS // HALVES
                for c in range(C):
                    at = c * P + half * heads * DK
                    ins = nc.vector.tensor_tensor(
                        att[:, :, at:at + heads * DK].rearrange("p t (h d) -> p t h d", d=DK), src[:, :, c::2, 0:DK],
                        mine[:, :, c::2].unsqueeze(3).to_broadcast([P, T, heads, DK]), ALU.mult)
                ins.then_inc(out_normed, 1)

            def residual(b):
                if not b.real:
                    return
                loaded(dve, xres_loaded, b)
                reached(dve, att_projected, b, 1, 1)
                nc.vector.scalar_tensor_tensor(x2[b.buf][:].rearrange("p t d -> p (t d)"), bank_b[:],
                                               keep["tanh"][:, 0:1], x2[b.buf][:].rearrange("p t d -> p (t d)"),
                                               ALU.mult, ALU.add).then_inc(x2_ready, 1)
                reached(dve, x2_ready, b, 1, 1)
                statistics(b, x2[b.buf], stats2, moments2, stats2_taken, moments2_taken)

            def steps(rnd, unit):
                nxt, b0, b1, b2, b3, b4 = (Batch(rnd, unit, k) for k in range(-1, 5))
                for slot in range(SLOTS):
                    if slot == 0:
                        residual(b4)
                    if slot == 2:
                        rope(b0, "k", bank_b)
                        divide(b3, 0)
                    if slot == 3:
                        shift_parts(b2, 1)
                        rope(b0, "q", bank_a)
                    if slot == 4:
                        remainder(b0, "k", bank_b)
                    if slot == 5:
                        low(dve, nc.vector, b0, "k")
                        remainder(b0, "q", bank_a)
                    if slot == 7:
                        shift_parts(b1, 0)
                    pair, late = pair_at(slot, S_FIRST)
                    maxima(Batch(rnd, unit, late), pair)
                    if slot == 5:
                        divide(b3, 1)
                    if slot == 4 and nxt.real:
                        reached(dve, x_loaded, nxt, 16, 16)
                        statistics(nxt, x_in, stats, moments, stats_taken, moments_taken)
                    if slot == 7 and b4.real:
                        reached(dve, xn2T_copied, b4, 1, 1)
                        nc.vector.tensor_reduce(keep["xmax"][:, bass.ds(b4.n, 1)], keep["xnT"][:, :, bass.ds(b4.n * S, S)],
                                                XY, ALU.max, apply_absolute_value=True).then_inc(xmax_taken, 1)

            run(dve, steps)
            dve.wait_ge(xmax_taken, B)

        @block.tensor
        def _(pe):
            pe.wait_ge(consts_set, 3 * NBUF)
            ident, identb = keep["ident"], keep["identb"]

            def transpose4(bank, src):
                for t in range(T):
                    for c in range(C):
                        last = nc.tensor.transpose(bank[:, c * S + t * P:c * S + (t + 1) * P],
                                                   src[:, t * D + c * P:t * D + (c + 1) * P], ident[:])
                return last

            def project(bank, srcT, weight, which):
                for t in range(T):
                    out = bank[:, t * D:(t + 1) * D]
                    nc.tensor.matmul(out, keep["ones3"][:], keep["bias"][:, which * D:(which + 1) * D],
                                     start=True, stop=False)
                    for c in range(C):
                        last = nc.tensor.matmul(out, srcT[:, c, t * P:(t + 1) * P], weight[:, c * D:(c + 1) * D],
                                                start=False, stop=(c == C - 1))
                return last

            def scores(b, pair):
                if not b.real:
                    return
                if pair == 0:
                    pe.wait_ge(stack_loaded["k"][b.buf], b.rnd * 48 + 48)
                    pe.wait_ge(stack_loaded["q"][b.buf], b.rnd * 48 + 48)
                for t in range(T):
                    reached(pe, max_taken, b, 2 * PAIRS, 2 * pair + t - 1)
                    bank = score_bank[t]
                    for e in range(2):
                        h = 2 * pair + e
                        last = nc.tensor.matmul(bank[:, e * SPAN:(e + 1) * SPAN],
                                                q_stack[b.buf][0:STACK, h, t * P:(t + 1) * P],
                                                k_stack[b.buf][0:STACK, h, t * FAR:t * FAR + SPAN],
                                                start=True, stop=True)
                    last.then_inc(scored, 1)

            def scoresT(b, pair):
                if not b.real:
                    return
                if pair % 4 == 0:
                    pe.wait_ge(shift_loaded[pair // 4][b.buf], b.rnd * 16 * SHIFT + 16 * SHIFT)
                for c in range(T):
                    reached(pe, exp_done, b, 2 * PAIRS, 2 * pair + c - 1)
                    for e in range(2):
                        h = 2 * pair + e
                        last = nc.tensor.matmul(scoreT_bank[c][:, e * SPAN:(e + 1) * SPAN],
                                                k_stack[b.buf][0:STACK + SHIFT, h, c * P:(c + 1) * P],
                                                q_stack[b.buf][0:STACK + SHIFT, h, c * FAR:c * FAR + SPAN],
                                                start=True, stop=True)
                    last.then_inc(scoredT, 1)

            def weigh(b, pair, later):
                if not b.real:
                    return
                half, col = pair // 4, (pair // 2 % 2) * S
                if pair == 0:
                    reached(pe, v_copied, b, 1, 1)
                if pair % 4 == 0:
                    reached(pe, outT_copied, b, 2, half - 1)
                    if half == 0:
                        reached(pe, shiftT_copied, b, HALVES, 2)
                    elif later.real:
                        reached(pe, shiftT_copied, later, HALVES, 1)
                reached(pe, band_cut, b, 2 * PAIRS, 2 * pair + 2)
                for e in range(2):
                    h = 2 * pair + e
                    row = (h % 4) * OUT
                    for c in range(T):
                        last = nc.tensor.matmul(out_bank[half][row:row + OUT, col + c * FAR:col + c * FAR + SPAN],
                                                V[b.buf][:, c * H + h // 2 + PAIRS * (h % 2), :], ring_tile(probs, b, pair, c)[:, e, :],
                                                start=(c == 0), stop=(c == T - 1), skip_group_check=True)
                last.then_inc(weighted, 1)

            def shift_rows(b, half):
                if not b.real:
                    return
                reached(pe, shift_ready, b, HALVES, half + 1)
                for t in range(T):
                    last = nc.tensor.transpose(shift_bank[half][0:SHIFT * 8, t * P // 2:(t + 1) * P // 2].bitcast(BF16),
                                               shift[:, t, half, :, :].rearrange("p a h -> p (a h)"), identb[:])
                last.then_inc(shift_transposed, 1)

            def out_rows(b, half):
                if not b.real:
                    return
                reached(pe, outT_copied, b, HALVES, half + 1)
                for t in range(T):
                    for quad in range(2):
                        last = nc.tensor.transpose(out_bank[half][:, (2 * t + quad) * P:(2 * t + quad + 1) * P],
                                                   outT[:, 2 * half + quad, t * P:(t + 1) * P], ident[:])
                last.then_inc(out_transposed, 1)

            def steps(rnd, unit):
                b0, b1, b2, b3, b4 = (Batch(rnd, unit, k) for k in range(5))
                for slot in range(SLOTS):
                    if slot == 0 and b0.real:
                        reached(pe, c_loaded, b0, 16, 16)
                        if b4.real:
                            reached(pe, attT_copied, b4, 1, 1)
                        else:
                            reached(pe, rest_ready["q"], b0.before(1), 1, 1)
                        transpose4(bank_a, c_in[:].rearrange("p t d -> p (t d)")).then_inc(c_transposed, 1)
                    if slot == 1 and b0.real:
                        reached(pe, x_normed, b0, T, T)
                        reached(pe, cT_copied, b0, 1, 1)
                        transpose4(bank_a, xn[:].rearrange("p t d -> p (t d)")).then_inc(x_transposed, 1)
                    if slot == 2 and b0.real:
                        reached(pe, xT_copied, b0, 1, 1)
                        project(bank_a, xT, keep["WqT"], 0).then_inc(projected["q"], 1)
                    if slot == 6 and b4.real:
                        if b0.real:
                            reached(pe, v_copied, b0, 1, 1)
                        reached(pe, x2_normed, b4, T, T)
                        transpose4(bank_b, xn2[:].rearrange("p t d -> p (t d)")).then_inc(x2_transposed, 1)
                    if slot == 5 and b0.real:
                        reached(pe, rest_ready["k"], b0, 1, 1)
                        project(bank_b, cT, keep["WvT"], 2).then_inc(projected["v"], 1)
                    if slot == 5:
                        out_rows(b3, 1)
                    if slot == 7 and b3.real:
                        reached(pe, out_normed, b3, HALVES, 2)
                        if b0.real:
                            reached(pe, rest_ready["q"], b0, 1, 1)
                        elif b4.real:
                            reached(pe, attT_copied, b4, 1, 1)
                        transpose4(bank_a, att[:].rearrange("p t d -> p (t d)")).then_inc(att_transposed, 1)

                    pair, late = pair_at(slot, S_FIRST)
                    scores(Batch(rnd, unit, late), pair)

                    if slot == 1 and b0.real:
                        reached(pe, cT_copied, b0, 1, 1)
                        if b4.real:
                            reached(pe, x2_ready, b4, 1, 1)
                        else:
                            reached(pe, v_copied, b0.before(1), 1, 1)
                        project(bank_b, cT, keep["WkT"], 1).then_inc(projected["k"], 1)
                    if slot == 1:
                        out_rows(b3, 0)
                    if slot == 3:
                        if b0.real:
                            reached(pe, rotated["k"], b0, 1, 1)
                            transpose4(bank_b, rot["k"]).then_inc(rot_transposed["k"], 1)
                        if b3.real:
                            reached(pe, out_normed, b3, HALVES, 1)
                        shift_rows(b2, 1)
                    if slot == 4 and b0.real:
                        reached(pe, rotated["q"], b0, 1, 1)
                        transpose4(bank_a, rot["q"]).then_inc(rot_transposed["q"], 1)
                    if slot == 7:
                        if b3.real:
                            if b4.real:
                                reached(pe, xn2T_copied, b4, 1, 1)
                            elif b0.real:
                                reached(pe, v_copied, b0, 1, 1)
                            reached(pe, attT_copied, b3, 1, 1)
                            project(bank_b, attT, keep["WoT"], 3).then_inc(att_projected, 1)
                        shift_rows(b1, 0)

                    pair, late = pair_at(slot, ST_FIRST)
                    scoresT(Batch(rnd, unit, late), pair)
                    pair, late = pair_at(slot, PV_FIRST)
                    weigh(Batch(rnd, unit, late), pair, b2)

            run(pe, steps)


def feed_forward(nc, scratch, out, banks, keep, rows):
    TILES = B * S // TILE
    F = I // P
    HF = F // 2
    UW = HF * TILE
    UNITS = 2 * TILES
    with ExitStack() as ctx:
        def sb(name, shape, dt=F32):
            return ctx.enter_context(nc.sbuf_tensor(name, shape, dt))

        def sem(name):
            return ctx.enter_context(nc.semaphore(name))

        def bufs(name, shape, dt=F32):
            return [sb(f"{name}{k}", shape, dt) for k in range(2)]

        scales = keep["scales"]
        (X_MAX, X_S, X_INV, G_W, U_W, O_W, G_MAX, G_S, G_INV, U_MAX, U_S, U_INV, H_MAX, H_S, H_INV, O_MAX, O_S, O_INV, UNIT_O) = range(19)
        col = lambda k: scales[:, k:k + 1]
        peak = keep["peak"]
        gmx, gmn, umx, hmx, omx = (keep["maxima"][:, k, :] for k in range(5))
        xnT = keep["xnT"]
        x_parts = xnT[:].rearrange("p c t -> p (c t)").bitcast(F16).rearrange("p (c t) -> p c t", c=C)

        def x_part(j, part):
            return x_parts[:, :, bass.ds(j * (2 * TILE) + part * TILE, TILE)]

        def inner_products(pe, bank, weights, j, f):
            for c in range(C):
                for k, (xp, wp) in enumerate(PRODUCTS):
                    last = nc.tensor.matmul(bank[:], weights[wp][:, c * I + f * P:c * I + (f + 1) * P],
                                            x_parts[:, c, bass.ds(j * (2 * TILE) + xp * TILE, TILE)],
                                            start=(c == 0 and k == 0), stop=(c == C - 1 and k == len(PRODUCTS) - 1))
            return last

        carried = sem("carried")
        small = sem("small")
        reduced = sem("reduced")
        asked = sem("asked")

        def scale_chain(dve, first, src, parts, maxi, s, inv, done_small, n_red):
            nc.vector.tensor_reduce(peak[:, 0:1], src, X, ALU.max).then_inc(asked, 1)
            dve.wait_ge(reduced, n_red)
            nc.vector.tensor_scalar(col(s), col(maxi), 1.0 / AQMAX, EPS_Q, ALU.mult, ALU.max).then_inc(small, 1)
            dve.wait_ge(small, done_small + 1)
            nc.vector.reciprocal(col(inv), col(s)).then_inc(small, 1)
            dve.wait_ge(small, done_small + 2)

        with ExitStack() as c1:
            def sb1(name, shape, dt=F32):
                return c1.enter_context(nc.sbuf_tensor(name, shape, dt))

            def sem1(name):
                return c1.enter_context(nc.semaphore(name))

            g_stage = [sb1(f"g_stage{k}", [P, UW]) for k in range(2)]
            xint = sb1("xint", [P, C, TILE], I16)
            x_rounded, x_quantised = sem1("x_rounded"), sem1("x_quantised")
            gate_made, gate_copied, gate_seen = sem1("gate_made"), sem1("gate_copied"), sem1("gate_seen")
            gate_stored = [sem1(f"gate_stored{k}") for k in range(2)]
            product_scales, x_high = sem1("product_scales"), sem1("x_high")
            block = c1.enter_context(nc.Block())

            @block.sync
            def _(sp):
                with sp.Fori(0, TILES) as j:
                    for h in range(2):
                        sp.wait_ge(gate_copied, j * F + HF * (h + 1))
                        sp.dma_start(scratch["gate"][j][:, h * UW:(h + 1) * UW], g_stage[h][:])\
                            .then_inc(gate_stored[h], 16)
                for h in range(2):
                    sp.wait_ge(gate_stored[h], 16 * TILES)

            @block.gpsimd
            def _(pool):
                pool.wait_ge(asked, 1)
                nc.gpsimd.partition_all_reduce(col(X_MAX), peak[:, 0:1], P, RMAX).then_inc(reduced, 1)

            @block.vector
            def _(dve):
                scale_chain(dve, True, keep["xmax"][:], B, X_MAX, X_S, X_INV, 0, 1)
                for k, dst in enumerate((G_W, U_W)):
                    nc.vector.tensor_tensor(col(dst), col(X_S), keep["unscale"][:, k:k + 1], ALU.mult)\
                        .then_inc(product_scales, 1)
                dve.wait_ge(product_scales, 2)

                def quantise(j):
                    cols = xnT[:, :, bass.ds(j * TILE, TILE)]
                    nc.vector.tensor_scalar(xint[:], cols, col(X_INV), None, ALU.mult).then_inc(x_rounded, 1)
                    dve.wait_ge(x_rounded, j + 1)
                    nc.vector.tensor_copy(x_part(j, 0), xint[:]).then_inc(x_high, 1)
                    dve.wait_ge(x_high, j + 1)
                    nc.vector.tensor_tensor(x_part(j, 1), xint[:], x_part(j, 0), ALU.subtract).then_inc(x_quantised, 1)
                    dve.wait_ge(x_quantised, j + 1)

                def extremes(j):
                    for h in range(2):
                        dve.wait_ge(gate_copied, j * F + HF * (h + 1))
                        nc.vector.tensor_reduce(gmx[:, bass.ds(j * 2 + h, 1)], g_stage[h][:], X, ALU.max)
                        nc.vector.tensor_reduce(gmn[:, bass.ds(j * 2 + h, 1)], g_stage[h][:], X, ALU.min)\
                            .then_inc(gate_seen, 1)

                quantise(0)
                with dve.Fori(0, TILES - 1) as j:
                    quantise(j + 1)
                    extremes(j)
                extremes(TILES - 1)
                dve.wait_ge(gate_seen, UNITS)

            @block.scalar
            def _(act):
                act.wait_ge(product_scales, 2)

                def copies(j, first):
                    for f in range(F):
                        h = f // HF
                        act.wait_ge(gate_made, j * F + f + 1)
                        if f % HF == 0 and not first:
                            act.wait_ge(gate_seen, j * 2 + h - 1)
                            act.wait_ge(gate_stored[h], j * 16)
                        nc.scalar.activation(g_stage[h][:, (f % HF) * TILE:(f % HF + 1) * TILE], banks[f][:], ACT.Copy,
                                             scale=col(G_W)).then_inc(gate_copied, 1)
                copies(0, True)
                with act.Fori(1, TILES) as j:
                    copies(j, False)

            @block.tensor
            def _(pe):
                def products(j, first):
                    pe.wait_ge(x_quantised, j + 1)
                    for f in range(F):
                        if not first:
                            pe.wait_ge(gate_copied, j * F - F + f + 1)
                        inner_products(pe, banks[f], keep["w_gateT"], j, f).then_inc(gate_made, 1)
                products(0, True)
                with pe.Fori(1, TILES) as j:
                    products(j, False)

        with ExitStack() as c2:
            def sb2(name, shape, dt=F32):
                return c2.enter_context(nc.sbuf_tensor(name, shape, dt))

            def sem2(name):
                return c2.enter_context(nc.semaphore(name))

            u_stage = [sb2(f"u_stage{k}", [P, UW]) for k in range(2)]
            g_in = [sb2(f"g_in{k}", [P, UW]) for k in range(2)]
            g_int = [sb2(f"g_int{k}", [P, UW], I16) for k in range(2)]
            sig = [sb2(f"sig{k}", [P, UW]) for k in range(2)]
            sig_int = [sb2(f"sig_int{k}", [P, UW], U16) for k in range(2)]
            silu = [sb2(f"silu{k}", [P, UW]) for k in range(2)]
            unit_max, max_kept = sb2("unit_max_h", [P, 2]), sem2("h_max_kept")
            probe = sb2("probe", [P, 4])
            probe_int = sb2("probe_int", [P, 1], I16)
            probe_sig = sb2("probe_sig", [P, 1], U16)
            up_made, up_copied, up_seen = sem2("up_made"), sem2("up_copied"), sem2("up_seen")
            up_stored = [sem2(f"up_stored{k}") for k in range(2)]
            gate_loaded = [sem2(f"gate_loaded{k}") for k in range(2)]
            silu_stored = [sem2(f"silu_stored{k}") for k in range(2)]
            gate_rounded, sig_done = sem2("gate_rounded"), sem2("sig_done")
            sig_rounded, silu_done = sem2("sig_rounded"), sem2("silu_done")
            scale_ready, probe_step, probe_act = sem2("scale_ready"), sem2("probe_step"), sem2("probe_act")
            block = c2.enter_context(nc.Block())

            @block.sync
            def _(sp):
                def load(j, h):
                    sp.dma_start(g_in[h][:], scratch["gate"][j][:, h * UW:(h + 1) * UW]).then_inc(gate_loaded[h], 16)

                def store(j, h):
                    sp.wait_ge(up_copied, j * F + HF * (h + 1))
                    sp.dma_start(scratch["up"][j][:, h * UW:(h + 1) * UW], u_stage[h][:]).then_inc(up_stored[h], 16)
                    sp.wait_ge(silu_done, j * 2 + h + 1)
                    sp.dma_start(scratch["silu"][j][:, h * UW:(h + 1) * UW], silu[h][:]).then_inc(silu_stored[h], 16)

                for h in range(2):
                    load(0, h)
                with sp.Fori(1, TILES) as j:
                    for h in range(2):
                        sp.wait_ge(gate_rounded, j * 2 + h - 1)
                        load(j, h)
                        store(j - 1, h)
                for h in range(2):
                    store(TILES - 1, h)
                for h in range(2):
                    sp.wait_ge(up_stored[h], 16 * TILES)
                    sp.wait_ge(silu_stored[h], 16 * TILES)

            @block.gpsimd
            def _(pool):
                pool.wait_ge(asked, 3)
                nc.gpsimd.partition_all_reduce(col(G_MAX), peak[:, 0:1], P, RMAX).then_inc(reduced, 1)
                nc.gpsimd.partition_all_reduce(probe[:, 0:1], peak[:, 1:2], P, RMAX).then_inc(reduced, 1)

            @block.vector
            def _(dve):
                nc.vector.tensor_reduce(peak[:, 1:2], gmx, X, ALU.max).then_inc(asked, 1)
                nc.vector.tensor_reduce(peak[:, 2:3], gmn, X, ALU.min).then_inc(small, 1)
                dve.wait_ge(asked, 2)
                dve.wait_ge(small, 3)
                nc.vector.scalar_tensor_tensor(peak[:, 0:1], peak[:, 2:3], -1.0, peak[:, 1:2], ALU.mult, ALU.max)\
                    .then_inc(asked, 1)
                dve.wait_ge(reduced, 3)
                nc.vector.tensor_scalar(col(G_S), col(G_MAX), 1.0 / AQMAX, EPS_Q, ALU.mult, ALU.max).then_inc(small, 1)
                dve.wait_ge(small, 4)
                nc.vector.reciprocal(col(G_INV), col(G_S)).then_inc(small, 1)
                nc.vector.tensor_scalar(col(UNIT_O), col(G_S), -1.0 / 65536.0, None, ALU.mult).then_inc(small, 1)
                dve.wait_ge(small, 6)
                nc.vector.tensor_scalar(probe_int[:], probe[:, 0:1], col(G_INV), None, ALU.mult).then_inc(scale_ready, 1)
                dve.wait_ge(probe_act, 1)
                nc.vector.tensor_scalar(probe_sig[:], probe[:, 1:2], 65536.0, 65535.0, ALU.mult, ALU.min)\
                    .then_inc(probe_step, 1)
                dve.wait_ge(probe_step, 1)
                nc.vector.tensor_scalar(probe[:, 2:3], probe_sig[:], col(UNIT_O), -1.0, ALU.mult, ALU.mult)\
                    .then_inc(probe_step, 1)
                dve.wait_ge(probe_step, 2)
                nc.vector.tensor_tensor(peak[:, 3:4], probe[:, 2:3], probe_int[:], ALU.mult).then_inc(probe_step, 1)

                def unit(j, h, first):
                    dve.wait_ge(sig_done, j * 2 + h + 1)
                    nc.vector.tensor_scalar(sig_int[h][:], sig[h][:], 65536.0, 65535.0, ALU.mult, ALU.min)\
                        .then_inc(sig_rounded, 1)
                    dve.wait_ge(up_copied, j * F + HF * (h + 1))
                    nc.vector.tensor_reduce(umx[:, bass.ds(j * 2 + h, 1)], u_stage[h][:], X, ALU.max,
                                            apply_absolute_value=True).then_inc(up_seen, 1)
                    dve.wait_ge(sig_rounded, j * 2 + h + 1)
                    if not first:
                        dve.wait_ge(silu_stored[h], j * 16)
                    carry(dve, carried)
                    nc.vector.tensor_tensor_reduce(out=silu[h][:], in0=g_int[h][:], in1=sig_int[h][:],
                                                   scale=col(UNIT_O), scalar=0.0, op0=ALU.mult, op1=ALU.max,
                                                   accum_out=unit_max[:, h:h + 1]).then_inc(silu_done, 1)
                    dve.wait_ge(silu_done, j * 2 + h + 1)
                    nc.vector.tensor_copy(hmx[:, bass.ds(j * 2 + h, 1)], unit_max[:, h:h + 1]).then_inc(max_kept, 1)

                for h in range(2):
                    unit(0, h, True)
                with dve.Fori(1, TILES) as j:
                    for h in range(2):
                        unit(j, h, False)
                dve.wait_ge(silu_done, UNITS)
                dve.wait_ge(max_kept, UNITS)
                dve.wait_ge(up_seen, UNITS)
                dve.wait_ge(probe_step, 3)

            @block.scalar
            def _(act):
                act.wait_ge(scale_ready, 1)
                nc.scalar.activation(probe[:, 1:2], probe_int[:], ACT.Sigmoid, scale=col(G_S)).then_inc(probe_act, 1)

                def unit(j, h, first):
                    for k in range(HF):
                        f = h * HF + k
                        act.wait_ge(up_made, j * F + f + 1)
                        if k == 0 and not first:
                            act.wait_ge(up_seen, j * 2 + h - 1)
                            act.wait_ge(up_stored[h], j * 16)
                        nc.scalar.activation(u_stage[h][:, k * TILE:(k + 1) * TILE], banks[f][:], ACT.Copy,
                                             scale=col(U_W)).then_inc(up_copied, 1)
                    act.wait_ge(gate_loaded[h], j * 16 + 16)
                    if not first:
                        act.wait_ge(silu_done, j * 2 + h - 1)
                    nc.scalar.activation(g_int[h][:], g_in[h][:], ACT.Copy, scale=col(G_INV)).then_inc(gate_rounded, 1)
                    act.wait_ge(gate_rounded, j * 2 + h + 1)
                    if not first:
                        act.wait_ge(sig_rounded, j * 2 + h - 1)
                    nc.scalar.activation(sig[h][:], g_int[h][:], ACT.Sigmoid, scale=col(G_S)).then_inc(sig_done, 1)

                for h in range(2):
                    unit(0, h, True)
                with act.Fori(1, TILES) as j:
                    for h in range(2):
                        unit(j, h, False)

            @block.tensor
            def _(pe):
                def products(j, first):
                    for f in range(F):
                        if not first:
                            pe.wait_ge(up_copied, j * F - F + f + 1)
                        inner_products(pe, banks[f], keep["w_upT"], j, f).then_inc(up_made, 1)
                products(0, True)
                with pe.Fori(1, TILES) as j:
                    products(j, False)

        rows.close()
        silu_int = sb("silu_int", [P, TILES * 2 * UW], I16)

        with ExitStack() as c3:
            def sb3(name, shape, dt=F32):
                return c3.enter_context(nc.sbuf_tensor(name, shape, dt))

            def sem3(name):
                return c3.enter_context(nc.semaphore(name))

            N = 2
            h_in = [sb3(f"h_in{k}", [P, UW]) for k in range(N)]
            u_in = [sb3(f"u_in{k}", [P, UW]) for k in range(N)]
            h_abs = [sb3(f"h_abs{k}", [P, UW], I16) for k in range(N)]
            u_abs = [sb3(f"u_abs{k}", [P, UW], I16) for k in range(N)]
            unit_max, max_kept = sb3("unit_max_o", [P, 2]), sem3("o_max_kept")
            prod = sb3("prod", [P, UW])
            h_loaded, u_loaded = [sem3(f"h_loaded{k}") for k in range(N)], [sem3(f"u_loaded{k}") for k in range(N)]
            silu_rounded, silu_sized, up_sized, prod_seen = (sem3("silu_rounded"), sem3("silu_sized"),
                                                             sem3("up_sized"), sem3("prod_seen"))
            scales_known = sem3("scales_known")
            block = c3.enter_context(nc.Block())

            @block.sync
            def _(sp):
                def load(j, h):
                    sp.dma_start(h_in[h][:], scratch["silu"][j][:, h * UW:(h + 1) * UW]).then_inc(h_loaded[h], 16)
                    sp.dma_start(u_in[h][:], scratch["up"][j][:, h * UW:(h + 1) * UW]).then_inc(u_loaded[h], 16)
                for h in range(N):
                    load(0, h)
                with sp.Fori(1, TILES) as j:
                    for h in range(N):
                        sp.wait_ge(silu_rounded, j * 2 + h - 1)
                        sp.wait_ge(silu_sized, j * 2 + h - 1)
                        sp.wait_ge(up_sized, j * 2 + h - 1)
                        load(j, h)

            @block.gpsimd
            def _(pool):
                pool.wait_ge(asked, 4)
                nc.gpsimd.partition_all_reduce(col(U_MAX), peak[:, 0:1], P, RMAX).then_inc(reduced, 1)
                pool.wait_ge(asked, 6)
                nc.gpsimd.partition_all_reduce(col(H_MAX), peak[:, 1:2], P, RMAX).then_inc(reduced, 1)

            @block.vector
            def _(dve):
                nc.vector.tensor_reduce(peak[:, 0:1], umx, X, ALU.max).then_inc(asked, 1)
                nc.vector.tensor_reduce(peak[:, 2:3], hmx, X, ALU.max).then_inc(asked, 1)
                dve.wait_ge(asked, 5)
                nc.vector.tensor_tensor(peak[:, 1:2], peak[:, 2:3], peak[:, 3:4], ALU.max).then_inc(asked, 1)
                dve.wait_ge(reduced, 4)
                nc.vector.tensor_scalar(col(U_S), col(U_MAX), 1.0 / AQMAX, EPS_Q, ALU.mult, ALU.max).then_inc(small, 1)
                dve.wait_ge(reduced, 5)
                nc.vector.tensor_scalar(col(H_S), col(H_MAX), 1.0 / AQMAX, EPS_Q, ALU.mult, ALU.max).then_inc(small, 1)
                dve.wait_ge(small, 8)
                nc.vector.reciprocal(col(U_INV), col(U_S)).then_inc(scales_known, 1)
                nc.vector.reciprocal(col(H_INV), col(H_S)).then_inc(scales_known, 1)
                dve.wait_ge(scales_known, 2)

                def unit(j, h):
                    dve.wait_ge(h_loaded[h], j * 16 + 16)
                    mine = silu_int[:, bass.ds(j * (2 * UW) + h * UW, UW)]
                    nc.vector.tensor_scalar(mine, h_in[h][:], col(H_INV), None, ALU.mult).then_inc(silu_rounded, 1)
                    dve.wait_ge(silu_sized, j * 2 + h + 1)
                    dve.wait_ge(up_sized, j * 2 + h + 1)
                    carry(dve, carried)
                    nc.vector.tensor_tensor_reduce(out=prod[:], in0=h_abs[h][:], in1=u_abs[h][:], scale=1.0,
                                                   scalar=0.0, op0=ALU.mult, op1=ALU.max,
                                                   accum_out=unit_max[:, h:h + 1]).then_inc(prod_seen, 1)
                    dve.wait_ge(prod_seen, j * 2 + h + 1)
                    nc.vector.tensor_copy(omx[:, bass.ds(j * 2 + h, 1)], unit_max[:, h:h + 1]).then_inc(max_kept, 1)

                with dve.Fori(0, TILES) as j:
                    for h in range(N):
                        unit(j, h)
                dve.wait_ge(max_kept, UNITS)

            @block.scalar
            def _(act):
                act.wait_ge(scales_known, 2)

                def unit(j, h, first):
                    act.wait_ge(u_loaded[h], j * 16 + 16)
                    if not first:
                        act.wait_ge(prod_seen, j * 2 + h - 1)
                    nc.scalar.activation(u_abs[h][:], u_in[h][:], ACT.Abs, scale=col(U_INV)).then_inc(up_sized, 1)
                    act.wait_ge(h_loaded[h], j * 16 + 16)
                    nc.scalar.activation(h_abs[h][:], h_in[h][:], ACT.Abs, scale=col(H_INV)).then_inc(silu_sized, 1)
                for h in range(N):
                    unit(0, h, True)
                with act.Fori(1, TILES) as j:
                    for h in range(N):
                        unit(j, h, False)

        with ExitStack() as c4:
            def sb4(name, shape, dt=F32):
                return c4.enter_context(nc.sbuf_tensor(name, shape, dt))

            def sem4(name):
                return c4.enter_context(nc.semaphore(name))

            u_in = [sb4(f"up_in{k}", [P, UW]) for k in range(2)]
            u_int = [sb4(f"u_int{k}", [P, UW], I16) for k in range(2)]
            o_int = [sb4(f"o_int{k}", [P, UW], I16) for k in range(2)]
            o = [[[sb4(f"o{k}_{h}_{part}", [P, UW], F16) for part in range(2)] for h in range(2)] for k in range(2)]
            SUB = TILE // P
            x2_in = [sb4(f"x2_in{k}", [P, SUB, D]) for k in range(2)]
            y = [sb4(f"y{k}", [P, SUB, D]) for k in range(2)]
            up_loaded = [sem4(f"up_loaded{k}") for k in range(2)]
            x2_loaded = [sem4(f"x2_loaded{k}") for k in range(2)]
            y_stored = [sem4(f"y_stored{k}") for k in range(2)]
            o_high, o_ready = sem4("o_high"), sem4("o_ready")
            up_rounded, o_rounded, y_made, y_ready = (sem4("up_rounded"), sem4("o_rounded"),
                                                               sem4("y_made"), sem4("y_ready"))
            o_scale, o_step = sem4("o_scale"), sem4("o_step")
            x2_rows = scratch["x2"].rearrange("b p t d -> p b t d")
            out_rows = out.rearrange("b (t p) d -> p b t d", p=P)
            BT = TILE // S
            block = c4.enter_context(nc.Block())

            @block.sync
            def _(sp):
                def load(j, h):
                    sp.dma_start(u_in[h][:], scratch["up"][j][:, h * UW:(h + 1) * UW]).then_inc(up_loaded[h], 16)

                def load_x2(j, odd):
                    sp.dma_start(x2_in[odd][:].rearrange("p (b t) d -> p b t d", b=BT), x2_rows[:, bass.ds(j * BT, BT)])\
                        .then_inc(x2_loaded[odd], 16)

                def store(j, odd):
                    sp.wait_ge(y_ready, j * SUB + SUB)
                    for k in range(BT):
                        sp.dma_start(out_rows[:, j * BT + k], y[odd][:, k * T:(k + 1) * T, :]).then_inc(y_stored[odd], 16)

                for j in range(2):
                    for h in range(2):
                        if j:
                            sp.wait_ge(up_rounded, j * 2 + h - 1)
                        load(j, h)
                    load_x2(j, j)
                with sp.Fori(1, TILES // 2) as pair:
                    for odd in range(2):
                        j = pair * 2 + odd
                        for h in range(2):
                            sp.wait_ge(up_rounded, j * 2 + h - 1)
                            load(j, h)
                        store(j - 2, odd)
                        load_x2(j, odd)
                for odd in range(2):
                    store(TILES - 2 + odd, odd)
                for odd in range(2):
                    sp.wait_ge(y_stored[odd], 16 * BT * (TILES // 2))

            @block.gpsimd
            def _(pool):
                pool.wait_ge(asked, 7)
                nc.gpsimd.partition_all_reduce(col(O_MAX), peak[:, 4:5], P, RMAX).then_inc(reduced, 1)

            @block.vector
            def _(dve):
                nc.vector.tensor_reduce(peak[:, 4:5], omx, X, ALU.max).then_inc(asked, 1)
                nc.vector.tensor_tensor(col(UNIT_O), col(H_S), col(U_S), ALU.mult).then_inc(o_step, 1)
                dve.wait_ge(reduced, 6)
                dve.wait_ge(o_step, 1)
                nc.vector.tensor_tensor(peak[:, 5:6], col(O_MAX), col(UNIT_O), ALU.mult).then_inc(o_step, 1)
                dve.wait_ge(o_step, 2)
                nc.vector.tensor_scalar(col(O_S), peak[:, 5:6], 1.0 / AQMAX, EPS_Q, ALU.mult, ALU.max).then_inc(o_step, 1)
                dve.wait_ge(o_step, 3)
                nc.vector.reciprocal(peak[:, 6:7], col(O_S)).then_inc(o_step, 1)
                nc.vector.tensor_tensor(peak[:, 7:8], col(O_S), keep["unscale"][:, 2:3], ALU.mult).then_inc(o_step, 1)
                dve.wait_ge(o_step, 5)
                nc.vector.tensor_tensor(col(O_W), peak[:, 7:8], keep["tanh"][:, 1:2], ALU.mult).then_inc(o_step, 1)
                dve.wait_ge(o_step, 6)
                nc.vector.scalar_tensor_tensor(col(O_INV), peak[:, 6:7], -1.0, col(UNIT_O), ALU.mult, ALU.mult)\
                    .then_inc(o_scale, 1)
                dve.wait_ge(o_scale, 1)

                def round_product(j, h, first):
                    dve.wait_ge(up_rounded, j * 2 + h + 1)
                    if not first:
                        dve.wait_ge(o_ready, j * 2 + h - 1)
                    nc.vector.scalar_tensor_tensor(o_int[h][:], silu_int[:, bass.ds(j * (2 * UW) + h * UW, UW)],
                                                   col(O_INV), u_int[h][:], ALU.mult, ALU.mult).then_inc(o_rounded, 1)

                def residual(pair, odd, first):
                    j = pair * 2 + odd
                    dve.wait_ge(x2_loaded[odd], pair * 16 + 16)
                    if not first:
                        dve.wait_ge(y_stored[odd], pair * 16 * BT)
                    for s in range(SUB):
                        dve.wait_ge(y_made, j * SUB + s + 1)
                        nc.vector.scalar_tensor_tensor(y[odd][:, s, :], banks[s + odd * SUB][:, 0:D],
                                                       col(O_W), x2_in[odd][:, s, :], ALU.mult, ALU.add)\
                            .then_inc(y_ready, 1)

                def round_tile(j, odd, first=False):
                    for h in range(2):
                        round_product(j, h, first)
                    for h in range(2):
                        dve.wait_ge(o_high, j * 2 + h + 1)
                        nc.vector.tensor_tensor(o[odd][h][1][:], o_int[h][:], o[odd][h][0][:], ALU.subtract)\
                            .then_inc(o_ready, 1)

                round_tile(0, 0, first=True)
                for odd in range(2):
                    round_tile(odd + 1, 1 - odd)
                    residual(0, odd, True)
                with dve.Fori(1, TILES // 2 - 1) as pair:
                    for odd in range(2):
                        round_tile(pair * 2 + odd + 1, 1 - odd)
                        residual(pair, odd, False)
                round_tile(TILES - 1, 1)
                for odd in range(2):
                    residual(TILES // 2 - 1, odd, False)

            @block.scalar
            def _(act):
                act.wait_ge(o_scale, 1)

                def unit(j, h, first):
                    act.wait_ge(up_loaded[h], j * 16 + 16)
                    if not first:
                        act.wait_ge(o_rounded, j * 2 + h - 1)
                    nc.scalar.activation(u_int[h][:], u_in[h][:], ACT.Copy, scale=col(U_INV)).then_inc(up_rounded, 1)

                def high_part(j, odd, h, first):
                    act.wait_ge(o_rounded, j * 2 + h + 1)
                    if not first:
                        act.wait_ge(y_made, (j - 1) * SUB)
                    nc.scalar.activation(o[odd][h][0][:], o_int[h][:], ACT.Copy).then_inc(o_high, 1)

                def tile_steps(j, odd, first):
                    for h in range(2):
                        unit(j, h, first and not odd)
                    for h in range(2):
                        high_part(j, odd, h, first)

                tile_steps(0, 0, True)
                tile_steps(1, 1, True)
                with act.Fori(1, TILES // 2) as pair:
                    for odd in range(2):
                        tile_steps(pair * 2 + odd, odd, False)

            @block.tensor
            def _(pe):
                def rows(j, odd, first):
                    for s in range(SUB):
                        bank = banks[(s + odd * SUB)]
                        if not first:
                            pe.wait_ge(y_ready, (j - 2) * SUB + s + 1)
                        for f in range(F):
                            if s == 0 and f % HF == 0:
                                pe.wait_ge(o_ready, j * 2 + f // HF + 1)
                            at = (f % HF) * TILE + s * P
                            for k, (op, wp) in enumerate(PRODUCTS):
                                last = nc.tensor.matmul(bank[:, 0:D], o[odd][f // HF][op][:, at:at + P],
                                                        keep["w_downT"][wp][:, f * D:(f + 1) * D],
                                                        start=(f == 0 and k == 0),
                                                        stop=(f == F - 1 and k == len(PRODUCTS) - 1))
                        last.then_inc(y_made, 1)
                for odd in range(2):
                    rows(odd, odd, True)
                with pe.Fori(1, TILES // 2) as pair:
                    for odd in range(2):
                        rows(pair * 2 + odd, odd, False)


def build(nc, dram, x, ctx_in, w, out):
    tile_of = nc.dram_tensor("gate_scratch", (B * S // TILE, P, I // P * TILE), F32, kind="Internal").ap()
    up = nc.dram_tensor("up_scratch", (B * S // TILE, P, I // P * TILE), F32, kind="Internal").ap()
    silu = nc.dram_tensor("silu_scratch", (B * S // TILE, P, I // P * TILE), F32, kind="Internal").ap()
    x2 = nc.dram_tensor("x2_scratch", (B, P, T, D), F32, kind="Internal").ap()
    scratch = {"gate": tile_of, "up": up, "silu": silu, "x2": x2}
    for n in "qk":
        parts = nc.dram_tensor(f"{n}_parts_scratch", (NBUF, 3, DK, H * S), BF16, kind="Internal").ap()
        scratch[n] = parts

        def rows_of(buf, g, n=n, parts=parts):
            if n == "q":
                return parts[buf][g].unsqueeze(0).to_broadcast([3 - g, DK, H * S])
            return parts[buf][0:3 - g]

        scratch[n + "_rows"] = rows_of

    with ExitStack() as ctx:
        def sb(name, shape, dt=F32):
            return ctx.enter_context(nc.sbuf_tensor(name, shape, dt))

        banks = [ctx.enter_context(nc.psum_tensor(f"bank{k}", [P, 512], F32)) for k in range(8)]
        keep = {
            "ident": sb("ident", [P, P]), "identb": sb("identb", [P, P], BF16),
            "cos": sb("cos", [P, T * D]), "sin": sb("sin", [P, T * D]), "band": sb("band", [P, T, SPAN], BF16),
            "ones3": sb("ones3", [3, P], BF16), "bias": sb("bias", [3, 4 * D], BF16),
            "lnconst": sb("lnconst", [P, 3 * T]), "tanh": sb("tanh", [P, 2]),
            "unscale": sb("unscale", [P, 3]),
            "xmax": sb("xmax", [P, B]), "scales": sb("scales", [P, 19]), "peak": sb("peak", [P, 8]),
            "maxima": sb("maxima", [P, 5, 2 * B * S // TILE]),
        }
        for n in ("Wq", "Wk", "Wv", "Wo"):
            keep[n + "T"] = sb(n + "T", [P, C * D])
        for n in ("w_gate", "w_up", "w_down"):
            keep[n + "T"] = [sb(f"{n}T{k}", [P, I * D // P], F16) for k in range(2)]
        rows = ctx.enter_context(ExitStack())
        keep["xnT"] = rows.enter_context(nc.sbuf_tensor("xnT", [P, C, B * S], F32))
        prepare(nc, dram, w, banks, keep)
        attention(nc, dram, x, ctx_in, scratch, banks, keep)
        feed_forward(nc, scratch, out, banks, keep, rows)


def tables():
    inv = np.float32(1.0) / np.float32(10000.0) ** (np.arange(0, DK, 2, dtype=np.float32) / np.float32(DK))
    angle = np.arange(S, dtype=np.float32)[:, None] * inv[None, :].astype(np.float32)
    cos, sin = np.cos(angle).astype(np.float32), np.sin(angle).astype(np.float32)
    cos = np.tile(np.concatenate([cos, cos], 1), (1, H))
    sin = np.tile(np.concatenate([-sin, sin], 1), (1, H))
    lay = lambda a: np.ascontiguousarray(a.reshape(T, P, D).transpose(1, 0, 2).reshape(P, T * D))
    band = np.zeros((P, T, SPAN), np.float32)
    for t in range(T):
        query = t * P + np.arange(P)[:, None]
        key = t * FAR + np.arange(SPAN)[None, :]
        band[:, t] = np.where(np.abs(query - key) <= WINDOW, 0.0, -1e9)
    return {"cos": lay(cos), "sin": lay(sin), "band": band, "ident": np.eye(P, dtype=np.float32)}


_INS = ["x", "ctx_1024", "g_xattn", "g_ffn", "L0_xattn_Wq", "L0_xattn_bq", "L0_xattn_Wk", "L0_xattn_bk",
        "L0_xattn_Wv", "L0_xattn_bv", "L0_xattn_Wo", "L0_xattn_bo", "L0_ffn_w_gate", "L0_ffn_w_up", "L0_ffn_w_down"]


def kernel(**inputs):
    import ml_dtypes
    import numpy as _np
    import concourse.bacc as _bacc
    from concourse import mybir as _mybir
    from concourse.bass_utils import run_bass_kernel_spmd as _run

    nc = _bacc.Bacc("TRN2", target_bir_lowering=False, num_devices=1)
    arrays, aps = {}, {}
    for name in _INS:
        a = _np.ascontiguousarray(inputs[name])
        arrays[f"in_{name}"] = a
        aps[name] = nc.dram_tensor(f"in_{name}", a.shape, _mybir.dt.from_np(a.dtype), kind="ExternalInput").ap()
    dram = {}
    for name, a in tables().items():
        a = a.astype(ml_dtypes.bfloat16) if name == "band" else a
        arrays[f"table_{name}"] = a
        dram[name] = nc.dram_tensor(f"table_{name}", a.shape, _mybir.dt.from_np(a.dtype), kind="ExternalInput").ap()
    out = nc.dram_tensor("out", (B, S, D), F32, kind="ExternalOutput").ap()
    w = {n.rsplit("L0_xattn_")[-1].rsplit("L0_ffn_")[-1]: a for n, a in aps.items()}
    build(nc, dram, aps["x"], aps["ctx_1024"], w, out)
    r = _run(nc, [arrays], core_ids=[0])
    return r.results[0]["out"]
```

```python
from contextlib import ExitStack

import numpy as np

import concourse.bass as bass
from concourse import mybir

F32 = mybir.dt.float32
BF16 = mybir.dt.bfloat16
F16 = mybir.dt.float16
I16 = mybir.dt.int16
U16 = mybir.dt.uint16
ALU = mybir.AluOpType
ACT = mybir.ActivationFunctionType
X = mybir.AxisListType.X
XY = mybir.AxisListType.XY
RMAX = bass.bass_isa.ReduceOp.max

P = 128
B, S, D = 32, 256, 256
H, DK = 16, 16
HALF = DK // 2
I = 768
WINDOW = 50
BLOCK, WQMAX = 32, 7.0
AQMAX = 32767.0
EPS_LN, EPS_Q = 1e-5, 1e-12
WTOP = 2048.0
PRODUCTS = ((0, 0), (0, 1), (1, 0))
T = S // P
C = D // P
SPAN = P + WINDOW
FAR = S - SPAN
PAIRS = H // 2
SLOTS = PAIRS
NBUF = 3
HALVES = 2
STACK_Q = (0, 0, 0, 1, 1, 2)
STACK_K = (0, 1, 2, 0, 1, 0)
STACK = len(STACK_Q) * DK
SHIFT = 2
OUT = 2 * DK
TILE = 512
RING = 6
FIRST_ROUND, LAST_ROUND = 3, B // NBUF
LATE = 4


class Batch:

    def __init__(self, rnd, unit, late):
        back, self.buf = divmod(unit - late, NBUF)
        self.rnd = rnd + back
        self.n = self.rnd * NBUF + self.buf
        self.fixed = isinstance(self.n, int)
        self.real = 0 <= self.n < B if self.fixed else True

    def before(self, k):
        return Batch(self.rnd, self.buf, k)


def ring_tile(probs, b, pair, c):
    return probs[(b.buf * T * PAIRS + T * pair + c) % RING]


def reached(eng, sem, batch, per, k):
    value = batch.n * per + k
    if isinstance(value, int) and value <= 0:
        return
    eng.wait_ge(sem, value)


def carry(eng, sem):
    eng.sem_inc(sem, 1)


def loaded(eng, sems, batch):
    eng.wait_ge(sems[batch.buf], batch.rnd * 16 + 16)


def prepare(nc, dram, w, banks, keep):
    with ExitStack() as ctx:
        def sb(name, shape, dt=F32):
            return ctx.enter_context(nc.sbuf_tensor(name, shape, dt))

        def sem(name):
            return ctx.enter_context(nc.semaphore(name))

        attn = ("Wq", "Wk", "Wv", "Wo")
        ffn = ("w_gate", "w_up", "w_down")
        nat = {n: sb(f"nat_{n}", [P, T * D]) for n in attn}
        nat.update({n: sb(f"nat_{n}", [P, I * D // P]) for n in ffn})
        brow = sb("brow", [1, 4 * D])
        bpart = sb("bpart", [1, 3, 4 * D], BF16)
        brest = sb("brest", [1, 4 * D])
        brest2 = sb("brest2", [1, 4 * D])
        grow = sb("grow", [1, 2])
        one_row = sb("one_row", [1, P])
        nblk = I * D // P // BLOCK
        wabs = sb("wabs", [P, nblk])
        wscale = sb("wscale", [P, nblk])
        winv = sb("winv", [P, nblk])
        wround = sb("wround", [P, I * D // P], I16)
        ident_in, consts_in = sem("ident_in"), sem("consts_in")
        bias_in = sem("bias_and_gates_in")
        nat_in = {n: sem(f"in_{n}") for n in attn + ffn}
        weight_quantised = sem("weight_quantised")
        scales_max, scales_spread = sem("scales_max"), sem("scales_spread")
        low_parts = sem("low_parts")
        smax = sb("smax", [P, 2 * len(ffn)])
        dve_step = sem("dve_step")
        part_step = sem("part_step")
        ones_set = sem("ones_set")
        blocks_transposed = sem("blocks_transposed")
        bank_copied = sem("bank_copied")
        bias_rows = sem("bias_rows")
        block = ctx.enter_context(nc.Block())

        @block.sync
        def _(sp):
            sp.dma_start(keep["ident"][:], dram["ident"]).then_inc(ident_in, 16)
            for n in ffn[:1] + attn + ffn[1:]:
                rows = w[n].shape[0] // P
                sp.dma_start(nat[n][:].rearrange("p (o i) -> p o i", o=rows),
                             w[n].rearrange("(o p) i -> p o i", p=P)).then_inc(nat_in[n], 16)
                if n == ffn[0]:
                    for k, n in enumerate(("bq", "bk", "bv", "bo")):
                        sp.dma_start(brow[:, k * D:(k + 1) * D], w[n].rearrange("(a n) -> a n", a=1)).then_inc(bias_in, 16)
                    sp.dma_start(grow[:, 0:1], w["g_xattn"].rearrange("(a n) -> a n", a=1)).then_inc(bias_in, 16)
                    sp.dma_start(grow[:, 1:2], w["g_ffn"].rearrange("(a n) -> a n", a=1)).then_inc(bias_in, 16)
            sp.dma_start(keep["cos"][:], dram["cos"]).then_inc(consts_in, 16)
            sp.dma_start(keep["sin"][:], dram["sin"]).then_inc(consts_in, 16)
            sp.dma_start(keep["band"][:], dram["band"]).then_inc(consts_in, 16)
            sp.wait_ge(part_step, 5)
            for k in range(3):
                sp.dma_start(keep["bias"][k:k + 1, :], bpart[:, k, :]).then_inc(bias_rows, 16)
            sp.wait_ge(bias_rows, 48)
            sp.wait_ge(consts_in, 48)

        plan = []
        for n in attn:
            plan.append([(n, o, c, [keep[n + "T"]], D) for c in range(C) for o in range(T)])
        for n in ffn:
            rows, cols = w[n].shape[0] // P, w[n].shape[1] // P
            blks = [(n, o, c, keep[n + "T"], rows * P) for c in range(cols) for o in range(rows)]
            plan += [blks[k:k + 4] for k in range(0, len(blks), 4)]

        def place(blks):
            _, o, c, _, rows = blks[0]
            return c * rows + o * P

        @block.vector
        def _(dve):
            nc.vector.memset(one_row[:], 1.0).then_inc(ones_set, 1)
            nc.vector.memset(keep["ones3"][:], 1.0).then_inc(ones_set, 1)
            for k, value in enumerate((EPS_LN, -0.5, -1.0)):
                nc.vector.memset(keep["lnconst"][:, k * T:(k + 1) * T], value).then_inc(ones_set, 1)
            dve.wait_ge(ident_in, 16)
            nc.vector.tensor_copy(keep["identb"][:], keep["ident"][:]).then_inc(ones_set, 1)
            steps = 0
            banks_used = len(attn)
            for m, n in enumerate(ffn):
                def step(ins):
                    ins.then_inc(dve_step, 1)
                dve.wait_ge(nat_in[n], 16)
                blocks = nat[n][:].rearrange("p (k i) -> p k i", i=BLOCK)
                spread = [P, nblk, BLOCK]
                step(nc.vector.tensor_reduce(wabs[:], blocks, X, ALU.max, apply_absolute_value=True))
                dve.wait_ge(dve_step, steps + 1)
                step(nc.vector.tensor_scalar(wscale[:], wabs[:], 1.0 / WQMAX, EPS_Q, ALU.mult, ALU.max))
                dve.wait_ge(dve_step, steps + 2)
                step(nc.vector.reciprocal(winv[:], wscale[:]))
                nc.vector.tensor_reduce(smax[:, 2 * m:2 * m + 1], wscale[:], X, ALU.max).then_inc(scales_max, 1)
                dve.wait_ge(dve_step, steps + 3)
                step(nc.vector.tensor_tensor(wround[:].rearrange("p (k i) -> p k i", i=BLOCK), blocks,
                                             winv[:].unsqueeze(2).to_broadcast(spread), ALU.mult))
                dve.wait_ge(scales_spread, m + 1)
                largest = smax[:, 2 * m + 1:2 * m + 2]
                step(nc.vector.tensor_scalar(keep["unscale"][:, m:m + 1], largest, 1.0 / WTOP, None, ALU.mult))
                dve.wait_ge(dve_step, steps + 5)
                step(nc.vector.reciprocal(smax[:, 2 * m:2 * m + 1], keep["unscale"][:, m:m + 1]))
                dve.wait_ge(dve_step, steps + 6)
                step(nc.vector.tensor_scalar(wscale[:], wscale[:], smax[:, 2 * m:2 * m + 1], None, ALU.mult))
                dve.wait_ge(dve_step, steps + 7)
                nc.vector.tensor_tensor(blocks, wround[:].rearrange("p (k i) -> p k i", i=BLOCK),
                                        wscale[:].unsqueeze(2).to_broadcast(spread), ALU.mult)\
                    .then_inc(weight_quantised, 1)
                steps += 7
                dve.wait_ge(weight_quantised, m + 1)
                for k in range(banks_used, banks_used + nat[n].shape[1] // (4 * P)):
                    dve.wait_ge(bank_copied, k + 1)
                    _, _, _, dst, rows = plan[k][0]
                    at = place(plan[k])
                    nc.vector.tensor_tensor(dst[1][:, at:at + 4 * P], banks[k % 4][:], dst[0][:, at:at + 4 * P],
                                            ALU.subtract).then_inc(low_parts, 1)
                banks_used = k + 1
            dve.wait_ge(low_parts, len(plan) - len(attn))

        @block.gpsimd
        def _(pool):
            for k, (src, dst) in enumerate(((brow, brest), (brest, brest2))):
                pool.wait_ge(part_step, 2 * k + 1)
                nc.gpsimd.tensor_tensor(dst[:], src[:], bpart[:, k, :], ALU.subtract).then_inc(part_step, 1)
            for m in range(len(ffn)):
                pool.wait_ge(scales_max, m + 1)
                nc.gpsimd.partition_all_reduce(smax[:, 2 * m + 1:2 * m + 2], smax[:, 2 * m:2 * m + 1], P, RMAX)\
                    .then_inc(scales_spread, 1)

        @block.tensor
        def _(pe):
            pe.wait_ge(ones_set, 6)
            for k, blks in enumerate(plan):
                n = blks[0][0]
                if n in attn:
                    pe.wait_ge(nat_in[n], 16)
                else:
                    pe.wait_ge(weight_quantised, ffn.index(n) + 1)
                if k >= 4:
                    pe.wait_ge(bank_copied, k - 3)
                if k - 4 >= len(attn):
                    pe.wait_ge(low_parts, k - 3 - len(attn))
                for q, (_, o, c, _, _) in enumerate(blks):
                    width = w[n].shape[1]
                    last = nc.tensor.transpose(banks[k % 4][:, q * P:(q + 1) * P],
                                               nat[n][:, o * width + c * P:o * width + (c + 1) * P],
                                               keep["ident"][:])
                last.then_inc(blocks_transposed, 1)
            pe.wait_ge(bias_in, 96)
            nc.tensor.matmul(banks[4][:, 0:2], one_row[:], grow[:], start=True, stop=True).then_inc(blocks_transposed, 1)

        @block.scalar
        def _(act):
            act.wait_ge(bias_in, 96)
            for k, src in enumerate((brow, brest, brest2)):
                if k:
                    act.wait_ge(part_step, 2 * k)
                nc.scalar.activation(bpart[:, k, :], src[:], ACT.Copy).then_inc(part_step, 1)
            for k, blks in enumerate(plan):
                act.wait_ge(blocks_transposed, k + 1)
                at = place(blks)
                nc.scalar.activation(blks[0][3][0][:, at:at + 4 * P], banks[k % 4][:], ACT.Copy).then_inc(bank_copied, 1)
            act.wait_ge(blocks_transposed, len(plan) + 1)
            nc.scalar.activation(keep["tanh"][:], banks[4][:, 0:2], ACT.Tanh).then_inc(bank_copied, 1)
            act.wait_ge(bank_copied, len(plan) + 1)


def attention(nc, dram, x, ctx_in, scratch, banks, keep):
    with ExitStack() as ctx:
        def sb(name, shape, dt=F32):
            return ctx.enter_context(nc.sbuf_tensor(name, shape, dt))

        def sem(name):
            return ctx.enter_context(nc.semaphore(name))

        def bufs(name, shape, dt=F32, n=NBUF):
            return [sb(f"{name}{k}", shape, dt) for k in range(n)]

        W2 = T * D
        x_in, c_in = sb("x_in", [P, T, D]), sb("c_in", [P, T, D])
        stats, moments = sb("stats", [P, T, 6]), sb("moments", [P, T, 2])
        scale, scale_small = sb("ln_scale", [P, 2 * T]), sb("ln_small", [P, 2 * T])
        xn = x_in
        xT, cT = sb("xT", [P, C, S]), sb("cT", [P, C, S])
        by_cos = {n: sb(f"{n}_cos", [P, W2]) for n in "qk"}
        by_sin = {n: sb(f"{n}_sin", [P, W2]) for n in "qk"}
        rot = by_cos
        parts = {n: sb(f"{n}_parts", [P, 3, C * S], BF16) for n in "qk"}
        rest = by_sin
        q_stack, k_stack = bufs("q_stack", [P, H, S], BF16), bufs("k_stack", [P, H, S], BF16)
        V = bufs("V", [P, T * H, OUT])
        smax = bufs("smax", [P, T, H])
        shift = sb("shift", [P, T, HALVES, SHIFT, H // 2], BF16)
        shiftT = bufs("shiftT", [SHIFT * H // 2, S], BF16, HALVES)
        probs = bufs("probs", [P, 2, SPAN], n=RING)
        outT = sb("outT", [P, 4, S])
        rden = sb("rden", [P, T, H])
        att = sb("att", [P, T, D])
        attT = sb("attT", [P, C, S])
        x2 = bufs("x2", [P, T, D])
        stats2, moments2 = sb("stats2", [P, T, 6]), sb("moments2", [P, T, 2])
        scale2, scale2_small = sb("ln_scale2", [P, 2 * T]), sb("ln_small2", [P, 2 * T])
        xn2 = sb("xn2", [P, T, D])

        score_bank, scoreT_bank, out_bank = banks[0:2], banks[2:4], banks[4:6]
        bank_a, bank_b = banks[6], banks[7]
        shift_bank = (out_bank[1], out_bank[0])

        x_loaded, c_loaded = sem("x_loaded"), sem("c_loaded")
        xres_loaded = [sem(f"xres_loaded{k}") for k in range(NBUF)]
        parts_stored = {n: sem(f"{n}_parts_stored") for n in "qk"}
        stack_loaded = {n: [sem(f"{n}_stack_loaded{k}") for k in range(NBUF)] for n in "qk"}
        shift_loaded = [[sem(f"shift_loaded{h}_{k}") for k in range(NBUF)] for h in range(HALVES)]
        x2_stored = [sem(f"x2_stored{k}") for k in range(NBUF)]
        dve_carried, pool_carried, sp_carried = sem("dve_carried"), sem("pool_carried"), sem("sp_carried")
        consts_set, ones_rows_set = sem("consts_set"), sem("ones_rows_set")
        stats_taken, moments_taken = sem("stats_taken"), sem("moments_taken")
        x_normed = sem("x_normed")
        multiplied = {n: sem(f"{n}_multiplied") for n in "qk"}
        rest_ready = {n: sem(f"{n}_rest_ready") for n in "qk"}
        low_ready = {n: sem(f"{n}_low_ready") for n in "qk"}
        max_taken = sem("max_taken")
        shift_high, shift_ready = sem("shift_high"), sem("shift_ready")
        rden_ready, out_normed = sem("rden_ready"), sem("out_normed")
        x2_ready, stats2_taken, moments2_taken = sem("x2_ready"), sem("stats2_taken"), sem("moments2_taken")
        x2_normed, xmax_taken = sem("x2_normed"), sem("xmax_taken")
        cT_copied, xT_copied, v_copied = sem("cT_copied"), sem("xT_copied"), sem("v_copied")
        high_ready = {n: sem(f"{n}_high_ready") for n in "qk"}
        mid_ready = {n: sem(f"{n}_mid_ready") for n in "qk"}
        shiftT_copied, exp_done = sem("shiftT_copied"), sem("exp_done")
        outT_copied, attT_copied, xn2T_copied = sem("outT_copied"), sem("attT_copied"), sem("xn2T_copied")
        scale_steps, scale_ready = sem("scale_steps"), sem("ln_scale_ready")
        scale2_steps, scale2_ready = sem("scale2_steps"), sem("ln_scale2_ready")
        rotated = {n: sem(f"{n}_rotated") for n in "qk"}
        below_cut, band_cut = sem("below_cut"), sem("band_cut")
        c_transposed, x_transposed = sem("c_transposed"), sem("x_transposed")
        projected = {n: sem(f"{n}_projected") for n in "qkv"}
        rot_transposed = {n: sem(f"{n}_rot_transposed") for n in "qk"}
        shift_transposed = sem("shift_transposed")
        scored, scoredT, weighted = sem("scored"), sem("scoredT"), sem("weighted")
        out_transposed, att_transposed = sem("out_transposed"), sem("att_transposed")
        att_projected, x2_transposed = sem("att_projected"), sem("x2_transposed")


        rows_x = x.rearrange("b (t p) d -> b p t d", p=P)
        rows_c = ctx_in.rearrange("b (t p) d -> b p t d", p=P)

        def run(eng, steps):
            for it in range(-1, FIRST_ROUND * NBUF):
                steps(it // NBUF, it % NBUF)
            with eng.Fori(FIRST_ROUND, LAST_ROUND) as rnd:
                for unit in range(NBUF):
                    steps(rnd, unit)
            for it in range(LAST_ROUND * NBUF, B + LATE + 1):
                steps(it // NBUF, it % NBUF)

        def pair_at(slot, first):
            return (slot - first) % SLOTS, (first + (slot - first) % SLOTS) // SLOTS

        def low(eng, by, b, n):
            if not b.real:
                return
            reached(eng, mid_ready[n], b, 1, 1)
            by.tensor_tensor(parts[n][:, 2, :], rest[n][:], parts[n][:, 1, :], ALU.subtract)\
                .then_inc(low_ready[n], 1)

        S_FIRST, ST_FIRST, PV_FIRST = 11, 18, 20
        block = ctx.enter_context(nc.Block())

        @block.sync
        def _(sp):
            def load_x(b):
                if not b.real:
                    return
                reached(sp, x_transposed, b.before(1), 1, 1)
                sp.dma_start(x_in[:], rows_x[b.n]).then_inc(x_loaded, 16)
                reached(sp, c_transposed, b.before(1), 1, 1)
                sp.dma_start(c_in[:], rows_c[b.n]).then_inc(c_loaded, 16)

            def load_residual(b):
                if not b.real:
                    return
                bb = b.before(NBUF)
                if not bb.fixed or bb.n >= 0:
                    sp.wait_ge(x2_stored[b.buf], bb.rnd * 16 + 16)
                reached(sp, x2_normed, bb, T, T)
                sp.dma_start(x2[b.buf][:], rows_x[b.n]).then_inc(xres_loaded[b.buf], 16)

            def store_parts(b, n):
                if not b.real:
                    return
                reached(sp, mid_ready[n], b, 1, 1)
                reached(sp, low_ready[n], b, 1, 1)
                if not b.fixed:
                    carry(sp, sp_carried)
                if not b.fixed or b.n >= NBUF:
                    sp.wait_ge(stack_loaded[n][b.buf], b.rnd * 48)
                for k in range(3):
                    sp.dma_start(scratch[n][b.buf][k].rearrange("d (h ct) -> h d ct", h=PAIRS), parts[n][:, k, :])\
                        .then_inc(parts_stored[n], 16)

            def load_stacks(b, n):
                if not b.real:
                    return
                stack = (q_stack if n == "q" else k_stack)[b.buf]
                reached(sp, parts_stored[n], b, 48, 48)
                reached(sp, scoredT, b.before(NBUF), 2 * PAIRS, 2 * PAIRS)
                row = 0
                for g in range(3):
                    rows = (3 - g) * DK
                    sp.dma_start(stack[row:row + rows, :, :].rearrange("r s t -> r (s t)"), scratch[n + "_rows"](b.buf, g)).then_inc(stack_loaded[n][b.buf], 16)
                    row += rows

            def load_shift(b, half):
                if not b.real:
                    return
                reached(sp, shiftT_copied, b, HALVES, half + 1)
                for k in range(SHIFT):
                    sp.dma_start(q_stack[b.buf][STACK + k:STACK + k + 1, half * 8:half * 8 + 8, :],
                                 shiftT[half][k * 8:(k + 1) * 8, :]).then_inc(shift_loaded[half][b.buf], 16)

            def store_x2(b):
                if not b.real:
                    return
                reached(sp, x2_ready, b, 1, 1)
                sp.dma_start(scratch["x2"][b.n], x2[b.buf][:]).then_inc(x2_stored[b.buf], 16)

            def steps(rnd, unit):
                load_shift(Batch(rnd, unit, 2), 0)
                load_stacks(Batch(rnd, unit, 1), "q")
                load_x(Batch(rnd, unit, -1))
                store_x2(Batch(rnd, unit, 4))
                load_residual(Batch(rnd, unit, 3))
                load_shift(Batch(rnd, unit, 2), 1)
                store_parts(Batch(rnd, unit, 0), "k")
                store_parts(Batch(rnd, unit, 0), "q")
                load_stacks(Batch(rnd, unit, 0), "k")

            run(sp, steps)
            for k in range(NBUF):
                sp.wait_ge(x2_stored[k], 16 * len(range(k, B, NBUF)))

        @block.gpsimd
        def _(pool):
            def scale_of(b, taken, steps_done, ready, mom, small, out):
                if not b.real:
                    return
                consts = keep["lnconst"]
                reached(pool, taken, b, T, T)
                nc.gpsimd.tensor_tensor(small[:, 0:T], mom[:, :, 1], consts[:, 0:T], ALU.add).then_inc(steps_done, 1)
                nc.gpsimd.tensor_tensor(small[:, T:2 * T], mom[:, :, 0], consts[:, 2 * T:3 * T], ALU.mult)\
                    .then_inc(steps_done, 1)
                reached(pool, steps_done, b, 3, 2)
                nc.gpsimd.tensor_tensor(out[:, 0:T], small[:, 0:T], consts[:, T:2 * T], ALU.pow).then_inc(steps_done, 1)
                reached(pool, steps_done, b, 3, 3)
                nc.gpsimd.tensor_tensor(out[:, T:2 * T], small[:, T:2 * T], out[:, 0:T], ALU.mult).then_inc(ready, 1)

            def rotate(b, n):
                if not b.real:
                    return
                reached(pool, multiplied[n], b, 3, 3)
                nc.gpsimd.tensor_tensor(rot[n][:], by_cos[n][:], by_sin[n][:], ALU.add).then_inc(rotated[n], 1)

            def cut(b, pair):
                if not b.real:
                    return
                for c in range(T):
                    off = c * WINDOW
                    t = ring_tile(probs, b, pair, c)
                    reached(pool, exp_done, b, 2 * PAIRS, 2 * pair + c + 1)
                    if not b.fixed:
                        carry(pool, pool_carried)
                    n = P - 1 - WINDOW + off
                    nc.gpsimd.affine_select(out=t[:, :, 0:n], in_=t[:, :, 0:n], pattern=[[0, 2], [1, n]],
                                            compare_op=ALU.is_ge, fill=0.0, base=WINDOW - off,
                                            channel_multiplier=-1).then_inc(below_cut, 1)
                for c in range(T):
                    off = c * WINDOW
                    t = ring_tile(probs, b, pair, c)
                    reached(pool, below_cut, b, 2 * PAIRS, 2 * pair + c + 1)
                    if not b.fixed:
                        carry(pool, pool_carried)
                    n = WINDOW + 1 + off
                    nc.gpsimd.affine_select(out=t[:, :, n:SPAN], in_=t[:, :, n:SPAN], pattern=[[0, 2], [-1, SPAN - n]],
                                            compare_op=ALU.is_ge, fill=0.0, base=WINDOW + off - n,
                                            channel_multiplier=1).then_inc(band_cut, 1)

            def steps(rnd, unit):
                for slot in range(SLOTS):
                    if slot == 5:
                        scale_of(Batch(rnd, unit, -1), moments_taken, scale_steps, scale_ready, moments, scale_small, scale)
                    if slot == 2:
                        rotate(Batch(rnd, unit, 0), "k")
                    if slot == 3:
                        rotate(Batch(rnd, unit, 0), "q")
                    if slot == 1:
                        scale_of(Batch(rnd, unit, 4), moments2_taken, scale2_steps, scale2_ready, moments2, scale2_small, scale2)
                    pair, late = pair_at(slot, ST_FIRST)
                    cut(Batch(rnd, unit, late), pair)
                    if slot == 5:
                        low(pool, nc.gpsimd, Batch(rnd, unit, 0), "q")

            run(pool, steps)

        @block.scalar
        def _(act):
            def copy_out(b, done, per, k, src, dst, signal, free=()):
                if not b.real:
                    return
                reached(act, done, b, per, k)
                for f in free:
                    reached(act, *f)
                nc.scalar.activation(dst, src, ACT.Copy).then_inc(signal, 1)

            def normalise(b, src, dst, scale, ready, signal):
                reached(act, ready, b, 1, 1)
                for t in range(T):
                    nc.scalar.activation(dst[:, t, :], src[:, t, :], ACT.Identity, scale=scale[:, t:t + 1],
                                         bias=scale[:, T + t:T + t + 1]).then_inc(signal, 1)

            def high(b, n, bank):
                if not b.real:
                    return
                reached(act, rot_transposed[n], b, 1, 1)
                reached(act, parts_stored[n], b.before(1), 48, 48)
                nc.scalar.activation(parts[n][:, 0, :], bank[:], ACT.Copy).then_inc(high_ready[n], 1)

            def middle(b, n):
                if not b.real:
                    return
                reached(act, rest_ready[n], b, 1, 1)
                nc.scalar.activation(parts[n][:, 1, :], rest[n][:], ACT.Copy).then_inc(mid_ready[n], 1)

            def exps(b, pair):
                if not b.real:
                    return
                for c in range(T):
                    reached(act, scoredT, b, 2 * PAIRS, 2 * pair + c + 1)
                    reached(act, weighted, b, PAIRS, pair - RING // 2 + 1)
                    nc.scalar.activation(ring_tile(probs, b, pair, c)[:].rearrange("p e j -> p (e j)"),
                                         scoreT_bank[c][:, 0:2 * SPAN], ACT.Exp, scale=DK ** -0.5)\
                        .then_inc(exp_done, 1)

            def shift_copy(b, half):
                if not b.real:
                    return
                reached(act, shift_transposed, b, HALVES, half + 1)
                bb = b.before(1)
                if not bb.fixed or bb.n >= 0:
                    act.wait_ge(shift_loaded[half][bb.buf], bb.rnd * 16 * SHIFT + 16 * SHIFT)
                nc.scalar.activation(shiftT[half][:], shift_bank[half][0:SHIFT * 8, 0:S // 2].bitcast(BF16), ACT.Copy)\
                    .then_inc(shiftT_copied, 1)

            def copy_outT(b, half):
                copy_out(b, weighted, PAIRS, PAIRS // 2 * (half + 1), out_bank[half][:],
                         outT[:, 2 * half:2 * half + 2, :].rearrange("p a t -> p (a t)"), outT_copied,
                         [(out_transposed, b.before(1), HALVES, half + 1)])

            def steps(rnd, unit):
                nxt, b0, b1, b2, b3, b4 = (Batch(rnd, unit, k) for k in range(-1, 5))
                for slot in range(SLOTS):
                    if slot == 0:
                        copy_outT(b3, 0)
                        copy_out(b0, c_transposed, 1, 1, bank_a[:], cT[:].rearrange("p c t -> p (c t)"), cT_copied,
                                 [(projected["v"], b0.before(1), 1, 1)])
                    if slot == 1:
                        copy_out(b0, x_transposed, 1, 1, bank_a[:], xT[:].rearrange("p c t -> p (c t)"), xT_copied,
                                 [(projected["q"], b0.before(1), 1, 1)])
                    if slot == 3:
                        high(b0, "k", bank_b)
                    if slot == 4:
                        shift_copy(b2, 1)
                        copy_outT(b3, 1)
                        middle(b0, "k")
                        high(b0, "q", bank_a)
                    if slot == 5:
                        if b0.fixed and b0.n == 0:
                            act.wait_ge(consts_set, 2 * NBUF)
                        if b0.real:
                            copy_out(b0, projected["v"], 1, 1, bank_b[:].rearrange("p (h d) -> p h d", d=DK),
                                     V[b0.buf][:, :, 0:DK], v_copied, [(weighted, b0.before(NBUF), PAIRS, PAIRS)])
                        middle(b0, "q")
                    if slot == 6:
                        if b4.real:
                            reached(act, x2_transposed, b4, 1, 1)
                            nc.scalar.activation(keep["xnT"][:, :, bass.ds(b4.n * S, S)],
                                                 bank_b[:].rearrange("p (c t) -> p c t", c=C), ACT.Copy)\
                                .then_inc(xn2T_copied, 1)
                    if slot == 7:
                        copy_out(b3, att_transposed, 1, 1, bank_a[:], attT[:].rearrange("p c t -> p (c t)"),
                                 attT_copied, [(att_projected, b3.before(1), 1, 1)])
                        if nxt.real:
                            normalise(nxt, x_in, xn, scale, scale_ready, x_normed)
                    pair, late = pair_at(slot, ST_FIRST)
                    exps(Batch(rnd, unit, late), pair)
                    if slot == 4 and b4.real:
                        reached(act, x2_transposed, b4.before(1), 1, 1)
                        normalise(b4, x2[b4.buf], xn2, scale2, scale2_ready, x2_normed)
                    if slot == 7:
                        shift_copy(b1, 0)

            run(act, steps)

        @block.vector
        def _(dve):
            for k in range(NBUF):
                nc.vector.memset(V[k][:], 0.0).then_inc(consts_set, 1)
            dve.wait_ge(consts_set, NBUF)
            for k in range(NBUF):
                nc.vector.memset(V[k][:, :, DK:DK + 1], 1.0).then_inc(consts_set, 1)
            dve.wait_ge(consts_set, 2 * NBUF)

            def statistics(b, src, st, mom, taken, aggregated):
                for t in range(T):
                    nc.vector.bn_stats(st[:, t, :], src[:, t, :]).then_inc(taken, 1)
                for t in range(T):
                    reached(dve, taken, b, T, t + 1)
                    if not b.fixed:
                        carry(dve, dve_carried)
                    nc.vector.bn_aggr(mom[:, t, :], st[:, t, :]).then_inc(aggregated, 1)

            def rope(b, n, bank):
                if not b.real:
                    return
                reached(dve, projected[n], b, 1, 1)
                reached(dve, rot_transposed[n], b.before(1), 1, 1)
                if n == "q":
                    reached(dve, low_ready[n], b.before(1), 1, 1)
                nc.vector.tensor_tensor(by_cos[n][:], bank[:], keep["cos"][:], ALU.mult).then_inc(multiplied[n], 1)
                src = bank[:].rearrange("p (h d) -> p h d", d=DK)
                sin = keep["sin"][:].rearrange("p (h d) -> p h d", d=DK)
                dst = by_sin[n][:].rearrange("p (h d) -> p h d", d=DK)
                nc.vector.tensor_tensor(dst[:, :, 0:HALF], src[:, :, HALF:DK], sin[:, :, 0:HALF], ALU.mult)\
                    .then_inc(multiplied[n], 1)
                nc.vector.tensor_tensor(dst[:, :, HALF:DK], src[:, :, 0:HALF], sin[:, :, HALF:DK], ALU.mult)\
                    .then_inc(multiplied[n], 1)

            def remainder(b, n, bank):
                if not b.real:
                    return
                reached(dve, high_ready[n], b, 1, 1)
                nc.vector.tensor_tensor(rest[n][:], bank[:], parts[n][:, 0, :], ALU.subtract)\
                    .then_inc(rest_ready[n], 1)

            def maxima(b, pair):
                if not b.real:
                    return
                for t in range(T):
                    reached(dve, scored, b, 2 * PAIRS, 2 * pair + t + 1)
                    if not b.fixed:
                        carry(dve, dve_carried)
                    for e in range(2):
                        h = 2 * pair + e
                        mine = score_bank[t][:, e * SPAN:(e + 1) * SPAN]
                        ins = nc.vector.tensor_tensor_reduce(
                            out=mine, in0=mine, in1=keep["band"][:, t, :],
                            scale=1.0, scalar=-3e38, op0=ALU.add, op1=ALU.max, accum_out=smax[b.buf][:, t, h:h + 1])
                    ins.then_inc(max_taken, 1)

            def shift_parts(b, half):
                if not b.real:
                    return
                reached(dve, max_taken, b, 2 * PAIRS, PAIRS * (half + 1))
                reached(dve, shift_transposed, b.before(1), HALVES, half + 1)
                src = smax[b.buf][:, :, half * 8:half * 8 + 8]
                nc.vector.tensor_scalar(shift[:, :, half, 0, :], src, -1.0, None, ALU.mult).then_inc(shift_high, 1)
                reached(dve, shift_high, b, HALVES, half + 1)
                nc.vector.scalar_tensor_tensor(shift[:, :, half, 1, :], src, -1.0, shift[:, :, half, 0, :],
                                               ALU.mult, ALU.subtract).then_inc(shift_ready, 1)

            def divide(b, half):
                if not b.real:
                    return
                reached(dve, out_transposed, b, HALVES, half + 1)
                src = out_bank[half][:].rearrange("p (t s d) -> p t s d", t=T, d=OUT)
                mine = rden[:, :, half * PAIRS:(half + 1) * PAIRS]
                nc.vector.reciprocal(mine, src[:, :, :, DK]).then_inc(rden_ready, 1)
                reached(dve, rden_ready, b, HALVES, half + 1)
                reached(dve, att_transposed, b.before(1), 1, 1)
                heads = PAIRS // HALVES
                for c in range(C):
                    at = c * P + half * heads * DK
                    ins = nc.vector.tensor_tensor(
                        att[:, :, at:at + heads * DK].rearrange("p t (h d) -> p t h d", d=DK), src[:, :, c::2, 0:DK],
                        mine[:, :, c::2].unsqueeze(3).to_broadcast([P, T, heads, DK]), ALU.mult)
                ins.then_inc(out_normed, 1)

            def residual(b):
                if not b.real:
                    return
                loaded(dve, xres_loaded, b)
                reached(dve, att_projected, b, 1, 1)
                nc.vector.scalar_tensor_tensor(x2[b.buf][:].rearrange("p t d -> p (t d)"), bank_b[:],
                                               keep["tanh"][:, 0:1], x2[b.buf][:].rearrange("p t d -> p (t d)"),
                                               ALU.mult, ALU.add).then_inc(x2_ready, 1)
                reached(dve, x2_ready, b, 1, 1)
                statistics(b, x2[b.buf], stats2, moments2, stats2_taken, moments2_taken)

            def steps(rnd, unit):
                nxt, b0, b1, b2, b3, b4 = (Batch(rnd, unit, k) for k in range(-1, 5))
                for slot in range(SLOTS):
                    if slot == 0:
                        residual(b4)
                    if slot == 1 and b0.fixed and 0 <= b0.n < NBUF:
                        nc.vector.memset(k_stack[b0.n][STACK:P, :, :], 1.0).then_inc(ones_rows_set, 1)
                    if slot == 2:
                        rope(b0, "k", bank_b)
                        divide(b3, 0)
                    if slot == 3:
                        shift_parts(b2, 1)
                        rope(b0, "q", bank_a)
                    if slot == 4:
                        remainder(b0, "k", bank_b)
                    if slot == 5:
                        low(dve, nc.vector, b0, "k")
                        remainder(b0, "q", bank_a)
                    if slot == 7:
                        shift_parts(b1, 0)
                    pair, late = pair_at(slot, S_FIRST)
                    maxima(Batch(rnd, unit, late), pair)
                    if slot == 5:
                        divide(b3, 1)
                    if slot == 4 and nxt.real:
                        reached(dve, x_loaded, nxt, 16, 16)
                        statistics(nxt, x_in, stats, moments, stats_taken, moments_taken)
                    if slot == 7 and b4.real:
                        reached(dve, xn2T_copied, b4, 1, 1)
                        nc.vector.tensor_reduce(keep["xmax"][:, bass.ds(b4.n, 1)], keep["xnT"][:, :, bass.ds(b4.n * S, S)],
                                                XY, ALU.max, apply_absolute_value=True).then_inc(xmax_taken, 1)

            run(dve, steps)
            dve.wait_ge(xmax_taken, B)

        @block.tensor
        def _(pe):
            ident, identb = keep["ident"], keep["identb"]

            def transpose4(bank, src):
                for t in range(T):
                    for c in range(C):
                        last = nc.tensor.transpose(bank[:, c * S + t * P:c * S + (t + 1) * P],
                                                   src[:, t * D + c * P:t * D + (c + 1) * P], ident[:])
                return last

            def project(bank, srcT, weight, which):
                for t in range(T):
                    out = bank[:, t * D:(t + 1) * D]
                    nc.tensor.matmul(out, keep["ones3"][:], keep["bias"][:, which * D:(which + 1) * D],
                                     start=True, stop=False)
                    for c in range(C):
                        last = nc.tensor.matmul(out, srcT[:, c, t * P:(t + 1) * P], weight[:, c * D:(c + 1) * D],
                                                start=False, stop=(c == C - 1))
                return last

            def scores(b, pair):
                if not b.real:
                    return
                if pair == 0:
                    pe.wait_ge(stack_loaded["k"][b.buf], b.rnd * 48 + 48)
                    pe.wait_ge(stack_loaded["q"][b.buf], b.rnd * 48 + 48)
                for t in range(T):
                    reached(pe, max_taken, b, 2 * PAIRS, 2 * pair + t - 1)
                    bank = score_bank[t]
                    for e in range(2):
                        h = 2 * pair + e
                        last = nc.tensor.matmul(bank[:, e * SPAN:(e + 1) * SPAN],
                                                q_stack[b.buf][0:STACK, h, t * P:(t + 1) * P],
                                                k_stack[b.buf][0:STACK, h, t * FAR:t * FAR + SPAN],
                                                start=True, stop=True)
                    last.then_inc(scored, 1)

            def scoresT(b, pair):
                if not b.real:
                    return
                if b.fixed and b.n < NBUF and pair == 0:
                    pe.wait_ge(ones_rows_set, b.n + 1)
                if pair % 4 == 0:
                    pe.wait_ge(shift_loaded[pair // 4][b.buf], b.rnd * 16 * SHIFT + 16 * SHIFT)
                for c in range(T):
                    reached(pe, exp_done, b, 2 * PAIRS, 2 * pair + c - 1)
                    for e in range(2):
                        h = 2 * pair + e
                        last = nc.tensor.matmul(scoreT_bank[c][:, e * SPAN:(e + 1) * SPAN],
                                                k_stack[b.buf][0:STACK + SHIFT, h, c * P:(c + 1) * P],
                                                q_stack[b.buf][0:STACK + SHIFT, h, c * FAR:c * FAR + SPAN],
                                                start=True, stop=True)
                    last.then_inc(scoredT, 1)

            def weigh(b, pair, later):
                if not b.real:
                    return
                half, col = pair // 4, (pair // 2 % 2) * S
                if pair == 0:
                    reached(pe, v_copied, b, 1, 1)
                if pair % 4 == 0:
                    reached(pe, outT_copied, b, 2, half - 1)
                    if half == 0:
                        reached(pe, shiftT_copied, b, HALVES, 2)
                    elif later.real:
                        reached(pe, shiftT_copied, later, HALVES, 1)
                reached(pe, band_cut, b, 2 * PAIRS, 2 * pair + 2)
                for e in range(2):
                    h = 2 * pair + e
                    row = (h % 4) * OUT
                    for c in range(T):
                        last = nc.tensor.matmul(out_bank[half][row:row + OUT, col + c * FAR:col + c * FAR + SPAN],
                                                V[b.buf][:, c * H + h // 2 + PAIRS * (h % 2), :], ring_tile(probs, b, pair, c)[:, e, :],
                                                start=(c == 0), stop=(c == T - 1), skip_group_check=True)
                last.then_inc(weighted, 1)

            def shift_rows(b, half):
                if not b.real:
                    return
                reached(pe, shift_ready, b, HALVES, half + 1)
                for t in range(T):
                    last = nc.tensor.transpose(shift_bank[half][0:SHIFT * 8, t * P // 2:(t + 1) * P // 2].bitcast(BF16),
                                               shift[:, t, half, :, :].rearrange("p a h -> p (a h)"), identb[:])
                last.then_inc(shift_transposed, 1)

            def out_rows(b, half):
                if not b.real:
                    return
                reached(pe, outT_copied, b, HALVES, half + 1)
                for t in range(T):
                    for quad in range(2):
                        last = nc.tensor.transpose(out_bank[half][:, (2 * t + quad) * P:(2 * t + quad + 1) * P],
                                                   outT[:, 2 * half + quad, t * P:(t + 1) * P], ident[:])
                last.then_inc(out_transposed, 1)

            def steps(rnd, unit):
                b0, b1, b2, b3, b4 = (Batch(rnd, unit, k) for k in range(5))
                for slot in range(SLOTS):
                    if slot == 0 and b0.real:
                        reached(pe, c_loaded, b0, 16, 16)
                        if b4.real:
                            reached(pe, attT_copied, b4, 1, 1)
                        else:
                            reached(pe, rest_ready["q"], b0.before(1), 1, 1)
                        transpose4(bank_a, c_in[:].rearrange("p t d -> p (t d)")).then_inc(c_transposed, 1)
                    if slot == 1 and b0.real:
                        reached(pe, x_normed, b0, T, T)
                        reached(pe, cT_copied, b0, 1, 1)
                        transpose4(bank_a, xn[:].rearrange("p t d -> p (t d)")).then_inc(x_transposed, 1)
                    if slot == 6 and b4.real:
                        if b0.real:
                            reached(pe, v_copied, b0, 1, 1)
                        reached(pe, x2_normed, b4, T, T)
                        transpose4(bank_b, xn2[:].rearrange("p t d -> p (t d)")).then_inc(x2_transposed, 1)
                    if slot == 5 and b0.real:
                        reached(pe, rest_ready["k"], b0, 1, 1)
                        project(bank_b, cT, keep["WvT"], 2).then_inc(projected["v"], 1)
                    if slot == 5:
                        out_rows(b3, 1)
                    if slot == 7 and b3.real:
                        reached(pe, out_normed, b3, HALVES, 2)
                        if b0.real:
                            reached(pe, rest_ready["q"], b0, 1, 1)
                        elif b4.real:
                            reached(pe, attT_copied, b4, 1, 1)
                        transpose4(bank_a, att[:].rearrange("p t d -> p (t d)")).then_inc(att_transposed, 1)

                    pair, late = pair_at(slot, S_FIRST)
                    scores(Batch(rnd, unit, late), pair)

                    if slot == 1 and b0.real:
                        reached(pe, cT_copied, b0, 1, 1)
                        if b4.real:
                            reached(pe, x2_ready, b4, 1, 1)
                        else:
                            reached(pe, v_copied, b0.before(1), 1, 1)
                        project(bank_b, cT, keep["WkT"], 1).then_inc(projected["k"], 1)
                    if slot == 1:
                        out_rows(b3, 0)
                    if slot == 2 and b0.real:
                        reached(pe, xT_copied, b0, 1, 1)
                        project(bank_a, xT, keep["WqT"], 0).then_inc(projected["q"], 1)
                    if slot == 3:
                        if b0.real:
                            reached(pe, rotated["k"], b0, 1, 1)
                            transpose4(bank_b, rot["k"]).then_inc(rot_transposed["k"], 1)
                        if b3.real:
                            reached(pe, out_normed, b3, HALVES, 1)
                        shift_rows(b2, 1)
                    if slot == 4 and b0.real:
                        reached(pe, rotated["q"], b0, 1, 1)
                        transpose4(bank_a, rot["q"]).then_inc(rot_transposed["q"], 1)
                    if slot == 7:
                        if b3.real:
                            if b4.real:
                                reached(pe, xn2T_copied, b4, 1, 1)
                            elif b0.real:
                                reached(pe, v_copied, b0, 1, 1)
                            reached(pe, attT_copied, b3, 1, 1)
                            project(bank_b, attT, keep["WoT"], 3).then_inc(att_projected, 1)
                        shift_rows(b1, 0)

                    pair, late = pair_at(slot, ST_FIRST)
                    scoresT(Batch(rnd, unit, late), pair)
                    pair, late = pair_at(slot, PV_FIRST)
                    weigh(Batch(rnd, unit, late), pair, b2)

            run(pe, steps)


def feed_forward(nc, scratch, out, banks, keep):
    TILES = B * S // TILE
    F = I // P
    HF = F // 2
    UW = HF * TILE
    UNITS = 2 * TILES
    with ExitStack() as ctx:
        def sb(name, shape, dt=F32):
            return ctx.enter_context(nc.sbuf_tensor(name, shape, dt))

        def sem(name):
            return ctx.enter_context(nc.semaphore(name))

        def bufs(name, shape, dt=F32):
            return [sb(f"{name}{k}", shape, dt) for k in range(2)]

        scales = keep["scales"]
        (X_MAX, X_S, X_INV, G_W, U_W, O_W, G_MAX, G_S, G_INV, U_MAX, U_S, U_INV, H_MAX, H_S, H_INV, O_MAX, O_S, O_INV, UNIT_O, H_FACTOR) = range(20)
        col = lambda k: scales[:, k:k + 1]
        peak = keep["peak"]
        gmx, gmn, umx, hmx, omx = (keep["maxima"][:, k, :] for k in range(5))
        xnT = keep["xnT"]
        x_parts = xnT[:].rearrange("p c t -> p (c t)").bitcast(F16).rearrange("p (c t) -> p c t", c=C)

        def x_part(j, part):
            return x_parts[:, :, bass.ds(j * (2 * TILE) + part * TILE, TILE)]

        def inner_products(pe, bank, weights, j, f):
            for c in range(C):
                for k, (xp, wp) in enumerate(PRODUCTS):
                    last = nc.tensor.matmul(bank[:], weights[wp][:, c * I + f * P:c * I + (f + 1) * P],
                                            x_parts[:, c, bass.ds(j * (2 * TILE) + xp * TILE, TILE)],
                                            start=(c == 0 and k == 0), stop=(c == C - 1 and k == len(PRODUCTS) - 1))
            return last

        carried = sem("carried")
        small = sem("small")
        reduced = sem("reduced")
        asked = sem("asked")

        def scale_chain(dve, src, maxi, s, inv, done_small, n_red):
            nc.vector.tensor_reduce(peak[:, 0:1], src, X, ALU.max).then_inc(asked, 1)
            dve.wait_ge(reduced, n_red)
            nc.vector.tensor_scalar(col(s), col(maxi), 1.0 / AQMAX, EPS_Q, ALU.mult, ALU.max).then_inc(small, 1)
            dve.wait_ge(small, done_small + 1)
            nc.vector.reciprocal(col(inv), col(s)).then_inc(small, 1)
            dve.wait_ge(small, done_small + 2)

        with ExitStack() as c1:
            def sb1(name, shape, dt=F32):
                return c1.enter_context(nc.sbuf_tensor(name, shape, dt))

            def sem1(name):
                return c1.enter_context(nc.semaphore(name))

            g_stage = [sb1(f"g_stage{k}", [P, UW]) for k in range(2)]
            xint = sb1("xint", [P, C, TILE], I16)
            x_rounded, x_quantised = sem1("x_rounded"), sem1("x_quantised")
            gate_made, gate_copied, gate_seen = sem1("gate_made"), sem1("gate_copied"), sem1("gate_seen")
            gate_stored = [sem1(f"gate_stored{k}") for k in range(2)]
            product_scales, x_high = sem1("product_scales"), sem1("x_high")
            block = c1.enter_context(nc.Block())

            @block.sync
            def _(sp):
                with sp.Fori(0, TILES) as j:
                    for h in range(2):
                        sp.wait_ge(gate_copied, j * F + HF * (h + 1))
                        sp.dma_start(scratch["gate"][j][:, h * UW:(h + 1) * UW], g_stage[h][:])\
                            .then_inc(gate_stored[h], 16)
                for h in range(2):
                    sp.wait_ge(gate_stored[h], 16 * TILES)

            @block.gpsimd
            def _(pool):
                pool.wait_ge(asked, 1)
                nc.gpsimd.partition_all_reduce(col(X_MAX), peak[:, 0:1], P, RMAX).then_inc(reduced, 1)

            @block.vector
            def _(dve):
                scale_chain(dve, keep["xmax"][:], X_MAX, X_S, X_INV, 0, 1)
                for k, dst in enumerate((G_W, U_W)):
                    nc.vector.tensor_tensor(col(dst), col(X_S), keep["unscale"][:, k:k + 1], ALU.mult)\
                        .then_inc(product_scales, 1)
                dve.wait_ge(product_scales, 2)

                def round_rows(j):
                    nc.vector.tensor_scalar(xint[:], xnT[:, :, bass.ds(j * TILE, TILE)], col(X_INV), None, ALU.mult)\
                        .then_inc(x_rounded, 1)

                def low_part(j):
                    dve.wait_ge(x_high, j + 1)
                    nc.vector.tensor_tensor(x_part(j, 1), xint[:], x_part(j, 0), ALU.subtract).then_inc(x_quantised, 1)
                    dve.wait_ge(x_quantised, j + 1)

                def extremes(j, h):
                    dve.wait_ge(gate_copied, j * F + HF * (h + 1))
                    nc.vector.tensor_reduce(gmx[:, bass.ds(j * 2 + h, 1)], g_stage[h][:], X, ALU.max)
                    nc.vector.tensor_reduce(gmn[:, bass.ds(j * 2 + h, 1)], g_stage[h][:], X, ALU.min)\
                        .then_inc(gate_seen, 1)

                round_rows(0)
                low_part(0)
                with dve.Fori(0, TILES - 1) as j:
                    round_rows(j + 1)
                    extremes(j, 0)
                    low_part(j + 1)
                    extremes(j, 1)
                for h in range(2):
                    extremes(TILES - 1, h)
                dve.wait_ge(gate_seen, UNITS)

            @block.scalar
            def _(act):
                act.wait_ge(product_scales, 2)

                def high_part(j):
                    act.wait_ge(x_rounded, j + 1)
                    nc.scalar.activation(x_part(j, 0), xint[:], ACT.Copy).then_inc(x_high, 1)

                def copies(j, h, first):
                    for f in range(h * HF, (h + 1) * HF):
                        act.wait_ge(gate_made, j * F + f + 1)
                        if f % HF == 0 and not first:
                            act.wait_ge(gate_seen, j * 2 + h - 1)
                            act.wait_ge(gate_stored[h], j * 16)
                        nc.scalar.activation(g_stage[h][:, (f % HF) * TILE:(f % HF + 1) * TILE], banks[f][:], ACT.Copy,
                                             scale=col(G_W)).then_inc(gate_copied, 1)

                def tile_steps(j, first):
                    copies(j, 0, first)
                    high_part(j + 1)
                    copies(j, 1, first)

                high_part(0)
                tile_steps(0, True)
                with act.Fori(1, TILES - 1) as j:
                    tile_steps(j, False)
                for h in range(2):
                    copies(TILES - 1, h, False)

            @block.tensor
            def _(pe):
                def products(j, first):
                    pe.wait_ge(x_quantised, j + 1)
                    for f in range(F):
                        if not first:
                            pe.wait_ge(gate_copied, j * F - F + f + 1)
                        inner_products(pe, banks[f], keep["w_gateT"], j, f).then_inc(gate_made, 1)
                products(0, True)
                with pe.Fori(1, TILES) as j:
                    products(j, False)

        inner_int = sb("inner_int", [P, TILES * 2 * UW], I16)
        pool_carried, act_carried = sem("pool_waits_carried"), sem("act_waits_carried")

        def kept(j, h):
            return inner_int[:, bass.ds(j * (2 * UW) + h * UW, UW)]

        with ExitStack() as c2:
            def sb2(name, shape, dt=F32):
                return c2.enter_context(nc.sbuf_tensor(name, shape, dt))

            def sem2(name):
                return c2.enter_context(nc.semaphore(name))

            u_stage = [sb2(f"u_stage{k}", [P, UW]) for k in range(2)]
            g_in = [sb2(f"g_in{k}", [P, UW]) for k in range(2)]
            g_int = [keep["w_gateT"][k][:].bitcast(I16) for k in range(2)]
            sig_int = sb2("sig_int", [P, UW], U16)
            sig = silu = g_in
            unit_max, max_kept = sb2("unit_max_h", [P, 2]), sem2("h_max_kept")
            probe = sb2("probe", [P, 4])
            probe_int = sb2("probe_int", [P, 1], I16)
            probe_sig = sb2("probe_sig", [P, 1], U16)
            up_made, up_copied, up_seen = sem2("up_made"), sem2("up_copied"), sem2("up_seen")
            up_stored = [sem2(f"up_stored{k}") for k in range(2)]
            gate_loaded = [sem2(f"gate_loaded{k}") for k in range(2)]
            gate_kept = sem2("gate_kept")
            gate_rounded, sig_done = sem2("gate_rounded"), sem2("sig_done")
            sig_rounded, silu_done = sem2("sig_rounded"), sem2("silu_done")
            scale_ready, probe_step, probe_act = sem2("scale_ready"), sem2("probe_step"), sem2("probe_act")
            block = c2.enter_context(nc.Block())

            @block.sync
            def _(sp):
                def load(j, h):
                    sp.dma_start(g_in[h][:], scratch["gate"][j][:, h * UW:(h + 1) * UW]).then_inc(gate_loaded[h], 16)

                def store(j, h):
                    sp.wait_ge(up_copied, j * F + HF * (h + 1))
                    sp.dma_start(scratch["up"][j][:, h * UW:(h + 1) * UW], u_stage[h][:]).then_inc(up_stored[h], 16)

                for h in range(2):
                    load(0, h)
                with sp.Fori(1, TILES) as j:
                    for h in range(2):
                        store(j - 1, h)
                        sp.wait_ge(silu_done, j * 2 + h - 1)
                        load(j, h)
                for h in range(2):
                    store(TILES - 1, h)
                for h in range(2):
                    sp.wait_ge(up_stored[h], 16 * TILES)

            @block.gpsimd
            def _(pool):
                pool.wait_ge(asked, 3)
                nc.gpsimd.partition_all_reduce(col(G_MAX), peak[:, 0:1], P, RMAX).then_inc(reduced, 1)
                nc.gpsimd.partition_all_reduce(probe[:, 0:1], peak[:, 1:2], P, RMAX).then_inc(reduced, 1)

                with pool.Fori(0, TILES) as j:
                    for h in range(2):
                        pool.wait_ge(gate_rounded, j * 2 + h + 1)
                        carry(pool, pool_carried)
                        nc.gpsimd.tensor_copy(kept(j, h), g_int[h]).then_inc(gate_kept, 1)
                pool.wait_ge(gate_kept, UNITS)

            @block.vector
            def _(dve):
                nc.vector.tensor_reduce(peak[:, 1:2], gmx, X, ALU.max).then_inc(asked, 1)
                nc.vector.tensor_reduce(peak[:, 2:3], gmn, X, ALU.min).then_inc(small, 1)
                dve.wait_ge(asked, 2)
                dve.wait_ge(small, 3)
                nc.vector.scalar_tensor_tensor(peak[:, 0:1], peak[:, 2:3], -1.0, peak[:, 1:2], ALU.mult, ALU.max)\
                    .then_inc(asked, 1)
                dve.wait_ge(reduced, 3)
                nc.vector.tensor_scalar(col(G_S), col(G_MAX), 1.0 / AQMAX, EPS_Q, ALU.mult, ALU.max).then_inc(small, 1)
                dve.wait_ge(small, 4)
                nc.vector.reciprocal(col(G_INV), col(G_S)).then_inc(small, 1)
                nc.vector.tensor_scalar(col(UNIT_O), col(G_S), -1.0 / 65536.0, None, ALU.mult).then_inc(small, 1)
                dve.wait_ge(small, 6)
                nc.vector.tensor_scalar(probe_int[:], probe[:, 0:1], col(G_INV), None, ALU.mult).then_inc(scale_ready, 1)
                dve.wait_ge(probe_act, 1)
                nc.vector.tensor_scalar(probe_sig[:], probe[:, 1:2], 65536.0, 65535.0, ALU.mult, ALU.min)\
                    .then_inc(probe_step, 1)
                dve.wait_ge(probe_step, 1)
                nc.vector.tensor_scalar(probe[:, 2:3], probe_sig[:], col(UNIT_O), -1.0, ALU.mult, ALU.mult)\
                    .then_inc(probe_step, 1)
                dve.wait_ge(probe_step, 2)
                nc.vector.tensor_tensor(peak[:, 3:4], probe[:, 2:3], probe_int[:], ALU.mult).then_inc(probe_step, 1)

                def unit(j, h, first):
                    dve.wait_ge(sig_done, j * 2 + h + 1)
                    nc.vector.tensor_scalar(sig_int[:], sig[h][:], 65536.0, 65535.0, ALU.mult, ALU.min)\
                        .then_inc(sig_rounded, 1)
                    dve.wait_ge(sig_rounded, j * 2 + h + 1)
                    carry(dve, carried)
                    nc.vector.tensor_tensor_reduce(out=silu[h][:], in0=g_int[h], in1=sig_int[:],
                                                   scale=col(UNIT_O), scalar=0.0, op0=ALU.mult, op1=ALU.max,
                                                   accum_out=unit_max[:, h:h + 1]).then_inc(silu_done, 1)
                    dve.wait_ge(up_copied, j * F + HF * (h + 1))
                    nc.vector.tensor_reduce(umx[:, bass.ds(j * 2 + h, 1)], u_stage[h][:], X, ALU.max,
                                            apply_absolute_value=True).then_inc(up_seen, 1)
                    dve.wait_ge(silu_done, j * 2 + h + 1)
                    nc.vector.tensor_copy(hmx[:, bass.ds(j * 2 + h, 1)], unit_max[:, h:h + 1]).then_inc(max_kept, 1)

                for h in range(2):
                    unit(0, h, True)
                with dve.Fori(1, TILES) as j:
                    for h in range(2):
                        unit(j, h, False)
                dve.wait_ge(silu_done, UNITS)
                dve.wait_ge(max_kept, UNITS)
                dve.wait_ge(up_seen, UNITS)
                dve.wait_ge(probe_step, 3)

            @block.scalar
            def _(act):
                act.wait_ge(scale_ready, 1)
                nc.scalar.activation(probe[:, 1:2], probe_int[:], ACT.Sigmoid, scale=col(G_S)).then_inc(probe_act, 1)

                def unit(j, h, first):
                    for k in range(HF):
                        f = h * HF + k
                        act.wait_ge(up_made, j * F + f + 1)
                        if k == 0 and not first:
                            act.wait_ge(up_seen, j * 2 + h - 1)
                            act.wait_ge(up_stored[h], j * 16)
                        nc.scalar.activation(u_stage[h][:, k * TILE:(k + 1) * TILE], banks[f][:], ACT.Copy,
                                             scale=col(U_W)).then_inc(up_copied, 1)
                    act.wait_ge(gate_loaded[h], j * 16 + 16)
                    if not first:
                        act.wait_ge(silu_done, j * 2 + h - 1)
                        act.wait_ge(gate_kept, j * 2 + h - 1)
                    nc.scalar.activation(g_int[h], g_in[h][:], ACT.Copy, scale=col(G_INV)).then_inc(gate_rounded, 1)
                    act.wait_ge(gate_rounded, j * 2 + h + 1)
                    nc.scalar.activation(sig[h][:], g_int[h], ACT.Sigmoid, scale=col(G_S)).then_inc(sig_done, 1)

                for h in range(2):
                    unit(0, h, True)
                with act.Fori(1, TILES) as j:
                    for h in range(2):
                        unit(j, h, False)

            @block.tensor
            def _(pe):
                def products(j, first):
                    for f in range(F):
                        if not first:
                            pe.wait_ge(up_copied, j * F - F + f + 1)
                        inner_products(pe, banks[f], keep["w_upT"], j, f).then_inc(up_made, 1)
                products(0, True)
                with pe.Fori(1, TILES) as j:
                    products(j, False)

        room = xnT[:].rearrange("p c t -> p (c t)")

        def carver():
            at = [0]

            def carve(cols, dt=F32):
                words = cols * mybir.dt.size(dt) // mybir.dt.size(F32)
                view = room[:, at[0]:at[0] + words]
                at[0] += words
                assert at[0] <= C * B * S
                return view if dt is F32 else view.bitcast(dt)
            return carve

        with ExitStack() as c3:
            def sb3(name, shape, dt=F32):
                return c3.enter_context(nc.sbuf_tensor(name, shape, dt))

            def sem3(name):
                return c3.enter_context(nc.semaphore(name))

            carve = carver()
            N = 2
            u_in = [carve(UW) for _ in range(N)]
            sig = [carve(UW) for _ in range(N)]
            prod = carve(UW)
            sig_int = [carve(UW, U16) for _ in range(N)]
            h_abs = [carve(UW, I16) for _ in range(N)]
            u_abs = [carve(UW, I16) for _ in range(N)]
            unit_max, max_kept = sb3("unit_max_o", [P, 2]), sem3("o_max_kept")
            u_loaded = [sem3(f"u_loaded{k}") for k in range(N)]
            sig_done, sig_rounded = sem3("sig_done_again"), sem3("sig_rounded_again")
            silu_rounded, silu_sized, up_sized, prod_seen = (sem3("silu_rounded"), sem3("silu_sized"),
                                                             sem3("up_sized"), sem3("prod_seen"))
            scales_known = sem3("scales_known")
            block = c3.enter_context(nc.Block())

            @block.sync
            def _(sp):
                def load(j, h):
                    sp.dma_start(u_in[h], scratch["up"][j][:, h * UW:(h + 1) * UW]).then_inc(u_loaded[h], 16)
                for h in range(N):
                    load(0, h)
                with sp.Fori(1, TILES) as j:
                    for h in range(N):
                        sp.wait_ge(up_sized, j * 2 + h - 1)
                        load(j, h)

            @block.gpsimd
            def _(pool):
                pool.wait_ge(asked, 4)
                nc.gpsimd.partition_all_reduce(col(U_MAX), peak[:, 0:1], P, RMAX).then_inc(reduced, 1)
                pool.wait_ge(asked, 6)
                nc.gpsimd.partition_all_reduce(col(H_MAX), peak[:, 1:2], P, RMAX).then_inc(reduced, 1)

            @block.vector
            def _(dve):
                nc.vector.tensor_reduce(peak[:, 0:1], umx, X, ALU.max).then_inc(asked, 1)
                nc.vector.tensor_reduce(peak[:, 2:3], hmx, X, ALU.max).then_inc(asked, 1)
                dve.wait_ge(asked, 5)
                nc.vector.tensor_tensor(peak[:, 1:2], peak[:, 2:3], peak[:, 3:4], ALU.max).then_inc(asked, 1)
                dve.wait_ge(reduced, 4)
                nc.vector.tensor_scalar(col(U_S), col(U_MAX), 1.0 / AQMAX, EPS_Q, ALU.mult, ALU.max).then_inc(small, 1)
                dve.wait_ge(reduced, 5)
                nc.vector.tensor_scalar(col(H_S), col(H_MAX), 1.0 / AQMAX, EPS_Q, ALU.mult, ALU.max).then_inc(small, 1)
                dve.wait_ge(small, 8)
                nc.vector.reciprocal(col(U_INV), col(U_S)).then_inc(scales_known, 1)
                nc.vector.reciprocal(col(H_INV), col(H_S)).then_inc(scales_known, 1)
                dve.wait_ge(scales_known, 2)
                nc.vector.scalar_tensor_tensor(col(H_FACTOR), col(UNIT_O), -1.0, col(H_INV), ALU.mult, ALU.mult)\
                    .then_inc(scales_known, 1)
                dve.wait_ge(scales_known, 3)

                def silu_of(j, h):
                    dve.wait_ge(sig_done, j * 2 + h + 1)
                    nc.vector.tensor_scalar(sig_int[h], sig[h], 65536.0, 65535.0, ALU.mult, ALU.min)\
                        .then_inc(sig_rounded, 1)
                    dve.wait_ge(sig_rounded, j * 2 + h + 1)
                    nc.vector.scalar_tensor_tensor(kept(j, h), kept(j, h), col(H_FACTOR), sig_int[h],
                                                   ALU.mult, ALU.mult).then_inc(silu_rounded, 1)

                def largest(j, h):
                    dve.wait_ge(up_sized, j * 2 + h + 1)
                    dve.wait_ge(silu_sized, j * 2 + h + 1)
                    carry(dve, carried)
                    nc.vector.tensor_tensor_reduce(out=prod, in0=h_abs[h], in1=u_abs[h], scale=1.0,
                                                   scalar=0.0, op0=ALU.mult, op1=ALU.max,
                                                   accum_out=unit_max[:, h:h + 1]).then_inc(prod_seen, 1)
                    dve.wait_ge(prod_seen, j * 2 + h + 1)
                    nc.vector.tensor_copy(omx[:, bass.ds(j * 2 + h, 1)], unit_max[:, h:h + 1]).then_inc(max_kept, 1)

                silu_of(0, 0)
                silu_of(0, 1)
                largest(0, 0)
                with dve.Fori(1, TILES) as j:
                    silu_of(j, 0)
                    largest(j - 1, 1)
                    silu_of(j, 1)
                    largest(j, 0)
                largest(TILES - 1, 1)
                dve.wait_ge(max_kept, UNITS)

            @block.scalar
            def _(act):
                act.wait_ge(scales_known, 2)

                def sigmoid(j, h, first):
                    if not first:
                        act.wait_ge(sig_rounded, j * 2 + h - 1)
                        carry(act, act_carried)
                    nc.scalar.activation(sig[h], kept(j, h), ACT.Sigmoid, scale=col(G_S)).then_inc(sig_done, 1)

                def size_of_up(j, h, first):
                    act.wait_ge(u_loaded[h], j * 16 + 16)
                    if not first:
                        act.wait_ge(prod_seen, j * 2 + h - 1)
                    nc.scalar.activation(u_abs[h], u_in[h], ACT.Abs, scale=col(U_INV)).then_inc(up_sized, 1)

                def size_of_silu(j, h):
                    act.wait_ge(silu_rounded, j * 2 + h + 1)
                    carry(act, act_carried)
                    nc.scalar.activation(h_abs[h], kept(j, h), ACT.Abs).then_inc(silu_sized, 1)

                sigmoid(0, 0, True)
                sigmoid(0, 1, True)
                size_of_up(0, 0, True)
                size_of_silu(0, 0)
                sigmoid(1, 0, False)
                size_of_up(0, 1, True)
                size_of_silu(0, 1)
                with act.Fori(1, TILES - 1) as j:
                    sigmoid(j, 1, False)
                    size_of_up(j, 0, False)
                    size_of_silu(j, 0)
                    sigmoid(j + 1, 0, False)
                    size_of_up(j, 1, False)
                    size_of_silu(j, 1)
                sigmoid(TILES - 1, 1, False)
                for h in range(N):
                    size_of_up(TILES - 1, h, False)
                    size_of_silu(TILES - 1, h)

        with ExitStack() as c4:
            def sb4(name, shape, dt=F32):
                return c4.enter_context(nc.sbuf_tensor(name, shape, dt))

            def sem4(name):
                return c4.enter_context(nc.semaphore(name))

            carve = carver()
            u_in = [carve(UW) for _ in range(2)]
            u_int = [carve(UW, I16) for _ in range(2)]
            o_int = [carve(UW, I16) for _ in range(2)]
            o = [[[carve(UW, F16) for _ in range(2)] for _ in range(2)] for _ in range(2)]
            SUB = TILE // P
            x2_in = [sb4(f"x2_in{k}", [P, SUB, D]) for k in range(2)]
            y = [sb4(f"y{k}", [P, SUB, D]) for k in range(2)]
            up_loaded = [sem4(f"up_loaded{k}") for k in range(2)]
            x2_loaded = [sem4(f"x2_loaded{k}") for k in range(2)]
            y_stored = [sem4(f"y_stored{k}") for k in range(2)]
            o_high, o_ready = sem4("o_high"), sem4("o_ready")
            up_rounded, o_rounded, y_made, y_ready = (sem4("up_rounded"), sem4("o_rounded"),
                                                               sem4("y_made"), sem4("y_ready"))
            o_step = sem4("o_step")
            x2_rows = scratch["x2"].rearrange("b p t d -> p b t d")
            out_rows = out.rearrange("b (t p) d -> p b t d", p=P)
            BT = TILE // S
            block = c4.enter_context(nc.Block())

            @block.sync
            def _(sp):
                def load(j, h):
                    sp.dma_start(u_in[h], scratch["up"][j][:, h * UW:(h + 1) * UW]).then_inc(up_loaded[h], 16)

                def load_x2(j, odd):
                    sp.dma_start(x2_in[odd][:].rearrange("p (b t) d -> p b t d", b=BT), x2_rows[:, bass.ds(j * BT, BT)])\
                        .then_inc(x2_loaded[odd], 16)

                def store(j, odd):
                    sp.wait_ge(y_ready, j * SUB + SUB)
                    for k in range(BT):
                        sp.dma_start(out_rows[:, j * BT + k], y[odd][:, k * T:(k + 1) * T, :]).then_inc(y_stored[odd], 16)

                for j in range(2):
                    for h in range(2):
                        if j:
                            sp.wait_ge(up_rounded, j * 2 + h - 1)
                        load(j, h)
                    load_x2(j, j)
                with sp.Fori(1, TILES // 2) as pair:
                    for odd in range(2):
                        j = pair * 2 + odd
                        for h in range(2):
                            sp.wait_ge(up_rounded, j * 2 + h - 1)
                            load(j, h)
                        store(j - 2, odd)
                        load_x2(j, odd)
                for odd in range(2):
                    store(TILES - 2 + odd, odd)
                for odd in range(2):
                    sp.wait_ge(y_stored[odd], 16 * BT * (TILES // 2))

            @block.gpsimd
            def _(pool):
                pool.wait_ge(asked, 7)
                nc.gpsimd.partition_all_reduce(col(O_MAX), peak[:, 4:5], P, RMAX).then_inc(reduced, 1)

            @block.vector
            def _(dve):
                nc.vector.tensor_reduce(peak[:, 4:5], omx, X, ALU.max).then_inc(asked, 1)
                nc.vector.tensor_tensor(col(UNIT_O), col(H_S), col(U_S), ALU.mult).then_inc(o_step, 1)
                dve.wait_ge(reduced, 6)
                dve.wait_ge(o_step, 1)
                nc.vector.tensor_tensor(peak[:, 5:6], col(O_MAX), col(UNIT_O), ALU.mult).then_inc(o_step, 1)
                dve.wait_ge(o_step, 2)
                nc.vector.tensor_scalar(col(O_S), peak[:, 5:6], 1.0 / AQMAX, EPS_Q, ALU.mult, ALU.max).then_inc(o_step, 1)
                dve.wait_ge(o_step, 3)
                nc.vector.reciprocal(peak[:, 6:7], col(O_S)).then_inc(o_step, 1)
                nc.vector.tensor_tensor(peak[:, 7:8], col(O_S), keep["unscale"][:, 2:3], ALU.mult).then_inc(o_step, 1)
                dve.wait_ge(o_step, 5)
                nc.vector.tensor_tensor(col(O_W), peak[:, 7:8], keep["tanh"][:, 1:2], ALU.mult).then_inc(o_step, 1)
                dve.wait_ge(o_step, 6)
                nc.vector.tensor_tensor(col(O_INV), peak[:, 6:7], col(UNIT_O), ALU.mult)\
                    .then_inc(o_step, 1)
                dve.wait_ge(o_step, 7)

                def round_product(j, h, first):
                    dve.wait_ge(up_rounded, j * 2 + h + 1)
                    if not first:
                        dve.wait_ge(o_ready, j * 2 + h - 1)
                    nc.vector.scalar_tensor_tensor(o_int[h], kept(j, h),
                                                   col(O_INV), u_int[h], ALU.mult, ALU.mult).then_inc(o_rounded, 1)

                def residual(pair, odd, first):
                    j = pair * 2 + odd
                    dve.wait_ge(x2_loaded[odd], pair * 16 + 16)
                    if not first:
                        dve.wait_ge(y_stored[odd], pair * 16 * BT)
                    for s in range(SUB):
                        dve.wait_ge(y_made, j * SUB + s + 1)
                        nc.vector.scalar_tensor_tensor(y[odd][:, s, :], banks[s + odd * SUB][:, 0:D],
                                                       col(O_W), x2_in[odd][:, s, :], ALU.mult, ALU.add)\
                            .then_inc(y_ready, 1)

                def round_tile(j, odd, first=False):
                    for h in range(2):
                        round_product(j, h, first)
                    for h in range(2):
                        dve.wait_ge(o_high, j * 2 + h + 1)
                        nc.vector.tensor_tensor(o[odd][h][1], o_int[h], o[odd][h][0], ALU.subtract)\
                            .then_inc(o_ready, 1)

                round_tile(0, 0, first=True)
                for odd in range(2):
                    round_tile(odd + 1, 1 - odd)
                    residual(0, odd, True)
                with dve.Fori(1, TILES // 2 - 1) as pair:
                    for odd in range(2):
                        round_tile(pair * 2 + odd + 1, 1 - odd)
                        residual(pair, odd, False)
                round_tile(TILES - 1, 1)
                for odd in range(2):
                    residual(TILES // 2 - 1, odd, False)

            @block.scalar
            def _(act):
                act.wait_ge(o_step, 7)

                def unit(j, h, first):
                    act.wait_ge(up_loaded[h], j * 16 + 16)
                    if not first:
                        act.wait_ge(o_rounded, j * 2 + h - 1)
                    nc.scalar.activation(u_int[h], u_in[h], ACT.Copy, scale=col(U_INV)).then_inc(up_rounded, 1)

                def high_part(j, odd, h, first):
                    act.wait_ge(o_rounded, j * 2 + h + 1)
                    if not first:
                        act.wait_ge(y_made, (j - 1) * SUB)
                    nc.scalar.activation(o[odd][h][0], o_int[h], ACT.Copy).then_inc(o_high, 1)

                def tile_steps(j, odd, first):
                    for h in range(2):
                        unit(j, h, first and not odd)
                    for h in range(2):
                        high_part(j, odd, h, first)

                tile_steps(0, 0, True)
                tile_steps(1, 1, True)
                with act.Fori(1, TILES // 2) as pair:
                    for odd in range(2):
                        tile_steps(pair * 2 + odd, odd, False)

            @block.tensor
            def _(pe):
                def rows(j, odd, first):
                    for s in range(SUB):
                        bank = banks[(s + odd * SUB)]
                        if not first:
                            pe.wait_ge(y_ready, (j - 2) * SUB + s + 1)
                        for f in range(F):
                            if s == 0 and f % HF == 0:
                                pe.wait_ge(o_ready, j * 2 + f // HF + 1)
                            at = (f % HF) * TILE + s * P
                            for k, (op, wp) in enumerate(PRODUCTS):
                                last = nc.tensor.matmul(bank[:, 0:D], o[odd][f // HF][op][:, at:at + P],
                                                        keep["w_downT"][wp][:, f * D:(f + 1) * D],
                                                        start=(f == 0 and k == 0),
                                                        stop=(f == F - 1 and k == len(PRODUCTS) - 1))
                        last.then_inc(y_made, 1)
                for odd in range(2):
                    rows(odd, odd, True)
                with pe.Fori(1, TILES // 2) as pair:
                    for odd in range(2):
                        rows(pair * 2 + odd, odd, False)


def build(nc, dram, x, ctx_in, w, out):
    gate = nc.dram_tensor("gate_scratch", (B * S // TILE, P, I // P * TILE), F32, kind="Internal").ap()
    up = nc.dram_tensor("up_scratch", (B * S // TILE, P, I // P * TILE), F32, kind="Internal").ap()
    x2 = nc.dram_tensor("x2_scratch", (B, P, T, D), F32, kind="Internal").ap()
    scratch = {"gate": gate, "up": up, "x2": x2}
    for n in "qk":
        parts = nc.dram_tensor(f"{n}_parts_scratch", (NBUF, 3, DK, H * S), BF16, kind="Internal").ap()
        scratch[n] = parts

        def rows_of(buf, g, n=n, parts=parts):
            if n == "q":
                return parts[buf][g].unsqueeze(0).to_broadcast([3 - g, DK, H * S])
            return parts[buf][0:3 - g]

        scratch[n + "_rows"] = rows_of

    with ExitStack() as ctx:
        def sb(name, shape, dt=F32):
            return ctx.enter_context(nc.sbuf_tensor(name, shape, dt))

        banks = [ctx.enter_context(nc.psum_tensor(f"bank{k}", [P, 512], F32)) for k in range(8)]
        keep = {
            "lnconst": sb("lnconst", [P, 3 * T]), "tanh": sb("tanh", [P, 2]),
            "unscale": sb("unscale", [P, 3]),
            "xmax": sb("xmax", [P, B]), "scales": sb("scales", [P, 20]), "peak": sb("peak", [P, 8]),
            "maxima": sb("maxima", [P, 5, 2 * B * S // TILE]),
        }
        for n in ("w_gate", "w_up", "w_down"):
            keep[n + "T"] = [sb(f"{n}T{k}", [P, I * D // P], F16) for k in range(2)]
        keep["xnT"] = sb("xnT", [P, C, B * S])
        with ExitStack() as before_ffn:
            def sba(name, shape, dt=F32):
                return before_ffn.enter_context(nc.sbuf_tensor(name, shape, dt))

            keep["ident"], keep["identb"] = sba("ident", [P, P]), sba("identb", [P, P], BF16)
            keep["ones3"], keep["bias"] = sba("ones3", [3, P], BF16), sba("bias", [3, 4 * D], BF16)
            keep["cos"], keep["sin"] = sba("cos", [P, T * D]), sba("sin", [P, T * D])
            keep["band"] = sba("band", [P, T, SPAN], BF16)
            for n in ("Wq", "Wk", "Wv", "Wo"):
                keep[n + "T"] = sba(n + "T", [P, C * D])
            prepare(nc, dram, w, banks, keep)
            attention(nc, dram, x, ctx_in, scratch, banks, keep)
        feed_forward(nc, scratch, out, banks, keep)


def tables():
    inv = np.float32(1.0) / np.float32(10000.0) ** (np.arange(0, DK, 2, dtype=np.float32) / np.float32(DK))
    angle = np.arange(S, dtype=np.float32)[:, None] * inv[None, :].astype(np.float32)
    cos, sin = np.cos(angle).astype(np.float32), np.sin(angle).astype(np.float32)
    cos = np.tile(np.concatenate([cos, cos], 1), (1, H))
    sin = np.tile(np.concatenate([-sin, sin], 1), (1, H))
    lay = lambda a: np.ascontiguousarray(a.reshape(T, P, D).transpose(1, 0, 2).reshape(P, T * D))
    band = np.zeros((P, T, SPAN), np.float32)
    for t in range(T):
        query = t * P + np.arange(P)[:, None]
        key = t * FAR + np.arange(SPAN)[None, :]
        band[:, t] = np.where(np.abs(query - key) <= WINDOW, 0.0, -1e9)
    return {"cos": lay(cos), "sin": lay(sin), "band": band, "ident": np.eye(P, dtype=np.float32)}


_INS = ["x", "ctx_1024", "g_xattn", "g_ffn", "L0_xattn_Wq", "L0_xattn_bq", "L0_xattn_Wk", "L0_xattn_bk",
        "L0_xattn_Wv", "L0_xattn_bv", "L0_xattn_Wo", "L0_xattn_bo", "L0_ffn_w_gate", "L0_ffn_w_up", "L0_ffn_w_down"]


def kernel(**inputs):
    import ml_dtypes
    import numpy as _np
    import concourse.bacc as _bacc
    from concourse import mybir as _mybir
    from concourse.bass_utils import run_bass_kernel_spmd as _run

    nc = _bacc.Bacc("TRN2", target_bir_lowering=False, num_devices=1)
    arrays, aps = {}, {}
    for name in _INS:
        a = _np.ascontiguousarray(inputs[name])
        arrays[f"in_{name}"] = a
        aps[name] = nc.dram_tensor(f"in_{name}", a.shape, _mybir.dt.from_np(a.dtype), kind="ExternalInput").ap()
    dram = {}
    for name, a in tables().items():
        a = a.astype(ml_dtypes.bfloat16) if name == "band" else a
        arrays[f"table_{name}"] = a
        dram[name] = nc.dram_tensor(f"table_{name}", a.shape, _mybir.dt.from_np(a.dtype), kind="ExternalInput").ap()
    out = nc.dram_tensor("out", (B, S, D), F32, kind="ExternalOutput").ap()
    w = {n.rsplit("L0_xattn_")[-1].rsplit("L0_ffn_")[-1]: a for n, a in aps.items()}
    build(nc, dram, aps["x"], aps["ctx_1024"], w, out)
    r = _run(nc, [arrays], core_ids=[0])
    return r.results[0]["out"]
```
